# Optimizing a Trainium2 kernel written in Bass

```python
import numpy as np
import jax
import jax.numpy as jnp

def _softmax(x, axis=-1):
    return jax.nn.softmax(x, axis=axis)

def _gelu(x):
    return jax.nn.gelu(x, approximate=True)

def _silu(x):
    return jax.nn.silu(x)

def _sigmoid(x):
    return jax.nn.sigmoid(x)

def _layernorm(x, axis=-1, eps=1e-05):
    m = jnp.mean(x, axis=axis, keepdims=True)
    v = jnp.var(x, axis=axis, keepdims=True)
    return (x - m) / jnp.sqrt(v + eps)

def _scatter_add(tgt, idx, src, axis=0):
    return tgt.at[idx].add(src)

def _segment_sum(src, seg, n):
    return jax.ops.segment_sum(src, seg, n)
kernel_name = 'mk_hybrid_d2_jaxref_r8_9e3780'

def setup_inputs(seed: int=0):
    np.random.seed(seed)
    _w = jnp.asarray

    def _L0_attn_a_setup():
        import jax, jax.numpy as jnp
        import numpy as np
        B, T, D = (4, 512, 256)
        W_SCALE = 0.02
        key = jax.random.key(seed)
        ks = jax.random.split(key, 10)
        x = jax.random.normal(ks[0], (B, T, D), dtype=jnp.float32)
        Wk = jax.random.normal(ks[1], (D, D), dtype=jnp.float32) * W_SCALE
        Wv = jax.random.normal(ks[2], (D, D), dtype=jnp.float32) * W_SCALE
        Wr = jax.random.normal(ks[3], (D, D), dtype=jnp.float32) * W_SCALE
        Wo = jax.random.normal(ks[4], (D, D), dtype=jnp.float32) * W_SCALE
        bk = jnp.zeros((D,), jnp.float32)
        bv = jnp.zeros((D,), jnp.float32)
        br = jnp.zeros((D,), jnp.float32)
        bo = jnp.zeros((D,), jnp.float32)
        tmk = jax.random.uniform(ks[5], (D,), dtype=jnp.float32)
        tmv = jax.random.uniform(ks[6], (D,), dtype=jnp.float32)
        tmr = jax.random.uniform(ks[7], (D,), dtype=jnp.float32)
        u = jax.random.normal(ks[8], (D,), dtype=jnp.float32) * 0.1
        w = jax.random.uniform(ks[9], (D,), dtype=jnp.float32)
        return {'x': x, 'Wk': Wk, 'bk': bk, 'Wv': Wv, 'bv': bv, 'Wr': Wr, 'br': br, 'Wo': Wo, 'bo': bo, 'tmk': tmk, 'tmv': tmv, 'tmr': tmr, 'u': u, 'w': w}
    _L0_attn_a_in = _L0_attn_a_setup()

    def _L0_attn_b_setup():
        import jax, jax.numpy as jnp
        import numpy as np
        B_, S, H = (2, 256, 256)
        E = 2 * H
        P = 64
        NH = E // P
        N = 64
        G = 1
        K = 4
        CS = 32
        CONV_DIM = E + 2 * G * N
        PROJ = E + CONV_DIM + NH
        EPS = 1e-06

        def segment_sum(a):
            l = a.shape[-1]
            a_exp = jnp.broadcast_to(a[..., None], (*a.shape, l))
            a_exp = jnp.where(jnp.tril(jnp.ones((l, l), bool), -1), a_exp, 0.0)
            s = jnp.cumsum(a_exp, axis=-2)
            return jnp.where(jnp.tril(jnp.ones((l, l), bool), 0), s, -jnp.inf)
        key = jax.random.key(seed)
        ks = jax.random.split(key, 8)
        s = 0.02
        return {'x': jax.random.normal(ks[0], (B_, S, H), jnp.float32), 'in_proj_w': jax.random.normal(ks[1], (PROJ, H), jnp.float32) * s, 'conv_w': jax.random.normal(ks[2], (CONV_DIM, K), jnp.float32) * s, 'conv_b': jnp.zeros((CONV_DIM,), jnp.float32), 'dt_bias': jax.random.uniform(ks[3], (NH,), jnp.float32, 0.0, 1.0), 'A_log': jnp.log(jax.random.uniform(ks[4], (NH,), jnp.float32, 1.0, 16.0)), 'D': jnp.ones((NH,), jnp.float32), 'norm_w': jnp.ones((E,), jnp.float32), 'out_proj_w': jax.random.normal(ks[5], (H, E), jnp.float32) * s}
    _L0_attn_b_in = _L0_attn_b_setup()

    def _L0_ffn_setup():
        import jax, jax.numpy as jnp
        import numpy as np
        B, S, H, E = (4, 256, 256, 8)
        key = jax.random.key(seed)
        k_x, k_wg, k_w, k_b = jax.random.split(key, 4)
        x = jax.random.normal(k_x, (B, S, H), dtype=jnp.float32)
        wg = jax.random.normal(k_wg, (H, E), dtype=jnp.float32) * (1.0 / np.sqrt(H))
        W = jax.random.normal(k_w, (E, H, H), dtype=jnp.float32) * (1.0 / np.sqrt(H))
        b = jax.random.normal(k_b, (E, H), dtype=jnp.float32) * 0.01
        return {'x': x, 'wg': wg, 'W': W, 'b': b}
    _L0_ffn_in = _L0_ffn_setup()

    def _L1_attn_a_setup():
        import jax, jax.numpy as jnp
        import numpy as np
        D_IN = 256
        D_OUT = 256
        NUM_HEADS = 16
        NUM_KV_GROUPS = 4
        GROUP_SIZE = NUM_HEADS // NUM_KV_GROUPS
        HEAD_DIM = D_OUT // NUM_HEADS
        key = jax.random.key(seed)
        ks = jax.random.split(key, 6)
        b, n = (2, 256)
        x = jax.random.normal(ks[0], (b, n, D_IN), dtype=jnp.float32)
        Wq = jax.random.normal(ks[1], (D_IN, D_OUT), dtype=jnp.float32) * (1.0 / np.sqrt(D_IN))
        Wk = jax.random.normal(ks[2], (D_IN, NUM_KV_GROUPS * HEAD_DIM), dtype=jnp.float32) * (1.0 / np.sqrt(D_IN))
        Wv = jax.random.normal(ks[3], (D_IN, NUM_KV_GROUPS * HEAD_DIM), dtype=jnp.float32) * (1.0 / np.sqrt(D_IN))
        Wo = jax.random.normal(ks[4], (D_OUT, D_OUT), dtype=jnp.float32) * (1.0 / np.sqrt(D_OUT))
        bo = jax.random.normal(ks[5], (D_OUT,), dtype=jnp.float32) * 0.01
        return {'x': x, 'Wq': Wq, 'Wk': Wk, 'Wv': Wv, 'Wo': Wo, 'bo': bo}
    _L1_attn_a_in = _L1_attn_a_setup()

    def _L1_attn_b_setup():
        import jax, jax.numpy as jnp
        import numpy as np
        B, T, C = (2, 256, 256)
        H, KVH = (16, 4)
        HD = C // H
        REP = H // KVH

        def _alibi_slopes(n_head):
            start = 2.0 ** (-2.0 ** (-(np.log2(n_head) - 3.0)))
            return jnp.asarray([start ** (i + 1) for i in range(n_head)], jnp.float32)
        key = jax.random.key(seed)
        ks = jax.random.split(key, 4)
        sc = 0.02
        return {'x': jax.random.normal(ks[0], (B, T, C), jnp.float32), 'Wq': jax.random.normal(ks[1], (C, C), jnp.float32) * sc, 'Wkv': jax.random.normal(ks[2], (C, HD * KVH * 2), jnp.float32) * sc, 'Wo': jax.random.normal(ks[3], (C, C), jnp.float32) * sc, 'bo': jnp.zeros((C,), jnp.float32)}
    _L1_attn_b_in = _L1_attn_b_setup()

    def _L1_ffn_setup():
        import jax, jax.numpy as jnp
        import numpy as np
        TOP_K = 4
        key = jax.random.key(seed)
        ks = jax.random.split(key, 5)
        H, I, E = (256, 96, 32)
        s = 0.02
        return {'hidden_states': jax.random.normal(ks[0], (1, 128, H), jnp.float32), 'router_w': jax.random.normal(ks[1], (E, H), jnp.float32) * s, 'gate_w': jax.random.normal(ks[2], (E, I, H), jnp.float32) * s, 'up_w': jax.random.normal(ks[3], (E, I, H), jnp.float32) * s, 'down_w': jax.random.normal(ks[4], (E, H, I), jnp.float32) * s}
    _L1_ffn_in = _L1_ffn_setup()
    _d = {'L0_attn_a_x': _L0_attn_a_in['x'], 'L0_attn_a_Wk': _L0_attn_a_in['Wk'], 'L0_attn_a_bk': _L0_attn_a_in['bk'], 'L0_attn_a_Wv': _L0_attn_a_in['Wv'], 'L0_attn_a_bv': _L0_attn_a_in['bv'], 'L0_attn_a_Wr': _L0_attn_a_in['Wr'], 'L0_attn_a_br': _L0_attn_a_in['br'], 'L0_attn_a_Wo': _L0_attn_a_in['Wo'], 'L0_attn_a_bo': _L0_attn_a_in['bo'], 'L0_attn_a_tmk': _L0_attn_a_in['tmk'], 'L0_attn_a_tmv': _L0_attn_a_in['tmv'], 'L0_attn_a_tmr': _L0_attn_a_in['tmr'], 'L0_attn_a_u': _L0_attn_a_in['u'], 'L0_attn_a_w': _L0_attn_a_in['w'], 'L0_attn_b_in_proj_w': _L0_attn_b_in['in_proj_w'], 'L0_attn_b_conv_w': _L0_attn_b_in['conv_w'], 'L0_attn_b_conv_b': _L0_attn_b_in['conv_b'], 'L0_attn_b_dt_bias': _L0_attn_b_in['dt_bias'], 'L0_attn_b_A_log': _L0_attn_b_in['A_log'], 'L0_attn_b_D': _L0_attn_b_in['D'], 'L0_attn_b_norm_w': _L0_attn_b_in['norm_w'], 'L0_attn_b_out_proj_w': _L0_attn_b_in['out_proj_w'], 'L0_ffn_wg': _L0_ffn_in['wg'], 'L0_ffn_W': _L0_ffn_in['W'], 'L0_ffn_b': _L0_ffn_in['b'], 'L1_attn_a_Wq': _L1_attn_a_in['Wq'], 'L1_attn_a_Wk': _L1_attn_a_in['Wk'], 'L1_attn_a_Wv': _L1_attn_a_in['Wv'], 'L1_attn_a_Wo': _L1_attn_a_in['Wo'], 'L1_attn_a_bo': _L1_attn_a_in['bo'], 'L1_attn_b_Wq': _L1_attn_b_in['Wq'], 'L1_attn_b_Wkv': _L1_attn_b_in['Wkv'], 'L1_attn_b_Wo': _L1_attn_b_in['Wo'], 'L1_attn_b_bo': _L1_attn_b_in['bo'], 'L1_ffn_router_w': _L1_ffn_in['router_w'], 'L1_ffn_gate_w': _L1_ffn_in['gate_w'], 'L1_ffn_up_w': _L1_ffn_in['up_w'], 'L1_ffn_down_w': _L1_ffn_in['down_w']}
    _x0 = _d['L0_attn_a_x']
    _d['L0_attn_a_x'] = jax.random.normal(jax.random.fold_in(jax.random.key(seed), 1), (4, 256, 256), dtype=_x0.dtype)
    del _x0
    return _d

def reference(L0_attn_a_x, L0_attn_a_Wk, L0_attn_a_bk, L0_attn_a_Wv, L0_attn_a_bv, L0_attn_a_Wr, L0_attn_a_br, L0_attn_a_Wo, L0_attn_a_bo, L0_attn_a_tmk, L0_attn_a_tmv, L0_attn_a_tmr, L0_attn_a_u, L0_attn_a_w, L0_attn_b_in_proj_w, L0_attn_b_conv_w, L0_attn_b_conv_b, L0_attn_b_dt_bias, L0_attn_b_A_log, L0_attn_b_D, L0_attn_b_norm_w, L0_attn_b_out_proj_w, L0_ffn_wg, L0_ffn_W, L0_ffn_b, L1_attn_a_Wq, L1_attn_a_Wk, L1_attn_a_Wv, L1_attn_a_Wo, L1_attn_a_bo, L1_attn_b_Wq, L1_attn_b_Wkv, L1_attn_b_Wo, L1_attn_b_bo, L1_ffn_router_w, L1_ffn_gate_w, L1_ffn_up_w, L1_ffn_down_w):

    def _L0_attn_a_ref(x, Wk, bk, Wv, bv, Wr, br, Wo, bo, tmk, tmv, tmr, u, w):
        import jax, jax.numpy as jnp
        import numpy as np
        B, T, D = (4, 512, 256)
        W_SCALE = 0.02
        xs = jnp.pad(x, ((0, 0), (1, 0), (0, 0)))[:, :-1]
        k = x * tmk + xs * (1.0 - tmk)
        v = x * tmv + xs * (1.0 - tmv)
        r = jax.nn.silu(x * tmr + xs * (1.0 - tmr))
        k = jnp.einsum('btd,ed->bte', k, Wk) + bk
        v = jnp.einsum('btd,ed->bte', v, Wv) + bv
        r = jnp.einsum('btd,ed->bte', r, Wr) + br

        def step(carry, kv_t):
            a, b = carry
            k_t, v_t = kv_t
            t = jnp.maximum(u + k_t, w)
            e1 = jnp.exp(-w - t)
            e2 = jnp.exp(u + k_t - t)
            a = e1 * a + e2 * v_t
            b = e1 * b + e2
            return ((a, b), a / b)
        a0 = jnp.zeros((x.shape[0], x.shape[2]), x.dtype)
        b0 = jnp.zeros_like(a0)
        _, wkv = jax.lax.scan(step, (a0, b0), (k.transpose(1, 0, 2), v.transpose(1, 0, 2)))
        wkv = wkv.transpose(1, 0, 2)
        return jnp.einsum('btd,ed->bte', wkv * r, Wo) + bo

    def _L0_attn_b_ref(x, in_proj_w, conv_w, conv_b, dt_bias, A_log, D, norm_w, out_proj_w):
        import jax, jax.numpy as jnp
        import numpy as np
        B_, S, H = (2, 256, 256)
        E = 2 * H
        P = 64
        NH = E // P
        N = 64
        G = 1
        K = 4
        CS = 32
        CONV_DIM = E + 2 * G * N
        PROJ = E + CONV_DIM + NH
        EPS = 1e-06

        def segment_sum(a):
            l = a.shape[-1]
            a_exp = jnp.broadcast_to(a[..., None], (*a.shape, l))
            a_exp = jnp.where(jnp.tril(jnp.ones((l, l), bool), -1), a_exp, 0.0)
            s = jnp.cumsum(a_exp, axis=-2)
            return jnp.where(jnp.tril(jnp.ones((l, l), bool), 0), s, -jnp.inf)
        b, s, _ = x.shape
        proj = x @ in_proj_w.T
        gate, hBC, dt = jnp.split(proj, [E, E + CONV_DIM], axis=-1)
        xp = jnp.pad(hBC, ((0, 0), (K - 1, 0), (0, 0)))
        conv = sum((xp[:, k:k + s, :] * conv_w[:, k] for k in range(K))) + conv_b
        hBC = jax.nn.silu(conv)
        h, Bm, Cm = jnp.split(hBC, [E, E + G * N], axis=-1)
        dt = jax.nn.softplus(dt + dt_bias)
        A = -jnp.exp(A_log)
        h = h.reshape(b, s, NH, P)
        Bm = jnp.tile(Bm.reshape(b, s, G, N), (1, 1, NH // G, 1))
        Cm = jnp.tile(Cm.reshape(b, s, G, N), (1, 1, NH // G, 1))
        pad = -s % CS
        D_res = D[:, None] * jnp.pad(h, ((0, 0), (0, pad), (0, 0), (0, 0)))
        h = h * dt[..., None]
        A_d = A * dt

        def chunk(t):
            t = jnp.pad(t, ((0, 0), (0, pad)) + ((0, 0),) * (t.ndim - 2))
            return t.reshape(b, -1, CS, *t.shape[2:])
        hc, Ac, Bc, Cc = (chunk(h), chunk(A_d), chunk(Bm), chunk(Cm))
        Ac = jnp.transpose(Ac, (0, 3, 1, 2))
        A_cs = jnp.cumsum(Ac, axis=-1)
        L = jnp.exp(segment_sum(Ac))
        Gm = jnp.einsum('bclhn,bcshn->bclsh', Cc, Bc)
        M = Gm * jnp.transpose(L, (0, 2, 3, 4, 1))
        Y_diag = jnp.einsum('bclsh,bcshp->bclhp', M, hc)
        decay = jnp.exp(A_cs[..., -1:] - A_cs)
        Bdec = Bc * jnp.transpose(decay, (0, 2, 3, 1))[..., None]
        states = jnp.einsum('bclhn,bclhp->bchpn', Bdec, hc)
        states = jnp.concatenate([jnp.zeros_like(states[:, :1]), states], axis=1)
        A_last = jnp.pad(A_cs[..., -1], ((0, 0), (0, 0), (1, 0)))
        dchunk = jnp.transpose(jnp.exp(segment_sum(A_last)), (0, 3, 2, 1))
        new_states = jnp.einsum('bzjh,bzhpn->bjhpn', dchunk, states)
        states = new_states[:, :-1]
        sdo = jnp.exp(A_cs)
        Y_off = jnp.einsum('bclhn,bchpn->bclhp', Cc, states) * jnp.transpose(sdo, (0, 2, 3, 1))[..., None]
        y = (Y_diag + Y_off).reshape(b, -1, NH, P) + D_res
        y = y[:, :s].reshape(b, s, E)
        yf = y * jax.nn.silu(gate)
        var = jnp.mean(yf * yf, axis=-1, keepdims=True)
        yn = norm_w * (yf * jax.lax.rsqrt(var + EPS))
        return yn @ out_proj_w.T

    def _L0_ffn_ref(x, wg, W, b):
        import jax, jax.numpy as jnp
        import numpy as np
        B, S, H, E = (4, 256, 256, 8)
        Bv, Sv, Hv = x.shape
        Ev = W.shape[0]
        xt = x.reshape(-1, Hv)
        logits = xt @ wg
        probs = jax.nn.softmax(logits, axis=-1)
        idx = jnp.argmax(probs, axis=-1)
        gate = jnp.take_along_axis(probs, idx[:, None], axis=1)
        onehot = jax.nn.one_hot(idx, Ev, dtype=x.dtype)
        expert_out = jnp.einsum('nh,eoh->neo', xt, W) + b[None, :, :]
        combine = onehot * gate
        out = jnp.einsum('ne,neo->no', combine, expert_out)
        return out.reshape(Bv, Sv, Hv)

    def _L1_attn_a_ref(x, Wq, Wk, Wv, Wo, bo):
        import jax, jax.numpy as jnp
        import numpy as np
        D_IN = 256
        D_OUT = 256
        NUM_HEADS = 16
        NUM_KV_GROUPS = 4
        GROUP_SIZE = NUM_HEADS // NUM_KV_GROUPS
        HEAD_DIM = D_OUT // NUM_HEADS
        b, n, _ = x.shape
        q = (x @ Wq).reshape(b, n, NUM_KV_GROUPS, GROUP_SIZE, HEAD_DIM)
        k = (x @ Wk).reshape(b, n, NUM_KV_GROUPS, HEAD_DIM)
        v = (x @ Wv).reshape(b, n, NUM_KV_GROUPS, HEAD_DIM)
        scale = 1.0 / np.sqrt(HEAD_DIM).astype(np.float32)
        scores = jnp.einsum('bqgsd,bkgd->bgsqk', q, k) * scale
        causal = jnp.arange(n)[:, None] < jnp.arange(n)[None, :]
        scores = jnp.where(causal, -jnp.inf, scores)
        attn = jax.nn.softmax(scores, axis=-1)
        ctx = jnp.einsum('bgsqk,bkgd->bqgsd', attn, v)
        ctx = ctx.reshape(b, n, D_OUT)
        return ctx @ Wo + bo

    def _L1_attn_b_ref(x, Wq, Wkv, Wo, bo):
        import jax, jax.numpy as jnp
        import numpy as np
        B, T, C = (2, 256, 256)
        H, KVH = (16, 4)
        HD = C // H
        REP = H // KVH

        def _alibi_slopes(n_head):
            start = 2.0 ** (-2.0 ** (-(np.log2(n_head) - 3.0)))
            return jnp.asarray([start ** (i + 1) for i in range(n_head)], jnp.float32)
        Bv, Tv, Cv = x.shape
        q = (x @ Wq).reshape(Bv, Tv, H, HD).transpose(0, 2, 1, 3)
        k, v = jnp.split(x @ Wkv, 2, axis=-1)
        k = k.reshape(Bv, Tv, KVH, HD).transpose(0, 2, 1, 3)
        v = v.reshape(Bv, Tv, KVH, HD).transpose(0, 2, 1, 3)
        qg = q.reshape(Bv, REP, KVH, Tv, HD)
        scores = jnp.einsum('brgtd,bgsd->brgts', qg, k) / jnp.sqrt(jnp.float32(HD))
        idx = jnp.arange(Tv)
        diff = (idx[None, :] - idx[:, None]).astype(jnp.float32)
        slopes = _alibi_slopes(H).reshape(REP, KVH)
        bias = jnp.tril(diff)[None, None] * slopes[:, :, None, None]
        causal = idx[None, :] <= idx[:, None]
        scores = jnp.where(causal[None, None, None], scores + bias[None], -jnp.inf)
        attn = jax.nn.softmax(scores, axis=-1)
        out = jnp.einsum('brgts,bgsd->brgtd', attn, v)
        out = out.reshape(Bv, H, Tv, HD).transpose(0, 2, 1, 3).reshape(Bv, Tv, Cv)
        return out @ Wo + bo

    def _L1_ffn_ref(hidden_states, router_w, gate_w, up_w, down_w):
        import jax, jax.numpy as jnp
        import numpy as np
        TOP_K = 4
        B, S, H = hidden_states.shape
        E = router_w.shape[0]
        x = hidden_states.reshape(-1, H)
        logits = x @ router_w.T
        probs = jax.nn.softmax(logits.astype(jnp.float32), axis=-1)
        rw, sel = jax.lax.top_k(probs, TOP_K)
        rw = rw / jnp.sum(rw, axis=-1, keepdims=True)
        rw = rw.astype(x.dtype)

        def body(acc, expert):
            gw, uw, dw, e = expert
            w_tok = jnp.sum(jnp.where(sel == e, rw, 0.0), axis=-1)
            h = jax.nn.silu(x @ gw.T) * (x @ uw.T)
            y = h @ dw.T
            return (acc + w_tok[:, None] * y, None)
        acc0 = jnp.zeros_like(x)
        out, _ = jax.lax.scan(body, acc0, (gate_w, up_w, down_w, jnp.arange(E)))
        return out.reshape(B, S, H)
    x = L0_attn_a_x
    x = x + _L0_attn_a_ref(_layernorm(x, axis=-1), L0_attn_a_Wk, L0_attn_a_bk, L0_attn_a_Wv, L0_attn_a_bv, L0_attn_a_Wr, L0_attn_a_br, L0_attn_a_Wo, L0_attn_a_bo, L0_attn_a_tmk, L0_attn_a_tmv, L0_attn_a_tmr, L0_attn_a_u, L0_attn_a_w)
    x = x + _L0_ffn_ref(_layernorm(x, axis=-1), L0_ffn_wg, L0_ffn_W, L0_ffn_b)
    x = x + _L0_attn_b_ref(_layernorm(x, axis=-1), L0_attn_b_in_proj_w, L0_attn_b_conv_w, L0_attn_b_conv_b, L0_attn_b_dt_bias, L0_attn_b_A_log, L0_attn_b_D, L0_attn_b_norm_w, L0_attn_b_out_proj_w)
    x = x + _L0_ffn_ref(_layernorm(x, axis=-1), L0_ffn_wg, L0_ffn_W, L0_ffn_b)
    x = x + _L1_attn_a_ref(_layernorm(x, axis=-1), L1_attn_a_Wq, L1_attn_a_Wk, L1_attn_a_Wv, L1_attn_a_Wo, L1_attn_a_bo)
    x = x + _L1_ffn_ref(_layernorm(x, axis=-1), L1_ffn_router_w, L1_ffn_gate_w, L1_ffn_up_w, L1_ffn_down_w)
    x = x + _L1_attn_b_ref(_layernorm(x, axis=-1), L1_attn_b_Wq, L1_attn_b_Wkv, L1_attn_b_Wo, L1_attn_b_bo)
    x = x + _L1_ffn_ref(_layernorm(x, axis=-1), L1_ffn_router_w, L1_ffn_gate_w, L1_ffn_up_w, L1_ffn_down_w)
    return x

_drawn_inputs = setup_inputs


def setup_inputs(seed=0):
    import zlib

    import numpy as np

    out = dict(_drawn_inputs(seed))
    spreads = {'L0_attn_a_bk': (0.0, 0.8),
     'L0_attn_a_bv': (0.0, 0.1),
     'L0_attn_a_br': (0.0, 0.291),
     'L0_attn_a_bo': (0.0, 0.1),
     'L0_attn_b_conv_b': (0.0, 0.1),
     'L0_attn_b_D': (1.0, 0.2),
     'L0_attn_b_norm_w': (1.0, 0.2),
     'L1_attn_b_bo': (0.0, 0.1)}
    factors = {'L0_attn_a_Wk': 8.0,
     'L0_attn_a_tmk': 8.0,
     'L0_attn_a_u': 5.15,
     'L0_attn_a_w': 2.956,
     'L0_attn_b_dt_bias': 8.0,
     'L0_attn_b_A_log': 8.0,
     'L0_ffn_b': 3.853,
     'L1_attn_a_bo': 7.158,
     'L1_attn_b_Wq': 21.45,
     'L1_ffn_router_w': 7.581,
     'L1_ffn_gate_w': 7.104,
     'L1_ffn_up_w': 7.004,
     'L1_ffn_down_w': 6.997}
    for name, (base, spread) in spreads.items():
        noise = np.random.default_rng([zlib.crc32(name.encode()), seed]).standard_normal(out[name].shape)
        drawn = base * np.exp(spread * noise) if base else spread * noise
        out[name] = jnp.asarray(drawn.astype(out[name].dtype))
    for name, factor in factors.items():
        out[name] = (out[name] * factor).astype(out[name].dtype)
    return out
```

```python
from contextlib import ExitStack

import concourse.bass as bass
from concourse import mybir

ALU = mybir.AluOpType
ACT = mybir.ActivationFunctionType
AX_X = mybir.AxisListType.X
F32 = mybir.dt.float32
BF16 = mybir.dt.bfloat16
I32 = mybir.dt.int32
U32 = mybir.dt.uint32

LAYERS = 8
P = 128
B, T, D = 4, 256, 256
TILES = B * T // P
HALVES = T // P
DC = D // P
E0 = 8
MH, MP, MN = 8, 64, 64
ME = MH * MP
MC = ME // P
MPROJ = 2 * ME + 2 * MN + MH
TAPS = 4
NG, NS, HD = 4, 4, 16
HP = 32
VW = HD + 1
E1, TOPK, FI = 32, 4, 96
NBLK = B * T * TOPK // P + E1
SLOTS = NBLK * P
LN_EPS, RMS_EPS = 1e-5, 1e-6
CHUNKS = MC + 2
RWKV, MOE0, MAMBA, MOE0B, ATTA, MOE1, ATTB, MOE1B = range(8)
BIASED = {RWKV: 0, ATTA: 1, ATTB: 2}


def build(nc, a, out):
    with ExitStack() as ctx:
        def sb(name, shape, dt=F32):
            return ctx.enter_context(nc.sbuf_tensor(name, shape, dt))[:]

        def sem(name):
            return ctx.enter_context(nc.semaphore(name))

        X = sb("X", [P, TILES, D])
        xn = sb("xn", [P, TILES, D])
        xT = sb("xT", [P, DC, B, T + 1])
        rw_w = sb("rw_w", [P, 4, DC, D])
        cols = sb("cols", [P, 8, DC])
        rows = sb("rows", [P, 3 * MH + 3 * D])
        f0_wg = sb("f0_wg", [P, DC, E0])
        f0_w = sb("f0_w", [P, DC, E0 * D])
        f0_b = sb("f0_b", [E0, D])
        mb_in = sb("mb_in", [P, DC, MPROJ])
        mb_conv = sb("mb_conv", [P, CHUNKS, TAPS + 1])
        mb_norm = sb("mb_norm", [P, MC])
        mb_out = sb("mb_out", [P, MC, D])
        at_q = sb("at_q", [P, 2, DC, NS * P])
        at_k = sb("at_k", [P, 2, DC, P])
        at_v = sb("at_v", [P, 2, DC, NG * HD])
        at_o = sb("at_o", [P, 2, DC, D])
        rt_w = sb("rt_w", [P, DC, E1])
        mats = sb("mats", [P, 5, P])
        iotas = sb("iotas", [P, E1 + 1])
        al_q = sb("al_q", [P, NS, T])
        al_k = sb("al_k", [P, T])
        mask_b = sb("mask_b", [P, 3 * P], BF16)
        ident_b = sb("ident_b", [P, P], BF16)
        zeros = sb("zeros", [P, 512])
        neghalf = sb("neghalf", [P, 1])
        ident, tri_gt, tri_le, tri_lt, ones = (mats[:, i, :] for i in range(5))
        iota_row, iota_col = iotas[:, 0:E1], iotas[:, E1:E1 + 1]
        wk_c, wv_c, wr_c, tmk, tmv, tmr, u_c, w_c = (cols[:, i, :] for i in range(8))
        dt_bias, a_log, d_row = (rows[:, i * MH:(i + 1) * MH] for i in range(3))

        def bo_row(layer):
            i = 3 * MH + BIASED[layer] * D
            return rows[:, i:i + D]

        st6 = sb("st6", [P, 8, 6])
        mv = sb("mv", [P, 8, 2])
        ve = sb("ve", [P, 8, 1])
        rstd = sb("rstd", [P, 8, 1])

        GUW = DC * E1 * 2 * FI
        arena = sb("arena", [P, GUW + E1 * D])
        gu_w = arena[:, 0:GUW].rearrange("p (c n) -> p c n", c=DC)
        dn_w = arena[0:FI, GUW:GUW + E1 * D]

        class Carver:
            def __init__(self, tensor, size):
                self.tensor, self.at, self.size = tensor, 0, size

            def take(self, *dims, parts=P):
                n = 1
                for d in dims:
                    n *= d
                ap = self.tensor[0:parts, self.at:self.at + n]
                self.at += n
                assert self.at <= self.size, (self.at, self.size)
                if len(dims) == 2:
                    return ap.rearrange("p (a b) -> p a b", a=dims[0])
                if len(dims) == 3:
                    return ap.rearrange("p (a b c) -> p a b c", a=dims[0], b=dims[1])
                return ap

        rw = Carver(arena, GUW + E1 * D)
        mix = [rw.take(DC, B, T) for _ in range(3)]
        rw_diff = rw.take(2, DC, T)
        rw_t, rw_d, rw_e1, rw_e2, rw_ev, rw_a, rw_b, rw_rb, rw_q, rw_z = (rw.take(DC, T) for _ in range(10))

        mb = Carver(arena, GUW + E1 * D)
        hs = mb.take(MC, B, T)
        bc = mb.take(2, B, T, parts=MN)
        sg = mb.take(TILES, ME)
        hcv = mb.take(2, CHUNKS, T)
        htok = mb.take(2, ME)
        btok = mb.take(MN)
        m1 = mb.take(2, MH, P)
        Lx = mb.take(MH, P)
        mt = mb.take(MH, P)
        gm = mb.take(P)
        hdec = mb.take(ME)
        dh = mb.take(ME)
        mst = mb.take(ME, parts=MN)
        a_row = sb("a_row", [P, MH])
        epre = sb("epre", [P, MH])
        esuf = sb("esuf", [P, MH])
        dsc = sb("dsc", [P, MH])
        mss = sb("mss", [P, TILES])
        mvar = sb("mvar", [P, TILES])
        mrs = sb("mrs", [P, TILES])
        negw = sb("negw", [P, DC])
        ubk = sb("ubk", [P, DC])

        lg0 = sb("lg0", [P, 2, E0])
        mx0 = sb("mx0", [P, 2, 8])
        ix0 = sb("ix0", [P, 2, 8], U32)
        ex0 = sb("ex0", [P, 2, E0])
        sc0 = sb("sc0", [P, 2, 4])
        cmb = sb("cmb", [P, 2, E0])
        cmbT = sb("cmbT", [E0, P])
        acc = sb("acc", [P, D])

        LATE = 6700
        late = sb("late", [P, LATE])
        mb_late = Carver(late, LATE)
        y1 = mb_late.take(ME)
        yf = mb_late.take(ME)
        ysq = mb_late.take(ME)
        yfT = mb_late.take(MC, P)
        dtr, sp_neg, sp_e, sp_u, sp_d, sp_l, dt, a_d, sp_mask, sp_q = (mb_late.take(TILES * MH) for _ in range(10))
        mask_f = late[:, 0:3 * P]
        at = Carver(late, LATE)
        qT = at.take(NS, T)
        kT = at.take(T)
        pexp = at.take(3, 3 * P)
        pT = at.take(3, 3 * P)
        rsum = at.take(NG * NS)
        ctx_t = at.take(2, D)
        ctxT = at.take(DC, P)
        nmax = sb("nmax", [P, 4, 2])
        vt = sb("vt", [P, HALVES, NG, VW])

        NXB, NYG = 4, 8
        mo = Carver(late, LATE)
        xb = mo.take(NXB, D)
        xbT = mo.take(2, DC, P)
        sgt = mo.take(2, FI)
        hh = mo.take(2, FI)
        hT = mo.take(2, P, parts=FI)
        yb = mo.take(NXB, D)
        yg = mo.take(NYG, D)
        lg1 = sb("lg1", [P, TILES, E1])
        mx1 = sb("mx1", [P, TILES, 8])
        ix1 = sb("ix1", [P, TILES, 8], U32)
        ixf = sb("ixf", [P, TILES, TOPK])
        oh = mo.take(TILES, TOPK, E1)
        pos = mo.take(TILES, E1)
        nmx1 = sb("nmx1", [P, TILES])
        wts = sb("wts", [P, TILES, TOPK])
        wsum = sb("wsum", [P, TILES])
        sel = sb("sel", [P, TILES, E1])
        rnk = sb("rnk", [P, TILES, E1])
        cnt = sb("cnt", [P, E1])
        cnt_i = sb("cnt_i", [P, 2, E1], I32)
        nblk = sb("nblk", [P, E1])
        cum = sb("cum", [P, E1])
        start = sb("start", [P, E1])
        blk_e = sb("blk_e", [P, 1])
        blk_c = sb("blk_c", [P, E1])
        blk_i = sb("blk_i", [1, 2, P], I32)
        slot_f = sb("slot_f", [P, TILES, TOPK])
        slot = sb("slot", [P, TILES * TOPK], U32)

        bank = [ctx.enter_context(nc.psum_tensor(f"bank{i}", [P, 512], F32)) for i in range(8)]

        xg = nc.dram_tensor("grouped_x", [SLOTS, D], F32, kind="Internal").ap()
        yg_d = nc.dram_tensor("grouped_y", [SLOTS, D], F32, kind="Internal").ap()

        x_in = [sem(f"x_in{t}") for t in range(TILES)]
        w_in = {k: sem(f"w_{k}") for k in ("small", "mats", "rwkv", "moe0", "mamba", "att", "moe1")}
        xg_zero = sem("xg_zero")
        out_done = sem("out_done")
        dve_step, act_step, pool_step = sem("dve_step"), sem("act_step"), sem("pool_step")
        prep = sem("prep")
        ln_var, ln_rstd, ln_done = sem("ln_var"), sem("ln_rstd"), sem("ln_done")
        xT_ready = sem("xT_ready")
        xb_ready = sem("xb_ready")
        x_ready = sem("x_ready")
        full = [sem(f"bank_full{i}") for i in range(8)]

        fills = {}
        used = [0] * 8
        free_at = [None] * 8

        def claim(pe, b, key, freed_by):
            if free_at[b] is not None:
                pe.wait_ge(*free_at[b])
            free_at[b] = freed_by
            used[b] += 1
            fills[key] = b, used[b]
            return bank[b]

        def filled(key):
            b, count = fills[key]
            return full[b], count

        def filled_bank(key):
            return bank[fills[key][0]]

        class Steps:
            def __init__(self, eng, s):
                self.eng, self.s, self.n = eng, s, 0

            def mark(self, ins):
                ins.then_inc(self.s, 1)
                self.n += 1
                return self.n

            def after(self, n):
                self.eng.wait_ge(self.s, n)

            def link(self, ins):
                self.after(self.mark(ins))

        MIXES = 3 * DC
        PREPS = 6
        SMALLS = 10
        TPB = (0, 1)

        def xcols(t):
            return xT[:, :, t // HALVES, 1 + (t % HALVES) * P:1 + (t % HALVES + 1) * P]

        rs = {k: sem(f"rw_{k}") for k in ("diff", "mix", "silu", "td", "exp", "ab", "q", "z", "col", "fr")}
        m0 = {k: sem(f"m0_{k}") for k in ("lg", "nmx", "sum", "cmb", "cmbT", "ex")}
        ms = {k: sem(f"mb_{k}") for k in ("dtr", "dtneg", "spe", "spu", "spl", "ad", "tap", "cv", "cvs", "sg", "htok", "btok",
                                          "gm", "esuf", "epre", "dsc", "m1", "L", "mt", "hdec", "dh", "st", "y", "yf",
                                          "yfT", "var", "rs", "sq", "y1", "ydone")}
        as_ = {k: sem(f"at_{k}") for k in ("qkv", "nmax", "exp", "pT", "ctx", "ctxT", "rv")}
        mo_s = {k: sem(f"m1_{k}") for k in ("lg", "nmx", "exw", "sel", "rnk", "cnt", "blk", "blki", "slot", "scat", "xbin",
                                            "xbT", "sg", "h", "hT", "yb", "comb", "turned", "gu", "hturned", "down", "ws")}

        xb_in = [sem(f"xb_in{k}") for k in range(NXB)]
        y_out = [sem(f"y_out{k}") for k in range(NXB)]
        y_in = [sem(f"y_in{k}") for k in range(NYG)]

        TURN_X, GATE_UP, TURN_H, DOWN = range(4)
        AHEAD = ((TURN_X, 3), (GATE_UP, 2), (TURN_H, 1), (DOWN, 0))
        PEEL = 4
        LOOPS = (NBLK - PEEL - 3 - NXB) // 4

        def over_blocks(eng, step):
            for j in range(-3, PEEL):
                for stage, ahead in AHEAD:
                    if j + ahead >= 0:
                        step(stage, 0, j + ahead, j + ahead < 2)
            with eng.Fori(0, LOOPS) as m:
                for c in range(PEEL, PEEL + 4):
                    for stage, ahead in AHEAD:
                        step(stage, m, c + ahead, False)
            for j in range(PEEL + 4 * LOOPS, NBLK):
                for stage, ahead in AHEAD:
                    if j + ahead < NBLK:
                        step(stage, 0, j + ahead, False)

        block = ctx.enter_context(nc.Block())

        @block.tensor
        def _(pe):
            mm = nc.tensor.matmul

            def ln_T(layer, t):
                n = layer * TILES + t
                pe.wait_ge(ln_done, n + 1)
                p = claim(pe, TPB[t % 2], ("xT", n), (xT_ready, n + 1))
                for c in range(DC):
                    ins = nc.tensor.transpose(p[:, c * P:(c + 1) * P], xn[:, t, c * P:(c + 1) * P], ident)
                ins.then_inc(full[TPB[t % 2]], 1)

            def rwkv():
                layer = RWKV
                pe.wait_ge(w_in["mats"], 16)
                for t in range(TILES):
                    ln_T(layer, t)
                pe.wait_ge(w_in["rwkv"], 16)

                def kvr(b):
                    pe.wait_ge(rs["mix"], MIXES * (b + 1))
                    for i, freed in enumerate(((rs["td"], b + 1), (rs["ab"], b + 1), (rs["z"], b + 1))):
                        bk = 2 + 3 * (b % 2) + i
                        if i == 2:
                            pe.wait_ge(rs["silu"], b + 1)
                        p = claim(pe, bk, ("kvr", b, i), freed)
                        for e in range(DC):
                            for c in range(DC):
                                ins = mm(p[:, e * T:(e + 1) * T], rw_w[:, i, c, e * P:(e + 1) * P],
                                         mix[i][:, c, b, :], start=(c == 0), stop=(c == DC - 1))
                        ins.then_inc(full[bk], 1)

                def project(b):
                    pe.wait_ge(rs["z"], b + 1)
                    for h in range(HALVES):
                        t = b * HALVES + h
                        p = claim(pe, TPB[t % 2], ("rwo", t), (x_ready, t + 1))
                        for c in range(DC):
                            ins = mm(p[:, 0:D], rw_z[:, c, h * P:(h + 1) * P], rw_w[:, 3, c, :],
                                     start=(c == 0), stop=(c == DC - 1))
                        ins.then_inc(full[TPB[t % 2]], 1)

                kvr(0)
                for b in range(B):
                    if b + 1 < B:
                        kvr(b + 1)
                    project(b)

            def moe0(layer):
                base = (0 if layer == MOE0 else 1) * TILES
                if layer == MOE0:
                    pe.wait_ge(w_in["moe0"], 32)

                def route(t):
                    ln_T(layer, t)
                    pe.wait_ge(xT_ready, layer * TILES + t + 1)
                    p = claim(pe, 6, ("lg0", base + t), (m0["lg"], base + t + 1))
                    for c in range(DC):
                        ins = mm(p[:, 0:E0], xcols(t)[:, c, :], f0_wg[:, c, :], start=(c == 0), stop=(c == DC - 1))
                    ins.then_inc(full[6], 1)

                route(0)
                for t in range(TILES):
                    if t + 1 < TILES:
                        route(t + 1)
                    for pair in range(E0 // 2):
                        p = claim(pe, 2 + pair, ("ex0", base + t, pair), (m0["ex"], E0 * (base + t) + 2 * pair + 2))
                        for c in range(DC):
                            ins = mm(p[:, :], xcols(t)[:, c, :], f0_w[:, c, pair * 512:(pair + 1) * 512],
                                     start=(c == 0), stop=(c == DC - 1))
                        ins.then_inc(full[2 + pair], 1)
                    pe.wait_ge(m0["cmb"], base + t + 1)
                    p = claim(pe, 7, ("cmbT", base + t), (m0["cmbT"], base + t + 1))
                    nc.tensor.transpose(p[0:E0, 0:P], cmb[:, t % 2, :], ident).then_inc(full[7], 1)
                    pe.wait_ge(m0["cmbT"], base + t + 1)
                    p = claim(pe, 7, ("bias0", base + t), (x_ready, layer * TILES + t + 1))
                    mm(p[:, 0:D], cmbT[:, :], f0_b[:, :], start=True, stop=True).then_inc(full[7], 1)

            def mamba():
                layer = MAMBA
                pe.wait_ge(w_in["mamba"], 32)
                for t in range(TILES):
                    ln_T(layer, t)
                    if t >= 1:
                        dt_proj(layer, t - 1)
                dt_proj(layer, TILES - 1)
                for b in range(B):
                    xb_ = xT[:, :, b, 1:T + 1]
                    for i in range(3):
                        bk = 2 + i
                        p = claim(pe, bk, ("conv", b, i), (ms["tap"], 3 * CHUNKS * b + 2 * CHUNKS + 2 * i + 2))
                        for j in range(2):
                            lo = ME + (2 * i + j) * P if i < 2 else 2 * ME + j * MN
                            m = P if i < 2 else MN
                            for c in range(DC):
                                ins = mm(p[0:m, j * T:(j + 1) * T], mb_in[:, c, lo:lo + m], xb_[:, c, :],
                                         start=(c == 0), stop=(c == DC - 1))
                        ins.then_inc(full[bk], 1)
                    for h in range(HALVES):
                        t = b * HALVES + h
                        p = claim(pe, 5 + h, ("gate", t), (ms["sg"], t + 1))
                        for c in range(DC):
                            ins = mm(p[:, :], xcols(t)[:, c, :], mb_in[:, c, 0:ME], start=(c == 0), stop=(c == DC - 1))
                        ins.then_inc(full[5 + h], 1)

                def head_work(t):
                    b, h = t // HALVES, t % HALVES
                    lo = h * P
                    pe.wait_ge(ms["cvs"], 2 * (b + 1))
                    p = claim(pe, TPB[0], ("htok", t), (ms["htok"], t + 1))
                    for c in range(MC):
                        ins = nc.tensor.transpose(p[:, c * P:(c + 1) * P], hs[:, c, b, lo:lo + P], ident)
                    ins.then_inc(full[TPB[0]], 1)
                    p = claim(pe, 2, ("gm", t), (ms["gm"], t + 1))
                    ins = mm(p[:, 0:P], bc[:, 0, b, lo:lo + P], bc[:, 1, b, lo:lo + P], start=True, stop=True)
                    ins.then_inc(full[2], 1)
                    pe.wait_ge(ms["ad"], 1)
                    if h == 0:
                        p = claim(pe, 7, ("btok", b), (ms["btok"], b + 1))
                        nc.tensor.transpose(p[:, 0:MN], bc[:, 0, b, lo:lo + P], ident[0:MN, 0:MN]).then_inc(full[7], 1)
                        p = claim(pe, 6, ("suf", b), (ms["esuf"], b + 1))
                        mm(p[:, 0:MH], tri_gt, a_d[:, t * MH:(t + 1) * MH], start=True, stop=True).then_inc(full[6], 1)
                    else:
                        p = claim(pe, 6, ("pre", b), (ms["epre"], b + 1))
                        mm(p[:, 0:MH], tri_le, a_d[:, t * MH:(t + 1) * MH], start=True, stop=True).then_inc(full[6], 1)
                    pe.wait_ge(ms["m1"], MH * (t + 1))
                    for q in range(2):
                        p = claim(pe, 3 + q, ("seg", t, q), (ms["L"], 2 * t + q + 1))
                        for i in range(4):
                            ins = mm(p[:, i * P:(i + 1) * P], m1[:, t % 2, 4 * q + i, :], tri_le, start=True, stop=True)
                        ins.then_inc(full[3 + q], 1)

                def outputs(t):
                    b, h = t // HALVES, t % HALVES
                    lo = h * P
                    if h == 0:
                        pe.wait_ge(ms["hdec"], b + 1)
                        pe.wait_ge(ms["btok"], b + 1)
                        p = claim(pe, 6, ("state", b), (ms["st"], b + 1))
                        mm(p[0:MN, :], btok, hdec, start=True, stop=True).then_inc(full[6], 1)
                    else:
                        pe.wait_ge(ms["st"], b + 1)
                        p = claim(pe, 6, ("yoff", b), (ms["y1"], b + 1))
                        mm(p[:, :], bc[:, 1, b, lo:lo + P], mst, start=True, stop=True).then_inc(full[6], 1)
                    p = claim(pe, 5, ("ydiag", t), (ms["y"], t + 1))
                    for i in range(MH):
                        pe.wait_ge(ms["mt"], MH * t + i + 1)
                        ins = mm(p[:, i * MP:(i + 1) * MP], mt[:, i, :], htok[:, t % 2, i * MP:(i + 1) * MP],
                                 start=True, stop=True)
                    ins.then_inc(full[5], 1)

                def project(t):
                    pe.wait_ge(ms["yf"], t + 1)
                    p = claim(pe, TPB[1], ("yfT", t), (ms["yfT"], t + 1))
                    for c in range(MC):
                        ins = nc.tensor.transpose(p[:, c * P:(c + 1) * P], yf[:, c * P:(c + 1) * P], ident)
                    ins.then_inc(full[TPB[1]], 1)
                    pe.wait_ge(ms["yfT"], t + 1)
                    p = claim(pe, 7, ("mbo", t), (x_ready, layer * TILES + t + 1))
                    for c in range(MC):
                        ins = mm(p[:, 0:D], yfT[:, c, :], mb_out[:, c, :], start=(c == 0), stop=(c == MC - 1))
                    ins.then_inc(full[7], 1)

                for t in range(TILES):
                    head_work(t)
                    if t >= 1:
                        project(t - 1)
                    outputs(t)
                project(TILES - 1)

            def dt_proj(layer, t):
                pe.wait_ge(xT_ready, layer * TILES + t + 1)
                if t == 0:
                    claim(pe, 7, ("dt",), (ms["dtr"], 1))
                for c in range(DC):
                    ins = mm(bank[7][:, t * MH:(t + 1) * MH], xcols(t)[:, c, :], mb_in[:, c, MPROJ - MH:MPROJ],
                             start=(c == 0), stop=(c == DC - 1))
                if t == TILES - 1:
                    ins.then_inc(full[7], 1)

            def attention(layer):
                r = (layer - ATTA) // 2
                if r == 0:
                    pe.wait_ge(w_in["att"], 64)
                    pe.wait_ge(prep, PREPS)
                SCORE, TURN = (2, 3, 4), (5, 6)

                def qkv(b):
                    n = r * B + b
                    for h in range(HALVES):
                        t = b * HALVES + h
                        m = layer * TILES + t
                        pe.wait_ge(ln_done, m + 1)
                        p = claim(pe, 0, ("xT", m), (xT_ready, m + 1))
                        for c in range(DC):
                            ins = nc.tensor.transpose(p[:, c * P:(c + 1) * P], xn[:, t, c * P:(c + 1) * P], ident)
                        ins.then_inc(full[0], 1)
                    pe.wait_ge(xT_ready, layer * TILES + (b + 1) * HALVES)
                    for i in range(2):
                        p = claim(pe, 2 + i, ("q", n, i), (as_["qkv"], 4 * n + i + 1))
                        for j in range(2):
                            s = 2 * i + j
                            for c in range(DC):
                                ins = mm(p[:, j * T:(j + 1) * T], at_q[:, r, c, s * P:(s + 1) * P], xT[:, c, b, 1:T + 1],
                                         start=(c == 0), stop=(c == DC - 1))
                        ins.then_inc(full[2 + i], 1)
                    p = claim(pe, 4, ("kv", n), (as_["qkv"], 4 * n + 4))
                    for c in range(DC):
                        mm(p[:, 0:T], at_k[:, r, c, :], xT[:, c, b, 1:T + 1], start=(c == 0), stop=(c == DC - 1))
                    for h in range(HALVES):
                        lo = T + h * NG * HD
                        for c in range(DC):
                            ins = mm(p[:, lo:lo + NG * HD], xcols(b * HALVES + h)[:, c, :], at_v[:, r, c, :],
                                     start=(c == 0), stop=(c == DC - 1))
                    ins.then_inc(full[4], 1)

                def scores(b, i):
                    n = (r * B + b) * NS * NG + i
                    s, g = i // NG, i % NG
                    bk = SCORE[i % 3]
                    p = claim(pe, bk, ("score", n), (as_["exp"], n + 1))
                    mm(p[:, 0:3 * P], ident_b[:, :], mask_b[:, :], start=True, stop=False)
                    lo, hi = g * HP, (g + 1) * HP
                    mm(p[:, 0:P], qT[lo:hi, s, 0:P], kT[lo:hi, 0:P], start=False, stop=False)
                    mm(p[:, P:3 * P], qT[lo:hi, s, P:T], kT[lo:hi, :], start=False, stop=True).then_inc(full[bk], 1)

                def turn(b, i):
                    n = (r * B + b) * NS * NG + i
                    pe.wait_ge(as_["exp"], n + 1)
                    bk = TURN[i % 2]
                    p = claim(pe, bk, ("turn", n), (as_["pT"], n + 1))
                    for j in range(3):
                        ins = nc.tensor.transpose(p[:, j * P:(j + 1) * P], pexp[:, n % 3, j * P:(j + 1) * P], ident)
                    ins.then_inc(full[bk], 1)

                def values(b, i):
                    n = (r * B + b) * NS * NG + i
                    s, g = i // NG, i % NG
                    head = g * NS + s if layer == ATTA else s * NG + g
                    pe.wait_ge(as_["pT"], n + 1)
                    if i == 0:
                        m = r * TILES + b * HALVES
                        claim(pe, 7, ("av", m), (as_["ctx"], m + 1))
                        claim(pe, 1, ("av", m + 1), (as_["ctx"], m + 2))
                    lo = head * VW
                    ins = mm(bank[7][:, lo:lo + VW], pT[:, n % 3, 0:P], vt[:, 0, g, :], start=True, stop=True)
                    if i == NS * NG - 1:
                        ins.then_inc(full[7], 1)
                    mm(bank[1][:, lo:lo + VW], pT[:, n % 3, P:2 * P], vt[:, 0, g, :], start=True, stop=False)
                    ins = mm(bank[1][:, lo:lo + VW], pT[:, n % 3, 2 * P:3 * P], vt[:, 1, g, :], start=False, stop=True)
                    if i == NS * NG - 1:
                        ins.then_inc(full[1], 1)

                def project(b):
                    for h in range(HALVES):
                        t = b * HALVES + h
                        m = r * TILES + t
                        pe.wait_ge(as_["ctx"], m + 1)
                        p = claim(pe, 0, ("ctxT", m), (as_["ctxT"], m + 1))
                        for c in range(DC):
                            ins = nc.tensor.transpose(p[:, c * P:(c + 1) * P], ctx_t[:, t % 2, c * P:(c + 1) * P], ident)
                        ins.then_inc(full[0], 1)
                        pe.wait_ge(as_["ctxT"], m + 1)
                        p = claim(pe, 0, ("ato", m), (x_ready, layer * TILES + t + 1))
                        for c in range(DC):
                            ins = mm(p[:, 0:D], ctxT[:, c, :], at_o[:, r, c, :], start=(c == 0), stop=(c == DC - 1))
                        ins.then_inc(full[0], 1)

                HEADS = NS * NG
                for b in range(B):
                    qkv(b)
                    pe.wait_ge(as_["qkv"], 4 * (r * B + b) + 4)
                    scores(b, 0)
                    scores(b, 1)
                    for i in range(HEADS):
                        if i + 2 < HEADS:
                            scores(b, i + 2)
                        turn(b, i)
                        if i >= 1:
                            values(b, i - 1)
                    values(b, HEADS - 1)
                    project(b)

            def moe1(layer):
                r = (layer - MOE1) // 2
                s = mo_s
                if r == 0:
                    pe.wait_ge(w_in["moe1"], 32)
                for t in range(TILES):
                    ln_T(layer, t)
                    pe.wait_ge(xT_ready, layer * TILES + t + 1)
                    n = r * TILES + t
                    p = claim(pe, 2 + t % 2, ("lg1", n), (s["lg"], n + 1))
                    for c in range(DC):
                        ins = mm(p[:, 0:E1], xcols(t)[:, c, :], rt_w[:, c, :], start=(c == 0), stop=(c == DC - 1))
                    ins.then_inc(full[2 + t % 2], 1)
                p = claim(pe, 4, ("rnk", r), (s["rnk"], r + 1))
                q = claim(pe, 5, ("cnt", r), (s["cnt"], r + 1))
                for t in range(TILES):
                    pe.wait_ge(s["sel"], r * TILES + t + 1)
                    for j in range(t + 1):
                        ins = mm(p[:, t * E1:(t + 1) * E1], tri_lt if j == t else ones, sel[:, j, :],
                                 start=(j == 0), stop=(j == t))
                ins.then_inc(full[4], 1)
                for t in range(TILES):
                    ins = mm(q[:, 0:E1], ones, sel[:, t, :], start=(t == 0), stop=(t == TILES - 1))
                ins.then_inc(full[5], 1)
                pe.wait_ge(s["blk"], r + 1)
                p = claim(pe, 6, ("blk", r), (s["blki"], 2 * r + 2))
                nc.tensor.transpose(p[0:1, 0:P], blk_e[:, :], ident).then_inc(full[6], 1)
                pe.wait_ge(s["blki"], 2 * r + 2)

                for k in range(8):
                    if free_at[k] is not None:
                        pe.wait_ge(*free_at[k])
                    free_at[k] = ((s["xbT"], s["h"], s["hT"], s["yb"])[k // 2], (r + 1) * NBLK)
                base = r * NBLK

                def step(stage, m, c, first):
                    j, k = 4 * m + c, c % 2
                    if stage == TURN_X:
                        pe.wait_ge(xb_in[c % 4], (m + (c // 4 + 1 + r * NBLK // 4)) * 16)
                        if not first:
                            pe.wait_ge(s["xbT"], j + (base - 1))
                        for i in range(DC):
                            ins = nc.tensor.transpose(bank[k][:, i * P:(i + 1) * P], xb[:, c % 4, i * P:(i + 1) * P], ident)
                        ins.then_inc(s["turned"], 1)
                    if stage == GATE_UP:
                        e = nc.tensor.value_load(blk_i[0:1, 0, bass.ds(j, 1)], min_val=0, max_val=(E1 - 1) * 2 * FI)
                        pe.wait_ge(s["xbT"], j + (base + 1))
                        if not first:
                            pe.wait_ge(s["h"], j + (base - 1))
                        for i in range(DC):
                            ins = mm(bank[2 + k][:, 0:2 * FI], xbT[:, k, i, :], gu_w[:, i, bass.ds(e, 2 * FI)],
                                     start=(i == 0), stop=(i == DC - 1))
                        ins.then_inc(s["gu"], 1)
                    if stage == TURN_H:
                        pe.wait_ge(s["h"], j + (base + 1))
                        if not first:
                            pe.wait_ge(s["hT"], j + (base - 1))
                        nc.tensor.transpose(bank[4 + k][0:FI, 0:P], hh[:, k, :], ident).then_inc(s["hturned"], 1)
                    if stage == DOWN:
                        e = nc.tensor.value_load(blk_i[0:1, 1, bass.ds(j, 1)], min_val=0, max_val=(E1 - 1) * D)
                        pe.wait_ge(s["hT"], j + (base + 1))
                        if not first:
                            pe.wait_ge(s["yb"], j + (base - 1))
                        mm(bank[6 + k][:, 0:D], hT[:, k, :], dn_w[:, bass.ds(e, D)],
                           start=True, stop=True).then_inc(s["down"], 1)

                over_blocks(pe, step)

            run = {RWKV: rwkv, MAMBA: mamba}
            for layer in range(LAYERS):
                if layer in (MOE0, MOE0B):
                    moe0(layer)
                elif layer in (ATTA, ATTB):
                    attention(layer)
                elif layer in (MOE1, MOE1B):
                    moe1(layer)
                else:
                    run[layer]()

        @block.scalar
        def _(act):
            steps = Steps(act, act_step)

            def xT_copy(layer, t):
                n = layer * TILES + t
                act.wait_ge(*filled(("xT", n)))
                b = t // HALVES
                nc.scalar.activation(xcols(t), filled_bank(("xT", n))[:, 0:D].rearrange("p (c n) -> p c n", c=DC),
                                     ACT.Copy).then_inc(xT_ready, 1)

            def rwkv():
                for t in range(TILES):
                    xT_copy(RWKV, t)
                for b in range(B):
                    act.wait_ge(rs["mix"], MIXES * b + DC)
                    nc.scalar.activation(mix[2][:, :, b, :], mix[2][:, :, b, :], ACT.Silu).then_inc(rs["silu"], 1)
                for b in range(B):
                    act.wait_ge(rs["td"], b + 1)
                    if b >= 1:
                        act.wait_ge(rs["ab"], b)
                    nc.scalar.activation(rw_e2, rw_d, ACT.Exp)
                    for c in range(DC):
                        ins = nc.scalar.activation(rw_e1[:, c, :], rw_t[:, c, :], ACT.Exp, bias=negw[:, c:c + 1], scale=-1.0)
                    ins.then_inc(rs["exp"], 1)

            def moe0(layer):
                base = (0 if layer == MOE0 else 1) * TILES

                def route(t):
                    n = base + t
                    xT_copy(layer, t)
                    act.wait_ge(*filled(("lg0", n)))
                    if n >= 2:
                        act.wait_ge(m0["cmb"], n - 1)
                    nc.scalar.activation(lg0[:, t % 2, :], filled_bank(("lg0", n))[:, 0:E0], ACT.Copy).then_inc(m0["lg"], 1)
                    act.wait_ge(m0["nmx"], n + 1)
                    nc.scalar.activation(ex0[:, t % 2, :], lg0[:, t % 2, :], ACT.Exp, bias=sc0[:, t % 2, 0:1],
                                         accum_out=sc0[:, t % 2, 1:2]).then_inc(m0["sum"], 1)

                route(0)
                for t in range(TILES):
                    if t + 1 < TILES:
                        route(t + 1)
                    act.wait_ge(*filled(("cmbT", base + t)))
                    if base + t >= 1:
                        act.wait_ge(*filled(("bias0", base + t - 1)))
                    nc.scalar.activation(cmbT, filled_bank(("cmbT", base + t))[0:E0, 0:P], ACT.Copy).then_inc(m0["cmbT"], 1)

            def mamba():
                layer = MAMBA
                nc.scalar.activation(a_row, a_log, ACT.Exp).then_inc(ms["dtneg"], 1)
                for t in range(TILES):
                    xT_copy(layer, t)
                act.wait_ge(ms["spu"], 1)
                nc.scalar.activation(sp_e, sp_neg, ACT.Exp).then_inc(ms["spe"], 1)
                act.wait_ge(ms["spu"], 2)
                nc.scalar.activation(sp_l, sp_u, ACT.Ln).then_inc(ms["spl"], 1)

                def conv(b):
                    for i in range(3):
                        act.wait_ge(*filled(("conv", b, i)))
                        if i == 0 and b >= 2:
                            act.wait_ge(ms["cvs"], 2 * (b - 1))
                        n = P if i < 2 else MN
                        for j in range(2):
                            ch = 2 * i + j
                            nc.scalar.activation(hcv[0:n, b % 2, ch, :], filled_bank(("conv", b, i))[0:n, j * T:(j + 1) * T],
                                                 ACT.Identity, bias=mb_conv[0:n, ch, TAPS:TAPS + 1],
                                                 scale=mb_conv[0:n, ch, TAPS - 1:TAPS]).then_inc(ms["cv"], 1)

                def silus(b):
                    act.wait_ge(ms["tap"], 3 * CHUNKS * (b + 1))
                    nc.scalar.activation(hs[:, :, b, :], hcv[:, b % 2, 0:MC, :], ACT.Silu).then_inc(ms["cvs"], 1)
                    nc.scalar.activation(bc[:, :, b, :], hcv[0:MN, b % 2, MC:CHUNKS, :], ACT.Silu).then_inc(ms["cvs"], 1)
                    for h in range(HALVES):
                        t = b * HALVES + h
                        act.wait_ge(*filled(("gate", t)))
                        nc.scalar.activation(sg[:, t, :], filled_bank(("gate", t))[:, :], ACT.Silu).then_inc(ms["sg"], 1)

                conv(0)
                for b in range(B):
                    if b + 1 < B:
                        conv(b + 1)
                    silus(b)

                for t in range(TILES):
                    b, h = t // HALVES, t % HALVES
                    act.wait_ge(*filled(("htok", t)))
                    if t >= 2:
                        act.wait_ge(*filled(("ydiag", t - 2)))
                        act.wait_ge(ms["dh"], t - 1)
                        act.wait_ge(ms["hdec"], (t - 2) // 2 + 1)
                    nc.scalar.activation(htok[:, t % 2, :], filled_bank(("htok", t))[:, :], ACT.Copy).then_inc(ms["htok"], 1)
                    if h == 0:
                        act.wait_ge(*filled(("btok", b)))
                        if b >= 1:
                            act.wait_ge(*filled(("state", b - 1)))
                        nc.scalar.activation(btok, filled_bank(("btok", b))[:, 0:MN], ACT.Copy).then_inc(ms["btok"], 1)
                        act.wait_ge(*filled(("suf", b)))
                        if b >= 1:
                            act.wait_ge(ms["dsc"], b)
                        nc.scalar.activation(esuf, filled_bank(("suf", b))[:, 0:MH], ACT.Exp).then_inc(ms["esuf"], 1)
                    else:
                        act.wait_ge(*filled(("pre", b)))
                        if b >= 1:
                            act.wait_ge(ms["y1"], b)
                        nc.scalar.activation(epre, filled_bank(("pre", b))[:, 0:MH], ACT.Exp).then_inc(ms["epre"], 1)
                    for q in range(2):
                        act.wait_ge(*filled(("seg", t, q)))
                        if t >= 1:
                            act.wait_ge(ms["mt"], MH * (t - 1) + 4 * q + 4)
                        nc.scalar.activation(Lx[:, 4 * q:4 * q + 4, :],
                                             filled_bank(("seg", t, q))[:, :].rearrange("p (i n) -> p i n", i=4),
                                             ACT.Exp).then_inc(ms["L"], 1)
                    if h == 0:
                        act.wait_ge(*filled(("state", b)))
                        if b >= 1:
                            act.wait_ge(*filled(("yoff", b - 1)))
                        nc.scalar.activation(mst, filled_bank(("state", b))[0:MN, :], ACT.Copy).then_inc(ms["st"], 1)
                    act.wait_ge(ms["yf"], t + 1)
                    if t >= 1:
                        steps.after(steps.n)
                    ins = nc.scalar.activation(ysq, yf, ACT.Square, accum_out=mss[:, t:t + 1])
                    steps.mark(ins)

            def attention(layer):
                r = (layer - ATTA) // 2
                for b in range(B):
                    for h in range(HALVES):
                        xT_copy(layer, b * HALVES + h)
                    for i in range(NS * NG):
                        n = (r * B + b) * NS * NG + i
                        act.wait_ge(as_["nmax"], 2 * (n + 1))
                        if n >= 3:
                            act.wait_ge(*filled(("turn", n - 3)))
                        p = filled_bank(("score", n))
                        nc.scalar.activation(pexp[:, n % 3, 0:P], p[:, 0:P], ACT.Exp, bias=nmax[:, n % 4, 0:1])
                        nc.scalar.activation(pexp[:, n % 3, P:3 * P], p[:, P:3 * P], ACT.Exp,
                                             bias=nmax[:, n % 4, 1:2]).then_inc(as_["exp"], 1)
                    for h in range(HALVES):
                        m = r * TILES + b * HALVES + h
                        act.wait_ge(*filled(("ctxT", m)))
                        if m >= 1:
                            act.wait_ge(*filled(("ato", m - 1)))
                        nc.scalar.activation(ctxT, filled_bank(("ctxT", m))[:, 0:D].rearrange("p (c n) -> p c n", c=DC),
                                             ACT.Copy).then_inc(as_["ctxT"], 1)

            def moe1(layer):
                r = (layer - MOE1) // 2
                s = mo_s
                for t in range(TILES):
                    n = r * TILES + t
                    xT_copy(layer, t)
                    act.wait_ge(*filled(("lg1", n)))
                    nc.scalar.activation(lg1[:, t, :], filled_bank(("lg1", n))[:, 0:E1], ACT.Copy).then_inc(s["lg"], 1)
                for t in range(TILES):
                    n = r * TILES + t
                    act.wait_ge(s["nmx"], n + 1)
                    nc.scalar.activation(wts[:, t, :], mx1[:, t, 0:TOPK], ACT.Exp, bias=nmx1[:, t:t + 1],
                                         accum_out=wsum[:, t:t + 1]).then_inc(s["exw"], 1)
                base = r * NBLK

                def step(stage, m, c, first):
                    j, k = 4 * m + c, c % 2
                    if stage == TURN_X:
                        act.wait_ge(s["turned"], j + (base + 1))
                        if not first:
                            act.wait_ge(s["gu"], j + (base - 1))
                        nc.scalar.activation(xbT[:, k, :, :], bank[k][:, 0:D].rearrange("p (c n) -> p c n", c=DC),
                                             ACT.Copy).then_inc(s["xbT"], 1)
                        if c + NXB < NBLK:
                            load(j + NXB, c % NXB)
                    if stage == GATE_UP:
                        act.wait_ge(s["gu"], j + (base + 1))
                        if not first:
                            act.wait_ge(s["h"], j + (base - 1))
                        nc.scalar.activation(sgt[:, k, :], bank[2 + k][:, 0:FI], ACT.Silu).then_inc(s["sg"], 1)
                    if stage == TURN_H:
                        act.wait_ge(s["hturned"], j + (base + 1))
                        if not first:
                            act.wait_ge(s["down"], j + (base - 1))
                        nc.scalar.activation(hT[:, k, :], bank[4 + k][0:FI, 0:P], ACT.Copy).then_inc(s["hT"], 1)

                def load(j, k):
                    act.dma_start(xb[:, k, :], xg[bass.ds(j * P, P), :]).then_inc(xb_in[k], 16)

                act.wait_ge(s["scat"], 16 * TILES * TOPK * (r + 1))
                for k in range(NXB):
                    load(k, k)
                over_blocks(act, step)

            act.wait_ge(prep, PREPS)
            for layer in range(LAYERS):
                if layer in (MOE0, MOE0B):
                    moe0(layer)
                elif layer in (ATTA, ATTB):
                    attention(layer)
                elif layer in (MOE1, MOE1B):
                    moe1(layer)
                else:
                    {RWKV: rwkv, MAMBA: mamba}[layer]()

        @block.vector
        def _(dve):
            V = nc.vector
            steps = Steps(dve, dve_step)

            def ln_stats(layer, t):
                n = layer * TILES + t
                if layer == 0:
                    dve.wait_ge(x_in[t], 16)
                else:
                    dve.wait_ge(x_ready, n - TILES + 1)
                k = n % 8
                steps.link(V.bn_stats(st6[:, k, :], X[:, t, :]))
                steps.link(V.bn_aggr(mv[:, k, :], st6[:, k, :]))
                V.tensor_scalar(ve[:, k, :], mv[:, k, 1:2], LN_EPS, None, ALU.add).then_inc(ln_var, 1)

            def ln_norm(layer, t):
                n = layer * TILES + t
                dve.wait_ge(ln_rstd, n + 1)
                V.tensor_scalar(xn[:, t, :], X[:, t, :], mv[:, n % 8, 0:1], rstd[:, n % 8, :],
                                ALU.subtract, ALU.mult).then_inc(ln_done, 1)

            def ln(layer, tiles):
                for t in tiles:
                    ln_stats(layer, t)
                for t in tiles:
                    ln_norm(layer, t)

            def rwkv():
                dve.wait_ge(w_in["small"], 16 * SMALLS)
                V.tensor_scalar(negw[:, :], w_c, -1.0, None, ALU.mult).then_inc(rs["col"], 1)
                V.tensor_tensor(ubk[:, :], u_c, wk_c, ALU.add).then_inc(rs["col"], 1)
                for b in range(B):
                    ln(RWKV, range(b * HALVES, (b + 1) * HALVES))

                def mixes(b):
                    dve.wait_ge(rs["diff"], b + 1)
                    for i, m in enumerate((tmr, tmk, tmv)):
                        for c in range(DC):
                            V.scalar_tensor_tensor(mix[(2, 0, 1)[i]][:, c, b, :], rw_diff[:, b % 2, c, :], m[:, c:c + 1],
                                                   xT[:, c, b, 0:T], ALU.mult, ALU.add).then_inc(rs["mix"], 1)

                def recurrence(b):
                    dve.wait_ge(*filled(("kvr", b, 0)))
                    k_ = filled_bank(("kvr", b, 0))
                    if b >= 1:
                        dve.wait_ge(rs["exp"], b)
                    dve.wait_ge(rs["col"], 2)
                    for c in range(DC):
                        steps.mark(V.tensor_scalar(rw_t[:, c, :], k_[:, c * T:(c + 1) * T], ubk[:, c:c + 1], w_c[:, c:c + 1],
                                                   ALU.add, ALU.max))
                    steps.after(steps.n)
                    for c in range(DC):
                        ins = V.scalar_tensor_tensor(rw_d[:, c, :], k_[:, c * T:(c + 1) * T], ubk[:, c:c + 1], rw_t[:, c, :],
                                                     ALU.add, ALU.subtract)
                    ins.then_inc(rs["td"], 1)
                    dve.wait_ge(rs["exp"], b + 1)
                    dve.wait_ge(*filled(("kvr", b, 1)))
                    v_ = filled_bank(("kvr", b, 1))
                    for c in range(DC):
                        steps.mark(V.scalar_tensor_tensor(rw_ev[:, c, :], v_[:, c * T:(c + 1) * T], wv_c[:, c:c + 1],
                                                          rw_e2[:, c, :], ALU.add, ALU.mult))
                    for c in range(DC):
                        steps.mark(V.tensor_tensor_scan(rw_b[:, c, :], rw_e1[:, c, :], rw_e2[:, c, :], 0.0, ALU.mult, ALU.add))
                    steps.after(steps.n)
                    rb = steps.mark(V.reciprocal(rw_rb, rw_b))
                    for c in range(DC):
                        ins = V.tensor_tensor_scan(rw_a[:, c, :], rw_e1[:, c, :], rw_ev[:, c, :], 0.0, ALU.mult, ALU.add)
                    ins.then_inc(rs["ab"], 1)
                    dve.wait_ge(rs["ab"], b + 1)
                    steps.after(rb)
                    steps.link(V.tensor_tensor(rw_q, rw_a, rw_rb, ALU.mult))
                    dve.wait_ge(*filled(("kvr", b, 2)))
                    if b >= 1:
                        dve.wait_ge(*filled(("rwo", b * HALVES - 1)))
                    r_ = filled_bank(("kvr", b, 2))
                    for c in range(DC):
                        ins = V.scalar_tensor_tensor(rw_z[:, c, :], r_[:, c * T:(c + 1) * T], wr_c[:, c:c + 1],
                                                     rw_q[:, c, :], ALU.add, ALU.mult)
                    ins.then_inc(rs["z"], 1)

                def residual(b):
                    for h in range(HALVES):
                        t = b * HALVES + h
                        dve.wait_ge(*filled(("rwo", t)))
                        dve.wait_ge(xb_ready, t + 1)
                        V.tensor_tensor(X[:, t, :], filled_bank(("rwo", t))[:, 0:D], X[:, t, :], ALU.add).then_inc(x_ready, 1)

                for b in range(B):
                    mixes(b)
                for b in range(B):
                    recurrence(b)
                    residual(b)

            def moe0(layer):
                base = (0 if layer == MOE0 else 1) * TILES

                def route(t):
                    n, k = base + t, t % 2
                    ln(layer, [t])
                    dve.wait_ge(m0["lg"], n + 1)
                    if n >= 2:
                        steps.after(steps.n)
                    steps.link(V.max(mx0[:, k, :], lg0[:, k, :]))
                    V.tensor_scalar(sc0[:, k, 0:1], mx0[:, k, 0:1], -1.0, None, ALU.mult).then_inc(m0["nmx"], 1)
                    steps.link(V.max_index(ix0[:, k, :], mx0[:, k, :], lg0[:, k, :]))
                    steps.mark(V.tensor_copy(sc0[:, k, 3:4], ix0[:, k, 0:1]))
                    dve.wait_ge(m0["sum"], n + 1)
                    steps.link(V.reciprocal(sc0[:, k, 2:3], sc0[:, k, 1:2]))
                    if n >= 2:
                        dve.wait_ge(m0["cmbT"], n - 1)
                    V.tensor_scalar(cmb[:, k, :], iota_row[:, 0:E0], sc0[:, k, 3:4], sc0[:, k, 2:3],
                                    ALU.is_equal, ALU.mult).then_inc(m0["cmb"], 1)

                route(0)
                for t in range(TILES):
                    if t + 1 < TILES:
                        route(t + 1)
                    n = base + t
                    dve.wait_ge(m0["cmb"], n + 1)
                    if n >= 1:
                        dve.wait_ge(x_ready, layer * TILES + t)
                    for e in range(E0):
                        dve.wait_ge(*filled(("ex0", n, e // 2)))
                        if e:
                            dve.wait_ge(m0["ex"], E0 * n + e)
                        V.scalar_tensor_tensor(acc, filled_bank(("ex0", n, e // 2))[:, (e % 2) * D:(e % 2 + 1) * D],
                                               cmb[:, t % 2, e:e + 1], acc if e else X[:, t, :],
                                               ALU.mult, ALU.add).then_inc(m0["ex"], 1)
                    dve.wait_ge(*filled(("bias0", n)))
                    dve.wait_ge(m0["ex"], E0 * (n + 1))
                    V.tensor_tensor(X[:, t, :], filled_bank(("bias0", n))[:, 0:D], acc, ALU.add).then_inc(x_ready, 1)

            def mamba():
                layer = MAMBA
                for b in range(B):
                    ln(layer, range(b * HALVES, (b + 1) * HALVES))
                heads = "p (t h) -> p t h"
                dve.wait_ge(*filled(("dt",)))
                V.tensor_tensor(dtr.rearrange(heads, h=MH), filled_bank(("dt",))[:, 0:TILES * MH].rearrange(heads, h=MH),
                                dt_bias.unsqueeze(1).to_broadcast([P, TILES, MH]), ALU.add).then_inc(ms["dtr"], 1)
                dve.wait_ge(ms["dtr"], 1)
                V.scalar_tensor_tensor(sp_neg, dtr, -1.0, dtr, ALU.mult, ALU.min).then_inc(ms["spu"], 1)
                dve.wait_ge(ms["spe"], 1)
                V.tensor_scalar(sp_u, sp_e, 1.0, None, ALU.add).then_inc(ms["spu"], 1)
                dve.wait_ge(ms["spu"], 2)
                steps.link(V.tensor_scalar(sp_d, sp_u, -1.0, None, ALU.add))
                steps.link(V.tensor_scalar(sp_mask, sp_d, 0.0, None, ALU.is_equal))
                steps.link(V.tensor_tensor(sp_d, sp_d, sp_mask, ALU.add))
                steps.link(V.reciprocal(sp_q, sp_d))
                dve.wait_ge(ms["spl"], 1)
                steps.link(V.tensor_tensor(sp_q, sp_q, sp_l, ALU.mult))
                steps.link(V.tensor_tensor(sp_q, sp_q, sp_mask, ALU.add))
                steps.link(V.tensor_tensor(sp_q, sp_q, sp_e, ALU.mult))
                steps.link(V.scalar_tensor_tensor(dt, dtr, 0.0, sp_q, ALU.max, ALU.add))
                dve.wait_ge(ms["dtneg"], 1)
                V.scalar_tensor_tensor(a_d.rearrange(heads, h=MH), dt.rearrange(heads, h=MH), -1.0,
                                       a_row[:, :].unsqueeze(1).to_broadcast([P, TILES, MH]),
                                       ALU.mult, ALU.mult).then_inc(ms["ad"], 1)
                for b in range(B):
                    for k in range(TAPS - 1):
                        sh = k + 1
                        for ch in range(CHUNKS):
                            n = P if ch < MC else MN
                            if k == 0:
                                dve.wait_ge(ms["cv"], CHUNKS * b + ch // 2 * 2 + 2)
                            else:
                                dve.wait_ge(ms["tap"], 3 * CHUNKS * b + CHUNKS * (k - 1) + ch + 1)
                            src = filled_bank(("conv", b, ch // 2))[0:n, (ch % 2) * T:(ch % 2 + 1) * T - sh]
                            V.scalar_tensor_tensor(hcv[0:n, b % 2, ch, sh:T], src,
                                                   mb_conv[0:n, ch, TAPS - 1 - sh:TAPS - sh], hcv[0:n, b % 2, ch, sh:T],
                                                   ALU.mult, ALU.add).then_inc(ms["tap"], 1)

                def project(t):
                    dve.wait_ge(*filled(("yfT", t)))
                    if t >= 1:
                        dve.wait_ge(*filled(("mbo", t - 1)))
                    V.tensor_tensor(yfT, filled_bank(("yfT", t))[:, :].rearrange("p (c n) -> p c n", c=MC),
                                    mb_norm[:, :].unsqueeze(2).to_broadcast([P, MC, P]), ALU.mult).then_inc(ms["yfT"], 1)
                    dve.wait_ge(act_step, t + 1)
                    V.tensor_scalar(mvar[:, t:t + 1], mss[:, t:t + 1], 1.0 / ME, RMS_EPS, ALU.mult, ALU.add).then_inc(ms["var"], 1)
                    dve.wait_ge(ms["rs"], t + 1)
                    dve.wait_ge(*filled(("mbo", t)))
                    V.scalar_tensor_tensor(X[:, t, :], filled_bank(("mbo", t))[:, 0:D], mrs[:, t:t + 1], X[:, t, :],
                                           ALU.mult, ALU.add).then_inc(x_ready, 1)

                wide = "p (h n) -> p h n"
                for t in range(TILES):
                    b, h = t // HALVES, t % HALVES
                    dve.wait_ge(*filled(("gm", t)))
                    if t >= 1:
                        dve.wait_ge(ms["mt"], MH * t)
                    V.tensor_tensor(gm, filled_bank(("gm", t))[:, 0:P], tri_le, ALU.mult).then_inc(ms["gm"], 1)
                    if h == 0:
                        dve.wait_ge(ms["esuf"], b + 1)
                        if b >= 1:
                            dve.wait_ge(ms["hdec"], b)
                        V.tensor_tensor(dsc[:, :], esuf[:, :], dt[:, t * MH:(t + 1) * MH], ALU.mult).then_inc(ms["dsc"], 1)
                    dve.wait_ge(ms["gm"], t + 1)
                    if t >= 1:
                        dve.wait_ge(*filled(("ydiag", t - 1)))
                    for i in range(MH):
                        if i % 4 == 0:
                            dve.wait_ge(ms["L"], 2 * t + i // 4 + 1)
                        V.scalar_tensor_tensor(mt[:, i, :], Lx[:, i, :], dt[:, t * MH + i:t * MH + i + 1], gm,
                                               ALU.mult, ALU.mult).then_inc(ms["mt"], 1)
                    if t >= 1:
                        project(t - 1)
                    dve.wait_ge(*filled(("ydiag", t)))
                    dve.wait_ge(ms["dh"], t + 1)
                    if t >= 1:
                        dve.wait_ge(*filled(("yfT", t - 1)))
                        dve.wait_ge(act_step, t)
                    yd = filled_bank(("ydiag", t))
                    V.tensor_tensor(yf, yd[:, :], dh, ALU.add).then_inc(ms["y"], 1)
                    dve.wait_ge(ms["y"], t + 1)
                    if h == 1:
                        dve.wait_ge(*filled(("yoff", b)))
                        dve.wait_ge(ms["epre"], b + 1)
                        V.tensor_tensor(y1.rearrange(wide, h=MH), filled_bank(("yoff", b))[:, :].rearrange(wide, h=MH),
                                        epre[:, :].unsqueeze(2).to_broadcast([P, MH, MP]), ALU.mult).then_inc(ms["y1"], 1)
                        dve.wait_ge(ms["y1"], b + 1)
                        steps.link(V.tensor_tensor(yf, yf, y1, ALU.add))
                    dve.wait_ge(ms["sg"], t + 1)
                    V.tensor_tensor(yf, yf, sg[:, t, :], ALU.mult).then_inc(ms["yf"], 1)
                project(TILES - 1)

            def attention(layer):
                r = (layer - ATTA) // 2

                def qkv(b):
                    n = r * B + b
                    if n == 0:
                        dve.wait_ge(prep, PREPS)
                    for i in range(2):
                        dve.wait_ge(*filled(("q", n, i)))
                        src = filled_bank(("q", n, i))[:, :].rearrange("p (s n) -> p s n", s=2)
                        if layer == ATTA:
                            ins = V.tensor_scalar(qT[:, 2 * i:2 * i + 2, :], src, HD ** -0.5, None, ALU.mult)
                        else:
                            ins = V.scalar_tensor_tensor(qT[:, 2 * i:2 * i + 2, :], src, HD ** -0.5,
                                                         al_q[:, 2 * i:2 * i + 2, :], ALU.mult, ALU.add)
                        ins.then_inc(as_["qkv"], 1)
                    dve.wait_ge(*filled(("kv", n)))
                    src = filled_bank(("kv", n))
                    if layer == ATTA:
                        ins = V.tensor_copy(kT, src[:, 0:T])
                    else:
                        ins = V.tensor_tensor(kT, src[:, 0:T], al_k[:, :], ALU.add)
                    ins.then_inc(as_["qkv"], 1)
                    V.tensor_copy(vt[:, :, :, 0:HD],
                                  src[:, T:T + HALVES * NG * HD].rearrange("p (h g d) -> p h g d", h=HALVES, g=NG)
                                  ).then_inc(as_["qkv"], 1)

                def maxima(b, i):
                    n = (r * B + b) * NS * NG + i
                    dve.wait_ge(*filled(("score", n)))
                    if n >= 4:
                        dve.wait_ge(as_["exp"], n - 3)
                    p = filled_bank(("score", n))
                    V.tensor_reduce(nmax[:, n % 4, 0:1], p[:, 0:P], AX_X, ALU.max, negate=True).then_inc(as_["nmax"], 1)
                    V.tensor_reduce(nmax[:, n % 4, 1:2], p[:, P:3 * P], AX_X, ALU.max, negate=True).then_inc(as_["nmax"], 1)

                def weights(b, i):
                    n = (r * B + b) * NS * NG + i
                    dve.wait_ge(*filled(("turn", n)))
                    V.tensor_copy(pT[:, n % 3, :], filled_bank(("turn", n))[:, 0:3 * P]).then_inc(as_["pT"], 1)

                HEADS = NS * NG
                ln(layer, range(HALVES))
                for b in range(B):
                    qkv(b)
                    if b + 1 < B:
                        ln(layer, range((b + 1) * HALVES, (b + 2) * HALVES))
                    maxima(b, 0)
                    maxima(b, 1)
                    for i in range(HEADS):
                        if i + 2 < HEADS:
                            maxima(b, i + 2)
                        weights(b, i)
                    for h in range(HALVES):
                        t = b * HALVES + h
                        m = r * TILES + t
                        dve.wait_ge(*filled(("av", m)))
                        av = filled_bank(("av", m))[:, 0:HEADS * VW].rearrange("p (i d) -> p i d", d=VW)
                        if m >= 1:
                            dve.wait_ge(as_["ctx"], m)
                        steps.link(V.reciprocal(rsum.unsqueeze(2), av[:, :, HD:VW]))
                        if m >= 2:
                            dve.wait_ge(*filled(("ctxT", m - 2)))
                        V.tensor_tensor(ctx_t[:, t % 2, :].rearrange("p (i d) -> p i d", d=HD), av[:, :, 0:HD],
                                        rsum.unsqueeze(2).to_broadcast([P, HEADS, HD]), ALU.mult).then_inc(as_["ctx"], 1)
                    for h in range(HALVES):
                        t = b * HALVES + h
                        m = r * TILES + t
                        dve.wait_ge(*filled(("ato", m)))
                        dve.wait_ge(xb_ready, BIASED[layer] * TILES + t + 1)
                        V.tensor_tensor(X[:, t, :], filled_bank(("ato", m))[:, 0:D], X[:, t, :], ALU.add).then_inc(x_ready, 1)

            def moe1(layer):
                r = (layer - MOE1) // 2
                s = mo_s
                for t in range(TILES):
                    ln(layer, [t])
                    if t >= 1:
                        pick(layer, r, t - 1)
                pick(layer, r, TILES - 1)
                dve.wait_ge(*filled(("rnk", r)))
                V.tensor_copy(rnk[:, :, :], filled_bank(("rnk", r))[:, 0:TILES * E1].rearrange("p (t e) -> p t e", e=E1)
                              ).then_inc(s["rnk"], 1)
                dve.wait_ge(*filled(("cnt", r)))
                V.tensor_scalar(cnt_i[:, 0, :], filled_bank(("cnt", r))[:, 0:E1], float(P - 1), None,
                                ALU.add).then_inc(s["cnt"], 1)
                dve.wait_ge(s["cnt"], r + 1)
                steps.link(V.tensor_scalar(cnt_i[:, 1, :], cnt_i[:, 0, :], P.bit_length() - 1, None,
                                           ALU.logical_shift_right))
                steps.link(V.tensor_copy(nblk[:, :], cnt_i[:, 1, :]))
                steps.link(V.tensor_tensor_scan(cum[:, :], ones[:, 0:E1], nblk[:, :], 0.0, ALU.mult, ALU.add))
                V.tensor_scalar(blk_c[:, :], cum[:, :], iota_col, None, ALU.is_le, ALU.add,
                                accum_out=blk_e[:, :]).then_inc(s["blk"], 1)
                steps.link(V.tensor_tensor(start[:, :], cum[:, :], nblk[:, :], ALU.subtract))
                dve.wait_ge(s["rnk"], r + 1)
                steps.link(V.scalar_tensor_tensor(pos, start[:, :].unsqueeze(1).to_broadcast([P, TILES, E1]), float(P),
                                                  rnk[:, :, :], ALU.mult, ALU.add))
                for t in range(TILES):
                    steps.mark(V.tensor_tensor(oh[:, t, :, :], oh[:, t, :, :],
                                               pos[:, t, :].unsqueeze(1).to_broadcast([P, TOPK, E1]), ALU.mult))
                steps.after(steps.n)
                steps.link(V.tensor_reduce(slot_f[:, :, :], oh, AX_X, ALU.add))
                V.tensor_copy(slot[:, :], slot_f[:, :, :].rearrange("p t k -> p (t k)")).then_inc(s["slot"], 1)
                dve.wait_ge(*filled(("blk", r)))
                for i, width in enumerate((2 * FI, D)):
                    V.tensor_scalar(blk_i[0:1, i, :], filled_bank(("blk", r))[0:1, 0:P], float(E1 - 1), float(width),
                                    ALU.min, ALU.mult).then_inc(s["blki"], 1)
                dve.wait_ge(s["exw"], (r + 1) * TILES)
                steps.link(V.reciprocal(wsum[:, :], wsum[:, :]))
                V.tensor_tensor(wts[:, :, :], wts[:, :, :], wsum[:, :].unsqueeze(2).to_broadcast([P, TILES, TOPK]),
                                ALU.mult).then_inc(s["ws"], 1)
                base = r * NBLK

                def step(stage, m, c, first):
                    j, k = 4 * m + c, c % 2
                    if stage == GATE_UP:
                        dve.wait_ge(s["sg"], j + (base + 1))
                        if not first:
                            dve.wait_ge(s["hturned"], j + (base - 1))
                        V.tensor_tensor(hh[:, k, :], sgt[:, k, :], bank[2 + k][:, FI:2 * FI], ALU.mult).then_inc(s["h"], 1)
                    if stage == DOWN:
                        dve.wait_ge(s["down"], j + (base + 1))
                        if c + base >= NXB:
                            dve.wait_ge(y_out[c % NXB], (m + (c // NXB + base // NXB)) * 16)
                        V.tensor_copy(yb[:, c % NXB, :], bank[6 + k][:, 0:D]).then_inc(s["yb"], 1)

                over_blocks(dve, step)
                dve.wait_ge(s["ws"], r + 1)
                for t in range(TILES):
                    for k in range(TOPK):
                        i = t * TOPK + k
                        dve.wait_ge(y_in[i % NYG], 16 * (i // NYG + 1 + r * TILES * TOPK // NYG))
                        if k:
                            dve.wait_ge(s["comb"], 3 * (r * TILES + t) + k)
                        ins = V.scalar_tensor_tensor(X[:, t, :], yg[:, i % NYG, :], wts[:, t, k:k + 1], X[:, t, :],
                                                     ALU.mult, ALU.add)
                        ins.then_inc(s["comb"] if k < TOPK - 1 else x_ready, 1)

            def pick(layer, r, t):
                s = mo_s
                n = r * TILES + t
                dve.wait_ge(s["lg"], n + 1)
                steps.link(V.max(mx1[:, t, :], lg1[:, t, :]))
                V.tensor_scalar(nmx1[:, t:t + 1], mx1[:, t, 0:1], -1.0, None, ALU.mult).then_inc(s["nmx"], 1)
                steps.link(V.max_index(ix1[:, t, :], mx1[:, t, :], lg1[:, t, :]))
                steps.link(V.tensor_copy(ixf[:, t, :], ix1[:, t, 0:TOPK]))
                steps.link(V.tensor_tensor(oh[:, t, :, :], iota_row.unsqueeze(1).to_broadcast([P, TOPK, E1]),
                                           ixf[:, t, :].unsqueeze(2).to_broadcast([P, TOPK, E1]), ALU.is_equal))
                V.tensor_reduce(sel[:, t, :], oh[:, t, :, :].rearrange("p k e -> p e k"), AX_X, ALU.add).then_inc(s["sel"], 1)

            dve.wait_ge(w_in["mats"], 16)
            for layer in range(LAYERS):
                if layer in (MOE0, MOE0B):
                    moe0(layer)
                elif layer in (ATTA, ATTB):
                    attention(layer)
                elif layer in (MOE1, MOE1B):
                    moe1(layer)
                else:
                    {RWKV: rwkv, MAMBA: mamba}[layer]()

        @block.gpsimd
        def _(pool):
            G = nc.gpsimd

            def ln_pow(layer, t):
                n = layer * TILES + t
                pool.wait_ge(ln_var, n + 1)
                G.tensor_tensor(rstd[:, n % 8, :], ve[:, n % 8, :], neghalf[:, :], ALU.pow).then_inc(ln_rstd, 1)

            def add_bias(layer, t):
                pool.wait_ge(ln_done, layer * TILES + t + 1)
                G.tensor_tensor(X[:, t, :], X[:, t, :], bo_row(layer), ALU.add).then_inc(xb_ready, 1)

            def rwkv():
                for t in range(TILES):
                    ln_pow(RWKV, t)
                for b in range(B):
                    pool.wait_ge(xT_ready, (b + 1) * HALVES)
                    if b >= 2:
                        pool.wait_ge(rs["mix"], MIXES * (b - 1))
                    G.tensor_tensor(rw_diff[:, b % 2, :, :], xT[:, :, b, 1:T + 1], xT[:, :, b, 0:T],
                                    ALU.subtract).then_inc(rs["diff"], 1)
                for t in range(TILES):
                    add_bias(RWKV, t)

            def mamba():
                for t in range(TILES):
                    ln_pow(MAMBA, t)
                pool.wait_ge(ms["ad"], 1)

                def decays(t):
                    if t >= 2:
                        pool.wait_ge(*filled(("seg", t - 2, 1)))
                    for i in range(MH):
                        G.tensor_scalar(m1[:, t % 2, i, :], tri_gt, a_d[:, t * MH + i:t * MH + i + 1], 1.0,
                                        ALU.mult, ALU.mult).then_inc(ms["m1"], 1)

                wide = "p (h n) -> p h n"
                decays(0)
                for t in range(TILES):
                    b, h = t // HALVES, t % HALVES
                    if t + 1 < TILES:
                        decays(t + 1)
                    pool.wait_ge(ms["htok"], t + 1)
                    if t >= 1:
                        pool.wait_ge(ms["y"], t)
                    G.tensor_tensor(dh.rearrange(wide, h=MH), htok[:, t % 2, :].rearrange(wide, h=MH),
                                    d_row.unsqueeze(2).to_broadcast([P, MH, MP]), ALU.mult).then_inc(ms["dh"], 1)
                    if h == 0:
                        pool.wait_ge(ms["dsc"], b + 1)
                        if b >= 1:
                            pool.wait_ge(*filled(("state", b - 1)))
                        G.tensor_tensor(hdec.rearrange(wide, h=MH), htok[:, t % 2, :].rearrange(wide, h=MH),
                                        dsc[:, :].unsqueeze(2).to_broadcast([P, MH, MP]), ALU.mult).then_inc(ms["hdec"], 1)
                    if t >= 1:
                        rms(t - 1)
                rms(TILES - 1)

            def rms(t):
                pool.wait_ge(ms["var"], t + 1)
                G.tensor_tensor(mrs[:, t:t + 1], mvar[:, t:t + 1], neghalf[:, :], ALU.pow).then_inc(ms["rs"], 1)

            def attention(layer):
                for t in range(HALVES):
                    ln_pow(layer, t)
                for b in range(B):
                    if b + 1 < B:
                        for h in range(HALVES):
                            ln_pow(layer, (b + 1) * HALVES + h)
                    for h in range(HALVES):
                        add_bias(layer, b * HALVES + h)

            def moe1(layer):
                r = (layer - MOE1) // 2
                s = mo_s
                for t in range(TILES):
                    ln_pow(layer, t)
                if r == 0:
                    pool.wait_ge(xg_zero, 16)
                pool.wait_ge(s["slot"], r + 1)
                for t in range(TILES):
                    for k in range(TOPK):
                        i = t * TOPK + k
                        G.indirect_dma_start(out=xg[:], out_offset=bass.IndirectOffsetOnAxis(ap=slot[:, i:i + 1], axis=0),
                                             in_=xn[:, t, :], in_offset=None).then_inc(s["scat"], 16)
                for k in range(NXB):
                    pool.wait_ge(y_out[k], 16 * (NBLK // NXB) * (r + 1))
                for t in range(TILES):
                    for k in range(TOPK):
                        i = t * TOPK + k
                        if i >= NYG:
                            if k < TOPK - 1:
                                pool.wait_ge(s["comb"], 3 * (r * TILES + t - NYG // TOPK) + k + 1)
                            else:
                                pool.wait_ge(x_ready, layer * TILES + t - NYG // TOPK + 1)
                        G.indirect_dma_start(out=yg[:, i % NYG, :], out_offset=None, in_=yg_d[:],
                                             in_offset=bass.IndirectOffsetOnAxis(ap=slot[:, i:i + 1], axis=0)
                                             ).then_inc(y_in[i % NYG], 16)

            G.memset(xT[:, :, :, 0:1], 0.0).then_inc(prep, 1)
            G.memset(neghalf[:, :], -0.5).then_inc(prep, 1)
            G.memset(zeros[:, :], 0.0).then_inc(prep, 1)
            G.memset(vt[:, :, :, :], 1.0).then_inc(prep, 1)
            pool.wait_ge(w_in["small"], 16 * SMALLS)
            pool.wait_ge(w_in["mats"], 16)
            G.tensor_copy(mask_b[:, :], mask_f).then_inc(prep, 1)
            G.tensor_copy(ident_b[:, :], ident).then_inc(prep, 1)
            pool.wait_ge(prep, PREPS)
            for layer in range(LAYERS):
                if layer in (MOE0, MOE0B):
                    for t in range(TILES):
                        ln_pow(layer, t)
                elif layer in (ATTA, ATTB):
                    attention(layer)
                elif layer in (MOE1, MOE1B):
                    moe1(layer)
                else:
                    {RWKV: rwkv, MAMBA: mamba}[layer]()

        @block.sync
        def _(sp):
            first_use = {"moe0": MOE0, "mamba": MAMBA, "att": ATTA}

            def load(key, tile, name):
                if first_use.get(key, 0) < LAYERS:
                    sp.dma_start(tile, a[name]).then_inc(w_in[key], 16)

            xv = a["x"].rearrange("(t p) d -> p t d", p=P)
            for t in range(TILES):
                sp.dma_start(X[:, t, :], xv[:, t, :]).then_inc(x_in[t], 16)
                if t == 0:
                    load("mats", mats[:, :, :], "mats")
            for tile, name in ((cols, "cols"), (rows, "rows"), (iotas, "iotas"), (mb_conv, "mb_conv"), (mb_norm, "mb_norm"),
                               (al_q, "al_q"), (al_k, "al_k"), (late[:, 0:3 * P], "mask"), (rt_w, "rt_w"), (f0_wg, "f0_wg")):
                load("small", tile[:], name)
            load("rwkv", rw_w[:], "rw_w")
            load("moe0", f0_w[:], "f0_w")
            load("moe0", f0_b[:], "f0_b")
            load("mamba", mb_in[:], "mb_in")
            load("mamba", mb_out[:], "mb_out")
            for tile, name in ((at_q, "at_q"), (at_k, "at_k"), (at_v, "at_v"), (at_o, "at_o")):
                load("att", tile[:], name)
            if LAYERS > MOE1:
                sp.wait_ge(prep, 3)
                sp.dma_start(xg.rearrange("(p n) d -> p (n d)", p=P).rearrange("p (n d) -> p n d", d=512),
                             zeros[:, :].unsqueeze(1).to_broadcast([P, SLOTS * D // P // 512, 512])).then_inc(xg_zero, 16)
                sp.wait_ge(x_ready, (MAMBA + 1) * TILES)
                load("moe1", gu_w, "gu_w")
                load("moe1", dn_w, "dn_w")
            for layer in (MOE1, MOE1B):
                if layer >= LAYERS:
                    break
                base = (layer - MOE1) // 2 * NBLK

                def store(j, c):
                    sp.wait_ge(mo_s["yb"], j + (base + 1))
                    sp.dma_start(yg_d[bass.ds(j * P, P), :], yb[:, c, :]).then_inc(y_out[c], 16)

                with sp.Fori(0, NBLK // NXB) as m:
                    for c in range(NXB):
                        store(NXB * m + c, c)
            ov = out.rearrange("(t p) d -> p t d", p=P)
            for t in range(TILES):
                sp.wait_ge(x_ready, (LAYERS - 1) * TILES + t + 1)
                sp.dma_start(ov[:, t, :], X[:, t, :]).then_inc(out_done, 16)
            sp.wait_ge(out_done, 16 * TILES)
            if LAYERS > MOE1:
                sp.wait_ge(xg_zero, 16)


def kernel(**inputs):
    import numpy as np
    import concourse.bacc as bacc
    from concourse import mybir as mb
    from concourse.bass_utils import run_bass_kernel_spmd

    def np32(name):
        return np.asarray(inputs[name])

    def feature(w):
        return w.reshape(-1, P, w.shape[-1]).transpose(1, 0, 2)

    def column(v):
        return v.reshape(-1, P).T

    def everywhere(v):
        return np.broadcast_to(v, (P, v.shape[-1]))

    L0, L1, L2, L3 = "L0_attn_a_", "L0_attn_b_", "L1_attn_a_", "L1_attn_b_"
    x = np32(L0 + "x")
    f = np.float32
    arrays = {"x": x.reshape(-1, D)}
    arrays["rw_w"] = np.stack([feature(np32(L0 + n).T) for n in ("Wk", "Wv", "Wr", "Wo")], axis=1)
    arrays["cols"] = np.stack([column(np32(L0 + n)) for n in ("bk", "bv", "br", "tmk", "tmv", "tmr", "u", "w")], axis=1)
    arrays["rows"] = everywhere(np.concatenate([np32(L1 + "dt_bias"), np32(L1 + "A_log"), np32(L1 + "D"),
                                                np32(L0 + "bo"), np32(L2 + "bo"), np32(L3 + "bo")]))
    arrays["f0_wg"] = feature(np32("L0_ffn_wg"))
    arrays["f0_w"] = feature(np32("L0_ffn_W").transpose(2, 0, 1).reshape(D, E0 * D))
    arrays["f0_b"] = np32("L0_ffn_b")
    arrays["mb_in"] = feature(np32(L1 + "in_proj_w").T)
    taps = np.concatenate([np32(L1 + "conv_w"), np32(L1 + "conv_b")[:, None]], axis=1)
    conv = np.zeros((P, CHUNKS, TAPS + 1), f)
    conv[:, :MC] = feature(taps[:ME])
    conv[:MN, MC:] = taps[ME:].reshape(2, MN, TAPS + 1).transpose(1, 0, 2)
    arrays["mb_conv"] = conv
    arrays["mb_norm"] = column(np32(L1 + "norm_w"))
    arrays["mb_out"] = feature(np32(L1 + "out_proj_w").T)

    wq_a = np32(L2 + "Wq").reshape(D, NG, NS, HD).transpose(0, 2, 1, 3)
    wq_b = np32(L3 + "Wq").reshape(D, NS, NG, HD)
    wkv = np32(L3 + "Wkv")

    def padded(w):
        out = np.zeros(w.shape[:-1] + (HP,), f)
        out[..., :HD] = w
        return feature(out.reshape(D, -1))

    arrays["at_q"] = np.stack([padded(wq_a), padded(wq_b)], axis=1)
    arrays["at_k"] = np.stack([padded(np32(L2 + "Wk").reshape(D, NG, HD)),
                               padded(wkv[:, :NG * HD].reshape(D, NG, HD))], axis=1)
    arrays["at_v"] = np.stack([feature(np32(L2 + "Wv")), feature(wkv[:, NG * HD:])], axis=1)
    arrays["at_o"] = np.stack([feature(np32(L2 + "Wo")), feature(np32(L3 + "Wo"))], axis=1)
    arrays["rt_w"] = feature(np32("L1_ffn_router_w").T)
    gate_up = np.concatenate([np32("L1_ffn_gate_w"), np32("L1_ffn_up_w")], axis=1)
    arrays["gu_w"] = feature(gate_up.transpose(2, 0, 1).reshape(D, E1 * 2 * FI))
    arrays["dn_w"] = np32("L1_ffn_down_w").transpose(2, 0, 1).reshape(FI, E1 * D)

    i, j = np.arange(P)[:, None], np.arange(P)[None, :]
    arrays["mats"] = np.stack([i == j, i > j, i <= j, i < j, i >= 0 * j], axis=1).astype(f)
    arrays["iotas"] = np.concatenate([np.broadcast_to(np.arange(E1), (P, E1)), np.arange(P)[:, None]], axis=1).astype(f)
    later = np.where(j > i, f(-1e30), f(0))
    arrays["mask"] = np.concatenate([later, np.zeros((P, P), f), later], axis=1)
    first = 2.0 ** (-2.0 ** (-(np.log2(NS * NG) - 3.0)))
    al_q, al_k = np.zeros((NG, HP, NS, T), f), np.zeros((NG, HP, T), f)
    for g in range(NG):
        for s in range(NS):
            slope = f(first ** (s * NG + g + 1))
            al_q[g, HD, s] = slope
            al_q[g, HD + 1, s] = -slope * np.arange(T)
        al_k[g, HD] = np.arange(T)
        al_k[g, HD + 1] = 1
    arrays["al_q"], arrays["al_k"] = al_q.reshape(P, NS, T), al_k.reshape(P, T)

    nc = bacc.Bacc("TRN2", target_bir_lowering=False, num_devices=1)
    arrays = {f"in_{k}": np.ascontiguousarray(v) for k, v in arrays.items()}
    aps = {k[3:]: nc.dram_tensor(k, v.shape, mb.dt.float32, kind="ExternalInput").ap() for k, v in arrays.items()}
    out = nc.dram_tensor("out_0", (B * T, D), mb.dt.float32, kind="ExternalOutput").ap()
    build(nc, aps, out)
    r = run_bass_kernel_spmd(nc, [arrays], core_ids=[0])
    return r.results[0]["out_0"].reshape(x.shape)
```

```python
from contextlib import ExitStack

import concourse.bass as bass
from concourse import mybir

ALU = mybir.AluOpType
ACT = mybir.ActivationFunctionType
AX_X = mybir.AxisListType.X
F32 = mybir.dt.float32
BF16 = mybir.dt.bfloat16
F16 = mybir.dt.float16
I32 = mybir.dt.int32
U32 = mybir.dt.uint32

LAYERS = 8
P = 128
B, T, D = 4, 256, 256
TILES = B * T // P
HALVES = T // P
DC = D // P
E0 = 8
MH, MP, MN = 8, 64, 64
ME = MH * MP
MC = ME // P
MPROJ = 2 * ME + 2 * MN + MH
TAPS = 4
NG, NS, HD = 4, 4, 16
PARTS = 3
SLOTS_Q, SLOTS_K = (0, 0, 0, 1, 1, 2), (0, 1, 2, 0, 1, 0)
QROWS = len(SLOTS_Q) * HD
AROWS = 2 * PARTS
HEADS = NS * NG
VW = HD + 1
E1, TOPK, FI = 32, 4, 96
NBLK = B * T * TOPK // P + E1
SLOTS = NBLK * P
BITS = (E1 - 1).bit_length()
WORD = 6
LN_EPS, RMS_EPS = 1e-5, 1e-6
CHUNKS = MC + 2
RWKV, MOE0, MAMBA, MOE0B, ATTA, MOE1, ATTB, MOE1B = range(8)
BIASED = {RWKV: 0, ATTA: 1, ATTB: 2}


def build(nc, a, out):
    with ExitStack() as ctx:
        def sb(name, shape, dt=F32):
            return ctx.enter_context(nc.sbuf_tensor(name, shape, dt))[:]

        def sem(name):
            return ctx.enter_context(nc.semaphore(name))

        X = sb("X", [P, TILES, D])
        xn = sb("xn", [P, TILES, D])
        xT = sb("xT", [P, DC, B, T + 1])
        cols = sb("cols", [P, 8, DC])
        rows = sb("rows", [P, 3 * MH + 3 * D])
        f0_wg = sb("f0_wg", [P, DC, E0])
        f0_b = sb("f0_b", [E0, D])
        mb_conv = sb("mb_conv", [P, CHUNKS, TAPS + 1])
        mb_norm = sb("mb_norm", [P, MC])
        at_q = sb("at_q", [P, 2, DC, HEADS * HD])
        at_k = sb("at_k", [P, 2, DC, NG * HD])
        at_v = sb("at_v", [P, 2, DC, NG * HD])
        at_o = sb("at_o", [P, 2, DC, D])
        rt_w = sb("rt_w", [P, DC, E1])
        mats = sb("mats", [P, 5, P])
        iotas = sb("iotas", [P, P + TILES])
        mask_b = sb("mask_b", [P, P], BF16)
        ident_b, tri_lt_b, ones_b = (sb(name, [P, P], BF16) for name in ("ident_b", "tri_lt_b", "ones_b"))
        neghalf = sb("neghalf", [P, TILES])
        ident, tri_gt, tri_le, tri_lt, ones = (mats[:, i, :] for i in range(5))
        iota_row, iota_col = iotas[:, 0:E1], iotas[:, P:P + 1]
        tok_id = iotas[:, P:P + TILES]
        wk_c, wv_c, wr_c, tmk, tmv, tmr, u_c, w_c = (cols[:, i, :] for i in range(8))
        dt_bias, a_log, d_row = (rows[:, i * MH:(i + 1) * MH] for i in range(3))

        def bo_row(layer):
            i = 3 * MH + BIASED[layer] * D
            return rows[:, i:i + D]

        st6 = sb("st6", [P, 8, 6])
        mv = sb("mv", [P, 8, 2])
        ve = sb("ve", [P, 8])
        rstd = sb("rstd", [P, 8])

        GUW = DC * E1 * 2 * FI
        arena = sb("arena", [P, GUW + E1 * D])
        gu_w = arena[:, 0:GUW].rearrange("p (c n) -> p c n", c=DC)
        dn_w = arena[0:FI, GUW:GUW + E1 * D]

        class Carver:
            def __init__(self, tensor, size):
                self.tensor, self.at, self.size = tensor, 0, size

            def take(self, *dims, parts=P):
                n = 1
                for d in dims:
                    n *= d
                ap = self.tensor[0:parts, self.at:self.at + n]
                self.at += n
                assert self.at <= self.size, (self.at, self.size)
                if len(dims) == 2:
                    return ap.rearrange("p (a b) -> p a b", a=dims[0])
                if len(dims) == 3:
                    return ap.rearrange("p (a b c) -> p a b c", a=dims[0], b=dims[1])
                return ap

        EARLY = 4 * DC * D + DC * E0 * D + DC * MPROJ + MC * D
        early = sb("early", [P, EARLY])
        ew = Carver(early, EARLY)
        rw_w = ew.take(4 * DC, D).rearrange("p (i c) n -> p i c n", i=4)
        f0_w = ew.take(DC, E0 * D)
        mb_in = ew.take(DC, MPROJ)
        mb_out = ew.take(MC, D)
        ea = Carver(early, EARLY)

        rw = Carver(arena, GUW + E1 * D)
        mix = [rw.take(DC, B, T) for _ in range(3)]
        rw_diff = rw.take(2, DC, T)
        rw_t, rw_d, rw_e1, rw_e2, rw_ev, rw_a, rw_b, rw_rb, rw_q, rw_z = (rw.take(DC, T) for _ in range(10))

        mb = Carver(arena, GUW + E1 * D)
        hs = mb.take(MC, B, T)
        bc = mb.take(2, B, T, parts=MN)
        sg = mb.take(TILES, ME)
        hcv = mb.take(2, CHUNKS, T)
        htok = mb.take(2, ME)
        btok = mb.take(MN)
        m1 = mb.take(2, MH, P)
        Lx = mb.take(MH, P)
        mt = mb.take(MH, P)
        gm = mb.take(P)
        hdec = mb.take(ME)
        dh = mb.take(ME)
        mst = mb.take(ME, parts=MN)
        a_row = sb("a_row", [P, MH])
        epre = sb("epre", [P, MH])
        esuf = sb("esuf", [P, MH])
        dsc = sb("dsc", [P, MH])
        mss = sb("mss", [P, TILES])
        mvar = sb("mvar", [P, TILES])
        mrs = sb("mrs", [P, TILES])
        negw = sb("negw", [P, DC])
        ubk = sb("ubk", [P, DC])

        lg0 = sb("lg0", [P, TILES, E0])
        mx0 = sb("mx0", [P, TILES, 8])
        ix0 = sb("ix0", [P, TILES, 8], U32)
        ex0 = sb("ex0", [P, TILES, E0])
        nmx0, sum0, gate0, idx0 = (sb(name, [P, TILES]) for name in ("nmx0", "sum0", "gate0", "idx0"))
        cmb = sb("cmb", [P, TILES, E0])
        cmbT = sb("cmbT", [E0, TILES, P])
        acc = sb("acc", [P, 2, D])

        LATE = 6700
        late = sb("late", [P, LATE])
        mb_late = Carver(late, LATE)
        y1 = mb_late.take(ME)
        yf = mb_late.take(ME)
        ysq = mb_late.take(ME)
        yfT = mb_late.take(MC, P)
        dtr, sp_neg, sp_e, sp_u, sp_d, sp_l, dt, a_d, sp_mask, sp_q = (mb_late.take(TILES * MH) for _ in range(10))
        mask_f = late[:, 0:P]
        at = Carver(late, LATE)
        QK = DC * T + T
        qkf = at.take(QK)
        vf = at.take(HALVES * NG * HD)
        q_rest = at.take(QK)
        v_rest = at.take(HALVES * NG * HD)
        qk_part = at.take(PARTS * QK // 2).bitcast(BF16).rearrange("p (l n) -> p l n", l=PARTS)
        pexp = at.take(3, 3 * P)
        p_hi, p_lo = (at.take(3 * 3 * P // 2).bitcast(F16).rearrange("p (i n) -> p i n", i=3) for _ in range(2))
        rsum = at.take(NG * NS)
        ctx_t = at.take(2, D)
        ctxT = at.take(DC, P)
        nmax = sb("nmax", [P, 4, 2])
        vt = sb("vt", [P, 3, PARTS, HALVES * NG, VW], BF16)

        NXB, NYG = 4, 8
        mo = Carver(late, LATE)
        xb = mo.take(NXB, D)
        xbT = mo.take(2, DC, P)
        sgt = mo.take(2, FI)
        hh = mo.take(2, FI)
        hT = mo.take(2, P, parts=FI)
        yb = mo.take(NXB, D)
        yg = mo.take(NYG, D)
        lg1 = sb("lg1", [P, TILES, E1])
        mx1 = sb("mx1", [P, TILES, 8])
        ix1 = sb("ix1", [P, TILES, 8], U32)
        ixf = sb("ixf", [P, TILES, TOPK])
        oh = mo.take(TILES, TOPK, E1)
        pos = mo.take(TILES, E1)
        nmx1 = sb("nmx1", [P, TILES])
        wts = sb("wts", [P, TILES, TOPK])
        wsum = sb("wsum", [P, TILES])
        sel = sb("sel", [P, TILES, E1], BF16)
        rnk = sb("rnk", [P, TILES, E1])
        cnt = sb("cnt", [P, E1])
        cnt_i = sb("cnt_i", [P, 2, E1], I32)
        nblk = sb("nblk", [P, E1])
        cum = sb("cum", [P, E1])
        start = sb("start", [P, E1])
        blk_e = sb("blk_e", [P, 1])
        blk_c = sb("blk_c", [P, E1])
        blk_i = sb("blk_i", [1, P], I32)
        shifted = sb("shifted", [1, WORD, NBLK // 4], I32)
        words = sb("words", [1, NBLK // 4], I32)
        slot_f = sb("slot_f", [P, TILES, TOPK])
        slot = sb("slot", [P, TILES * TOPK], U32)
        row_blk = sb("row_blk", [P, 2, TILES * TOPK], I32)
        row_f = sb("row_f", [P, 2, TILES * TOPK])
        iota_h = sb("iota_h", [P, P], F16)
        PAIRS = 4
        Qs = ea.take(2 * HEADS * T // 2).bitcast(BF16).rearrange("p (b h t) -> p b h t", b=2, h=HEADS)
        Ks = ea.take(2 * NG * T // 2).bitcast(BF16).rearrange("p (b h t) -> p b h t", b=2, h=NG)
        at_row = ea.take(PAIRS * P // 2).bitcast(F16).rearrange("p (i n) -> p i n", i=PAIRS)
        at_blk = ea.take(PAIRS * NBLK // 2).bitcast(F16).rearrange("p (i n) -> p i n", i=PAIRS)
        tok = sb("tok", [P, NBLK], U32)

        bank = [ctx.enter_context(nc.psum_tensor(f"bank{i}", [P, 512], F32)) for i in range(8)]

        xn_d = nc.dram_tensor("normed_x", [B * T, D], F32, kind="Internal").ap()
        q_d = nc.dram_tensor("q_parts", [PARTS, HEADS, HD, T], BF16, kind="Internal").ap()
        k_d = nc.dram_tensor("k_parts", [PARTS, NG, HD, T], BF16, kind="Internal").ap()
        yg_d = nc.dram_tensor("grouped_y", [SLOTS, D], F32, kind="Internal").ap()

        x_in = [sem(f"x_in{t}") for t in range(TILES)]
        w_in = {k: sem(f"w_{k}") for k in ("small", "mats", "rwkv", "moe0", "mamba", "att", "alibi", "moe1")}
        xn_out = sem("xn_out")
        out_done = sem("out_done")
        k_out, q_out = sem("k_out"), sem("q_out")
        qk_in = sem("qk_in")
        dve_step, act_step, pool_step = sem("dve_step"), sem("act_step"), sem("pool_step")
        prep = sem("prep")
        ln_var, ln_rstd, ln_done = sem("ln_var"), sem("ln_rstd"), sem("ln_done")
        xT_ready = sem("xT_ready")
        xb_ready = sem("xb_ready")
        x_ready = sem("x_ready")
        full = [sem(f"bank_full{i}") for i in range(8)]

        fills = {}
        used = [0] * 8
        free_at = [None] * 8

        def claim(pe, b, key, freed_by):
            if free_at[b] is not None:
                pe.wait_ge(*free_at[b])
            free_at[b] = freed_by
            used[b] += 1
            fills[key] = b, used[b]
            return bank[b]

        def filled(key):
            b, count = fills[key]
            return full[b], count

        def filled_bank(key):
            return bank[fills[key][0]]

        class Steps:
            def __init__(self, eng, s):
                self.eng, self.s, self.n = eng, s, 0

            def mark(self, ins):
                ins.then_inc(self.s, 1)
                self.n += 1
                return self.n

            def after(self, n):
                self.eng.wait_ge(self.s, n)

            def link(self, ins):
                self.after(self.mark(ins))

        MIXES = 3 * DC
        PREPS = 9
        SMALLS = 8
        TPB = (0, 1)

        def xcols(t):
            return xT[:, :, t // HALVES, 1 + (t % HALVES) * P:1 + (t % HALVES + 1) * P]

        rs = {k: sem(f"rw_{k}") for k in ("diff", "mix", "silu", "td", "exp", "ab", "q", "z", "col", "fr")}
        m0 = {k: sem(f"m0_{k}") for k in ("lg", "nmx", "sum", "cmb", "cmbT", "ex")}
        ms = {k: sem(f"mb_{k}") for k in ("dtr", "dtneg", "spe", "spu", "spl", "ad", "tap", "cv", "cvs", "sg", "htok", "btok",
                                          "gm", "esuf", "epre", "dsc", "m1", "L", "mt", "hdec", "dh", "st", "y", "yf",
                                          "yfT", "rs", "y1")}
        as_ = {k: sem(f"at_{k}") for k in ("k", "v", "q", "kparts", "qparts", "vparts", "nmax", "exp", "hi", "lo", "ctx", "ctxT")}
        mo_s = {k: sem(f"m1_{k}") for k in ("lg", "nmx", "exw", "sel", "rnk", "cnt", "blk", "blki", "slot", 
                                            "xbT", "sg", "h", "hT", "yb", "comb", "rowf", "pair", "paired", "tok", "turned", "gu", "hturned", "down", "ws")}

        xb_in = [sem(f"xb_in{k}") for k in range(NXB)]
        y_out = [sem(f"y_out{k}") for k in range(NXB)]
        y_in = [sem(f"y_in{k}") for k in range(NYG)]

        NEXT = {8: ("turn_x", 0), 9: ("turn_x", 1), 10: ("keys", 0), 11: ("queries", 0), 12: ("queries", 1), 13: ("values", 0)}
        LAST = {3: ("turn_ctx", 0), 4: ("project", 0), 5: ("turn_ctx", 1), 6: ("project", 1)}

        def pair(b):
            return range(b * HALVES, (b + 1) * HALVES)

        def attention_next(layer):
            return layer + 1 in (ATTA, ATTB) and layer + 1 < LAYERS

        AHEAD_SEQ = 2
        STATS, NORM = 1, 6

        def between(b, i, work):
            if i in NEXT and b + AHEAD_SEQ < B:
                work(NEXT[i][0], b + AHEAD_SEQ, NEXT[i][1])
            if i in LAST and b >= 1:
                work(LAST[i][0], b - 1, LAST[i][1])

        TURN_X, GATE_UP, TURN_H, DOWN, FETCH = range(5)
        AHEAD = ((TURN_X, 3), (GATE_UP, 2), (TURN_H, 1), (DOWN, 0))
        PEEL = 4
        LOOPS = (NBLK - PEEL - 3 - NXB) // 4

        def over_blocks(eng, step):
            step(FETCH, 0, 0, True)
            for j in range(-3, PEEL):
                for stage, ahead in AHEAD:
                    if j + ahead >= 0:
                        step(stage, 0, j + ahead, j + ahead < 2)
            with eng.Fori(0, LOOPS) as m:
                step(FETCH, m, PEEL, False)
                for c in range(PEEL, PEEL + 4):
                    for stage, ahead in AHEAD:
                        step(stage, m, c + ahead, False)
            for j in range(PEEL + 4 * LOOPS, NBLK):
                if j % 4 == 0:
                    step(FETCH, 0, j, False)
                for stage, ahead in AHEAD:
                    if j + ahead < NBLK:
                        step(stage, 0, j + ahead, False)

        block = ctx.enter_context(nc.Block())

        @block.tensor
        def _(pe):
            mm = nc.tensor.matmul

            def ln_T(layer, t):
                n = layer * TILES + t
                pe.wait_ge(ln_done, n + 1)
                p = claim(pe, TPB[t % 2], ("xT", n), (xT_ready, n + 1))
                for c in range(DC):
                    ins = nc.tensor.transpose(p[:, c * P:(c + 1) * P], xn[:, t, c * P:(c + 1) * P], ident)
                ins.then_inc(full[TPB[t % 2]], 1)

            def rwkv():
                layer = RWKV
                pe.wait_ge(w_in["mats"], 16)
                for t in range(TILES):
                    ln_T(layer, t)
                pe.wait_ge(w_in["rwkv"], 16)

                def kvr(b):
                    pe.wait_ge(rs["mix"], MIXES * (b + 1))
                    for i, freed in enumerate(((rs["td"], b + 1), (rs["ab"], b + 1), (rs["z"], b + 1))):
                        bk = 2 + 3 * (b % 2) + i
                        if i == 2:
                            pe.wait_ge(rs["silu"], b + 1)
                        p = claim(pe, bk, ("kvr", b, i), freed)
                        for e in range(DC):
                            for c in range(DC):
                                ins = mm(p[:, e * T:(e + 1) * T], rw_w[:, i, c, e * P:(e + 1) * P],
                                         mix[i][:, c, b, :], start=(c == 0), stop=(c == DC - 1))
                        ins.then_inc(full[bk], 1)

                def project(b):
                    pe.wait_ge(rs["z"], b + 1)
                    for h in range(HALVES):
                        t = b * HALVES + h
                        p = claim(pe, TPB[t % 2], ("rwo", t), (x_ready, t + 1))
                        for c in range(DC):
                            ins = mm(p[:, 0:D], rw_z[:, c, h * P:(h + 1) * P], rw_w[:, 3, c, :],
                                     start=(c == 0), stop=(c == DC - 1))
                        ins.then_inc(full[TPB[t % 2]], 1)

                kvr(0)
                for b in range(B):
                    if b + 1 < B:
                        kvr(b + 1)
                    project(b)

            def moe0(layer):
                base = (0 if layer == MOE0 else 1) * TILES
                if layer == MOE0:
                    pe.wait_ge(w_in["moe0"], 32)

                def logits(t):
                    pe.wait_ge(xT_ready, layer * TILES + t + 1)
                    for c in range(DC):
                        ins = mm(bank[6][:, t * E0:(t + 1) * E0], xcols(t)[:, c, :], f0_wg[:, c, :],
                                 start=(c == 0), stop=(c == DC - 1))
                    if t == TILES - 1:
                        ins.then_inc(full[6], 1)

                def experts(t):
                    for pair in range(E0 // 2):
                        p = claim(pe, 2 + pair, ("ex0", base + t, pair), (m0["ex"], E0 * (base + t) + 2 * pair + 2))
                        for c in range(DC):
                            ins = mm(p[:, :], xcols(t)[:, c, :], f0_w[:, c, pair * 512:(pair + 1) * 512],
                                     start=(c == 0), stop=(c == DC - 1))
                        ins.then_inc(full[2 + pair], 1)

                r = base // TILES
                claim(pe, 6, ("lg0", r), (m0["lg"], r + 1))
                for t in range(TILES):
                    ln_T(layer, t)
                    if t >= 1:
                        logits(t - 1)
                logits(TILES - 1)
                experts(0)
                pe.wait_ge(m0["cmb"], r + 1)
                for k in range(2):
                    p = claim(pe, 6 + k, ("cmbT", r, k), (m0["cmbT"], 2 * r + k + 1))
                    for i in range(TILES // 2):
                        ins = nc.tensor.transpose(p[0:E0, i * P:(i + 1) * P], cmb[:, k * TILES // 2 + i, :], ident)
                    ins.then_inc(full[6 + k], 1)
                for t in range(TILES):
                    if t >= 1:
                        experts(t)
                    pe.wait_ge(m0["cmbT"], 2 * r + t // (TILES // 2) + 1)
                    bk = 6 + t % 2
                    p = claim(pe, bk, ("bias0", base + t), (x_ready, layer * TILES + t + 1))
                    mm(p[:, 0:D], cmbT[:, t, :], f0_b[:, :], start=True, stop=True).then_inc(full[bk], 1)
                    if t >= TILES - AHEAD_SEQ and attention_next(layer):
                        attention(layer + 1, start=t - (TILES - AHEAD_SEQ))

            def mamba():
                layer = MAMBA
                pe.wait_ge(w_in["mamba"], 32)
                for t in range(TILES):
                    ln_T(layer, t)
                    if t >= 1:
                        dt_proj(layer, t - 1)
                dt_proj(layer, TILES - 1)
                for b in range(B):
                    xb_ = xT[:, :, b, 1:T + 1]
                    for i in range(3):
                        bk = 2 + 3 * (b % 2) + i
                        p = claim(pe, bk, ("conv", b, i), (ms["tap"], 3 * CHUNKS * b + 2 * CHUNKS + 2 * i + 2))
                        for j in range(2):
                            lo = ME + (2 * i + j) * P if i < 2 else 2 * ME + j * MN
                            m = P if i < 2 else MN
                            for c in range(DC):
                                ins = mm(p[0:m, j * T:(j + 1) * T], mb_in[:, c, lo:lo + m], xb_[:, c, :],
                                         start=(c == 0), stop=(c == DC - 1))
                        ins.then_inc(full[bk], 1)
                    for h in range(HALVES):
                        t = b * HALVES + h
                        p = claim(pe, TPB[h], ("gate", t), (ms["sg"], t + 1))
                        for c in range(DC):
                            ins = mm(p[:, :], xcols(t)[:, c, :], mb_in[:, c, 0:ME], start=(c == 0), stop=(c == DC - 1))
                        ins.then_inc(full[TPB[h]], 1)

                def head_work(t):
                    b, h = t // HALVES, t % HALVES
                    lo = h * P
                    pe.wait_ge(ms["cvs"], 2 * (b + 1))
                    p = claim(pe, TPB[0], ("htok", t), (ms["htok"], t + 1))
                    for c in range(MC):
                        ins = nc.tensor.transpose(p[:, c * P:(c + 1) * P], hs[:, c, b, lo:lo + P], ident)
                    ins.then_inc(full[TPB[0]], 1)
                    p = claim(pe, 2, ("gm", t), (ms["gm"], t + 1))
                    ins = mm(p[:, 0:P], bc[:, 0, b, lo:lo + P], bc[:, 1, b, lo:lo + P], start=True, stop=True)
                    ins.then_inc(full[2], 1)
                    pe.wait_ge(ms["ad"], 1)
                    if h == 0:
                        p = claim(pe, 7, ("btok", b), (ms["btok"], b + 1))
                        nc.tensor.transpose(p[:, 0:MN], bc[:, 0, b, lo:lo + P], ident[0:MN, 0:MN]).then_inc(full[7], 1)
                        p = claim(pe, 6, ("suf", b), (ms["esuf"], b + 1))
                        mm(p[:, 0:MH], tri_gt, a_d[:, t * MH:(t + 1) * MH], start=True, stop=True).then_inc(full[6], 1)
                    else:
                        p = claim(pe, 6, ("pre", b), (ms["epre"], b + 1))
                        mm(p[:, 0:MH], tri_le, a_d[:, t * MH:(t + 1) * MH], start=True, stop=True).then_inc(full[6], 1)
                    pe.wait_ge(ms["m1"], MH * (t + 1))
                    for q in range(2):
                        p = claim(pe, 3 + q, ("seg", t, q), (ms["L"], 2 * t + q + 1))
                        for i in range(4):
                            ins = mm(p[:, i * P:(i + 1) * P], m1[:, t % 2, 4 * q + i, :], tri_le, start=True, stop=True)
                        ins.then_inc(full[3 + q], 1)

                def outputs(t):
                    b, h = t // HALVES, t % HALVES
                    lo = h * P
                    if h == 0:
                        pe.wait_ge(ms["hdec"], b + 1)
                        pe.wait_ge(ms["btok"], b + 1)
                        p = claim(pe, 6, ("state", b), (ms["st"], b + 1))
                        mm(p[0:MN, :], btok, hdec, start=True, stop=True).then_inc(full[6], 1)
                    else:
                        pe.wait_ge(ms["st"], b + 1)
                        p = claim(pe, 6, ("yoff", b), (ms["y1"], b + 1))
                        mm(p[:, :], bc[:, 1, b, lo:lo + P], mst, start=True, stop=True).then_inc(full[6], 1)
                    p = claim(pe, 5, ("ydiag", t), (ms["y"], t + 1))
                    for i in range(MH):
                        pe.wait_ge(ms["mt"], MH * t + i + 1)
                        ins = mm(p[:, i * MP:(i + 1) * MP], mt[:, i, :], htok[:, t % 2, i * MP:(i + 1) * MP],
                                 start=True, stop=True)
                    ins.then_inc(full[5], 1)

                def turn_y(t):
                    pe.wait_ge(ms["yf"], t + 1)
                    p = claim(pe, TPB[1], ("yfT", t), (ms["yfT"], t + 1))
                    for c in range(MC):
                        ins = nc.tensor.transpose(p[:, c * P:(c + 1) * P], yf[:, c * P:(c + 1) * P], ident)
                    ins.then_inc(full[TPB[1]], 1)

                def project(t):
                    pe.wait_ge(ms["yfT"], t + 1)
                    p = claim(pe, 7, ("mbo", t), (x_ready, layer * TILES + t + 1))
                    for c in range(MC):
                        ins = mm(p[:, 0:D], yfT[:, c, :], mb_out[:, c, :], start=(c == 0), stop=(c == MC - 1))
                    ins.then_inc(full[7], 1)

                head_work(0)
                for t in range(TILES):
                    if t + 1 < TILES:
                        head_work(t + 1)
                    outputs(t)
                    if t >= 1:
                        project(t - 1)
                    turn_y(t)
                project(TILES - 1)

            def dt_proj(layer, t):
                pe.wait_ge(xT_ready, layer * TILES + t + 1)
                if t == 0:
                    claim(pe, 7, ("dt",), (ms["dtr"], 1))
                for c in range(DC):
                    ins = mm(bank[7][:, t * MH:(t + 1) * MH], xcols(t)[:, c, :], mb_in[:, c, MPROJ - MH:MPROJ],
                             start=(c == 0), stop=(c == DC - 1))
                if t == TILES - 1:
                    ins.then_inc(full[7], 1)

            def attention(layer, start=None):
                r = (layer - ATTA) // 2
                if r == 0 and start == 0:
                    pe.wait_ge(w_in["att"], 64)
                    pe.wait_ge(prep, PREPS)
                SCORE, TURN = (2, 3, 4), (5, 6)
                K = QROWS + (AROWS if layer == ATTB else 0)

                def work(name, b, h):
                    t = b * HALVES + h
                    n, m = layer * TILES + t, r * TILES + t
                    if name == "turn_x":
                        pe.wait_ge(ln_done, n + 1)
                        p = claim(pe, 0, ("xT", n), (xT_ready, n + 1))
                        for c in range(DC):
                            ins = nc.tensor.transpose(p[:, c * P:(c + 1) * P], xn[:, t, c * P:(c + 1) * P], ident)
                    seq = r * B + b
                    if name == "keys":
                        pe.wait_ge(xT_ready, layer * TILES + (b + 1) * HALVES)
                        p = claim(pe, 0, ("k", seq), (as_["k"], seq + 1))
                        for c in range(DC):
                            ins = mm(p[0:NG * HD, 0:T], at_k[:, r, c, :], xT[:, c, b, 1:T + 1],
                                     start=(c == 0), stop=(c == DC - 1))
                    if name == "values":
                        p = claim(pe, 0, ("v", seq), (as_["v"], seq + 1))
                        for k in range(HALVES):
                            lo = k * NG * HD
                            for c in range(DC):
                                ins = mm(p[:, lo:lo + NG * HD], xcols(b * HALVES + k)[:, c, :], at_v[:, r, c, :],
                                         start=(c == 0), stop=(c == DC - 1))
                    if name == "queries":
                        p = claim(pe, 0, ("q", seq, h), (as_["q"], DC * seq + h + 1))
                        for c in range(DC):
                            ins = mm(p[:, 0:T], at_q[:, r, c, h * P:(h + 1) * P], xT[:, c, b, 1:T + 1],
                                     start=(c == 0), stop=(c == DC - 1))
                    if name == "turn_ctx":
                        pe.wait_ge(as_["ctx"], m + 1)
                        p = claim(pe, 0, ("ctxT", m), (as_["ctxT"], m + 1))
                        for c in range(DC):
                            ins = nc.tensor.transpose(p[:, c * P:(c + 1) * P], ctx_t[:, t % 2, c * P:(c + 1) * P], ident)
                    if name == "project":
                        pe.wait_ge(as_["ctxT"], m + 1)
                        p = claim(pe, 0, ("ato", m), (x_ready, n + 1))
                        for c in range(DC):
                            ins = mm(p[:, 0:D], ctxT[:, c, :], at_o[:, r, c, :], start=(c == 0), stop=(c == DC - 1))
                    ins.then_inc(full[0], 1)

                def group(i):
                    return i // NS if layer == ATTA else i % NG

                def scores(j):
                    b, i, n = j // HEADS, j % HEADS, r * B * HEADS + j
                    seq = r * B + b
                    if j == 0:
                        pe.wait_ge(w_in["alibi"], 64)
                    if i == 0:
                        pe.wait_ge(qk_in, 16 * 2 * len(SLOTS_Q) * (seq + 1))
                    bk = SCORE[n % 3]
                    p = claim(pe, bk, ("score", n), (as_["exp"], n + 1))
                    q_, k_ = Qs[0:K, seq % 2, i, :], Ks[0:K, seq % 2, group(i), :]
                    mm(p[:, 0:P], q_[:, 0:P], k_[:, 0:P], start=True, stop=False)
                    mm(p[:, 0:P], ident_b[:, :], mask_b[:, :], start=False, stop=True)
                    mm(p[:, P:3 * P], q_[:, P:T], k_, start=True, stop=False)
                    mm(p[:, 2 * P:3 * P], ident_b[:, :], mask_b[:, :], start=False, stop=True).then_inc(full[bk], 1)

                def turn(j):
                    n = r * B * HEADS + j
                    pe.wait_ge(as_["exp"], n + 1)
                    bk = TURN[n % 2]
                    p = claim(pe, bk, ("turn", n), (as_["lo"], n + 1))
                    for c in range(3):
                        ins = nc.tensor.transpose(p[:, c * P:(c + 1) * P], pexp[:, n % 3, c * P:(c + 1) * P], ident)
                    ins.then_inc(full[bk], 1)

                def values(j):
                    b, i, n = j // HEADS, j % HEADS, r * B * HEADS + j
                    g, seq = group(i), r * B + b
                    pe.wait_ge(as_["lo"], n + 1)
                    if i == 0:
                        pe.wait_ge(as_["vparts"], seq + 1)
                        m = r * TILES + b * HALVES
                        claim(pe, 7, ("av", m), (as_["ctx"], m + 1))
                        claim(pe, 1, ("av", m + 1), (as_["ctx"], m + 2))
                    lo = i * VW
                    products = [(p_hi, l) for l in range(PARTS)] + [(p_lo, l) for l in range(PARTS - 1)]
                    for bk, halves in ((7, ((0, 0),)), (1, ((1, 0), (2, 1)))):
                        todo = [(w, l, c, h) for c, h in halves for w, l in products]
                        for k, (w, l, c, h) in enumerate(todo):
                            ins = mm(bank[bk][:, lo:lo + VW], w[:, n % 3, c * P:(c + 1) * P], vt[:, seq % 3, l, h * NG + g, :],
                                     start=(k == 0), stop=(k == len(todo) - 1))
                        if i == HEADS - 1:
                            ins.then_inc(full[bk], 1)

                if start is not None:
                    for i in sorted(NEXT):
                        work(NEXT[i][0], start, NEXT[i][1])
                    return
                scores(0)
                scores(1)
                for j in range(B * HEADS):
                    if j + 2 < B * HEADS:
                        scores(j + 2)
                    turn(j)
                    if j >= 2:
                        values(j - 2)
                    between(j // HEADS, j % HEADS, work)
                values(B * HEADS - 2)
                values(B * HEADS - 1)
                for i in sorted(LAST):
                    work(LAST[i][0], B - 1, LAST[i][1])

            def moe1(layer):
                r = (layer - MOE1) // 2
                s = mo_s
                if r == 0:
                    pe.wait_ge(w_in["moe1"], 32)

                def logits(t):
                    pe.wait_ge(xT_ready, layer * TILES + t + 1)
                    n = r * TILES + t
                    p = claim(pe, 2 + t % 2, ("lg1", n), (s["lg"], n + 1))
                    for c in range(DC):
                        ins = mm(p[:, 0:E1], xcols(t)[:, c, :], rt_w[:, c, :], start=(c == 0), stop=(c == DC - 1))
                    ins.then_inc(full[2 + t % 2], 1)

                for t in range(TILES):
                    ln_T(layer, t)
                    if t >= 1:
                        logits(t - 1)
                logits(TILES - 1)
                p = claim(pe, 4, ("rnk", r), (s["rnk"], r + 1))
                q = claim(pe, 5, ("cnt", r), (s["cnt"], r + 1))
                pe.wait_ge(s["sel"], r + 1)
                for t in range(TILES):
                    for j in range(t + 1):
                        ins = mm(p[:, t * E1:(t + 1) * E1], tri_lt_b[:, :] if j == t else ones_b[:, :], sel[:, j, :],
                                 start=(j == 0), stop=(j == t))
                ins.then_inc(full[4], 1)
                for t in range(TILES):
                    ins = mm(q[:, 0:E1], ones_b[:, :], sel[:, t, :], start=(t == 0), stop=(t == TILES - 1))
                ins.then_inc(full[5], 1)
                p = claim(pe, 7, ("tok", r), (s["tok"], r + 1))
                for i in range(TILES * TOPK):
                    n = r * TILES * TOPK + i
                    pe.wait_ge(s["pair"], 2 * (n + 1))
                    ins = mm(p[:, 0:NBLK], at_row[:, i % PAIRS, :], at_blk[:, i % PAIRS, :],
                             start=(i == 0), stop=(i == TILES * TOPK - 1))
                    if i < TILES * TOPK - 1:
                        ins.then_inc(s["paired"], 1)
                ins.then_inc(full[7], 1)

                pe.wait_ge(s["blk"], r + 1)
                p = claim(pe, 6, ("blk", r), (s["blki"], 2 * r + 2))
                nc.tensor.transpose(p[0:1, 0:P], blk_e[:, :], ident).then_inc(full[6], 1)
                pe.wait_ge(s["blki"], 2 * r + 2)

                for k in range(8):
                    if free_at[k] is not None:
                        pe.wait_ge(*free_at[k])
                    free_at[k] = ((s["xbT"], s["h"], s["hT"], s["yb"])[k // 2], (r + 1) * NBLK)
                base = r * NBLK
                col_g, col_d = {}, {}

                def step(stage, m, c, first):
                    j, k = 4 * m + c, c % 2
                    if stage == TURN_X:
                        pe.wait_ge(xb_in[c % 4], (m + (c // 4 + 1 + r * NBLK // 4)) * 16)
                        if not first:
                            pe.wait_ge(s["xbT"], j + (base - 1))
                        for i in range(DC):
                            ins = nc.tensor.transpose(bank[k][:, i * P:(i + 1) * P], xb[:, c % 4, i * P:(i + 1) * P], ident)
                        ins.then_inc(s["turned"], 1)
                    if stage == FETCH:
                        word = nc.tensor.value_load(words[0:1, bass.ds(m + c // 4, 1)], min_val=0, max_val=2 ** (BITS * WORD) - 1)
                        for i in range(WORD):
                            e = (word >> BITS * i) & (E1 - 1)
                            if i < 4:
                                col_d[i] = nc.tensor.snap(e * D, min_val=0, max_val=(E1 - 1) * D)
                            if i >= 2 or first:
                                col_g[i] = nc.tensor.snap(e * (2 * FI), min_val=0, max_val=(E1 - 1) * 2 * FI)
                    if stage == GATE_UP:
                        e = col_g[c if first else (c - 2) % 4 + 2]
                        pe.wait_ge(s["xbT"], j + (base + 1))
                        if not first:
                            pe.wait_ge(s["h"], j + (base - 1))
                        for i in range(DC):
                            ins = mm(bank[2 + k][:, 0:2 * FI], xbT[:, k, i, :], gu_w[:, i, bass.ds(e, 2 * FI)],
                                     start=(i == 0), stop=(i == DC - 1))
                        ins.then_inc(s["gu"], 1)
                    if stage == TURN_H:
                        pe.wait_ge(s["h"], j + (base + 1))
                        if not first:
                            pe.wait_ge(s["hT"], j + (base - 1))
                        nc.tensor.transpose(bank[4 + k][0:FI, 0:P], hh[:, k, :], ident).then_inc(s["hturned"], 1)
                    if stage == DOWN:
                        e = col_d[c % 4]
                        pe.wait_ge(s["hT"], j + (base + 1))
                        if not first:
                            pe.wait_ge(s["yb"], j + (base - 1))
                        mm(bank[6 + k][:, 0:D], hT[:, k, :], dn_w[:, bass.ds(e, D)],
                           start=True, stop=True).then_inc(s["down"], 1)

                over_blocks(pe, step)
                if attention_next(layer):
                    for b in range(AHEAD_SEQ):
                        attention(layer + 1, start=b)

            run = {RWKV: rwkv, MAMBA: mamba}
            for layer in range(LAYERS):
                if layer in (MOE0, MOE0B):
                    moe0(layer)
                elif layer in (ATTA, ATTB):
                    attention(layer)
                elif layer in (MOE1, MOE1B):
                    moe1(layer)
                else:
                    run[layer]()

        @block.scalar
        def _(act):
            steps = Steps(act, act_step)

            def xT_copy(layer, t):
                n = layer * TILES + t
                act.wait_ge(*filled(("xT", n)))
                b = t // HALVES
                nc.scalar.activation(xcols(t), filled_bank(("xT", n))[:, 0:D].rearrange("p (c n) -> p c n", c=DC),
                                     ACT.Copy).then_inc(xT_ready, 1)

            def rwkv():
                for t in range(TILES):
                    xT_copy(RWKV, t)
                for b in range(B):
                    act.wait_ge(rs["mix"], MIXES * b + DC)
                    nc.scalar.activation(mix[2][:, :, b, :], mix[2][:, :, b, :], ACT.Silu).then_inc(rs["silu"], 1)
                for b in range(B):
                    act.wait_ge(rs["td"], b + 1)
                    if b >= 1:
                        act.wait_ge(rs["ab"], b)
                    nc.scalar.activation(rw_e2, rw_d, ACT.Exp)
                    for c in range(DC):
                        ins = nc.scalar.activation(rw_e1[:, c, :], rw_t[:, c, :], ACT.Exp, bias=negw[:, c:c + 1], scale=-1.0)
                    ins.then_inc(rs["exp"], 1)

            def moe0(layer):
                base = (0 if layer == MOE0 else 1) * TILES

                r = base // TILES
                for t in range(TILES):
                    xT_copy(layer, t)
                act.wait_ge(*filled(("lg0", r)))
                nc.scalar.activation(lg0[:, :, :], filled_bank(("lg0", r))[:, 0:TILES * E0].rearrange("p (t e) -> p t e", e=E0),
                                     ACT.Copy).then_inc(m0["lg"], 1)
                act.wait_ge(m0["nmx"], r + 1)
                for t in range(TILES):
                    ins = nc.scalar.activation(ex0[:, t, :], lg0[:, t, :], ACT.Exp, bias=nmx0[:, t:t + 1],
                                               accum_out=sum0[:, t:t + 1])
                ins.then_inc(m0["sum"], 1)
                for k in range(2):
                    act.wait_ge(*filled(("cmbT", r, k)))
                    half = slice(k * TILES // 2, (k + 1) * TILES // 2)
                    nc.scalar.activation(cmbT[:, half, :],
                                         filled_bank(("cmbT", r, k))[0:E0, :].rearrange("p (t n) -> p t n", n=P),
                                         ACT.Copy).then_inc(m0["cmbT"], 1)
                if attention_next(layer):
                    for b in range(AHEAD_SEQ):
                        attention(layer + 1, start=b)

            def mamba():
                layer = MAMBA
                nc.scalar.activation(a_row, a_log, ACT.Exp).then_inc(ms["dtneg"], 1)
                for t in range(TILES):
                    xT_copy(layer, t)
                act.wait_ge(ms["spu"], 1)
                nc.scalar.activation(sp_e, sp_neg, ACT.Exp).then_inc(ms["spe"], 1)
                act.wait_ge(ms["spu"], 2)
                nc.scalar.activation(sp_l, sp_u, ACT.Ln).then_inc(ms["spl"], 1)

                def conv(b):
                    for i in range(3):
                        act.wait_ge(*filled(("conv", b, i)))
                        if i == 0 and b >= 2:
                            act.wait_ge(ms["cvs"], 2 * (b - 1))
                        n = P if i < 2 else MN
                        for j in range(2):
                            ch = 2 * i + j
                            nc.scalar.activation(hcv[0:n, b % 2, ch, :], filled_bank(("conv", b, i))[0:n, j * T:(j + 1) * T],
                                                 ACT.Identity, bias=mb_conv[0:n, ch, TAPS:TAPS + 1],
                                                 scale=mb_conv[0:n, ch, TAPS - 1:TAPS]).then_inc(ms["cv"], 1)

                def convolved(b):
                    act.wait_ge(ms["tap"], 3 * CHUNKS * (b + 1))
                    nc.scalar.activation(hs[:, :, b, :], hcv[:, b % 2, 0:MC, :], ACT.Silu).then_inc(ms["cvs"], 1)
                    nc.scalar.activation(bc[:, :, b, :], hcv[0:MN, b % 2, MC:CHUNKS, :], ACT.Silu).then_inc(ms["cvs"], 1)

                def gates(b):
                    for h in range(HALVES):
                        t = b * HALVES + h
                        act.wait_ge(*filled(("gate", t)))
                        nc.scalar.activation(sg[:, t, :], filled_bank(("gate", t))[:, :], ACT.Silu).then_inc(ms["sg"], 1)

                for b in range(B):
                    conv(b)
                    gates(b)
                    if b >= 1:
                        convolved(b - 1)
                convolved(B - 1)

                def head_work(t):
                    b, h = t // HALVES, t % HALVES
                    act.wait_ge(*filled(("htok", t)))
                    if t >= 2:
                        act.wait_ge(*filled(("ydiag", t - 2)))
                        act.wait_ge(ms["dh"], t - 1)
                        act.wait_ge(ms["hdec"], (t - 2) // 2 + 1)
                    nc.scalar.activation(htok[:, t % 2, :], filled_bank(("htok", t))[:, :], ACT.Copy).then_inc(ms["htok"], 1)
                    if h == 0:
                        act.wait_ge(*filled(("btok", b)))
                        if b >= 1:
                            act.wait_ge(*filled(("state", b - 1)))
                        nc.scalar.activation(btok, filled_bank(("btok", b))[:, 0:MN], ACT.Copy).then_inc(ms["btok"], 1)
                        act.wait_ge(*filled(("suf", b)))
                        if b >= 1:
                            act.wait_ge(ms["dsc"], b)
                        nc.scalar.activation(esuf, filled_bank(("suf", b))[:, 0:MH], ACT.Exp).then_inc(ms["esuf"], 1)
                    else:
                        act.wait_ge(*filled(("pre", b)))
                        if b >= 1:
                            act.wait_ge(ms["y1"], b)
                        nc.scalar.activation(epre, filled_bank(("pre", b))[:, 0:MH], ACT.Exp).then_inc(ms["epre"], 1)
                    for q in range(2):
                        act.wait_ge(*filled(("seg", t, q)))
                        if t >= 1:
                            act.wait_ge(ms["mt"], MH * (t - 1) + 4 * q + 4)
                        nc.scalar.activation(Lx[:, 4 * q:4 * q + 4, :],
                                             filled_bank(("seg", t, q))[:, :].rearrange("p (i n) -> p i n", i=4),
                                             ACT.Exp).then_inc(ms["L"], 1)

                head_work(0)
                for t in range(TILES):
                    b, h = t // HALVES, t % HALVES
                    if t + 1 < TILES:
                        head_work(t + 1)
                    if h == 0:
                        act.wait_ge(*filled(("state", b)))
                        if b >= 1:
                            act.wait_ge(*filled(("yoff", b - 1)))
                        nc.scalar.activation(mst, filled_bank(("state", b))[0:MN, :], ACT.Copy).then_inc(ms["st"], 1)
                    act.wait_ge(ms["yf"], t + 1)
                    if t >= 1:
                        steps.after(steps.n)
                    ins = nc.scalar.activation(ysq, yf, ACT.Square, accum_out=mss[:, t:t + 1])
                    steps.mark(ins)

            def attention(layer, start=None):
                r = (layer - ATTA) // 2

                def work(name, b, h):
                    t = b * HALVES + h
                    seq, m = r * B + b, r * TILES + t
                    if name == "turn_x":
                        xT_copy(layer, t)
                    if name == "keys":
                        act.wait_ge(*filled(("k", seq)))
                        if seq >= 1:
                            act.wait_ge(as_["kparts"], seq)
                        nc.scalar.activation(qkf[0:NG * HD, DC * T:QK], filled_bank(("k", seq))[0:NG * HD, 0:T],
                                             ACT.Copy).then_inc(as_["k"], 1)
                    if name == "values":
                        act.wait_ge(*filled(("v", seq)))
                        if seq >= 1:
                            act.wait_ge(as_["vparts"], seq)
                        nc.scalar.activation(vf, filled_bank(("v", seq))[:, 0:HALVES * NG * HD], ACT.Copy).then_inc(as_["v"], 1)
                    if name == "queries":
                        act.wait_ge(*filled(("q", seq, h)))
                        if seq >= 1:
                            act.wait_ge(as_["qparts"], DC * (seq - 1) + h + 1)
                        nc.scalar.activation(qkf[:, h * T:(h + 1) * T], filled_bank(("q", seq, h))[:, 0:T], ACT.Copy,
                                             scale=HD ** -0.5).then_inc(as_["q"], 1)
                    if name == "turn_ctx":
                        act.wait_ge(*filled(("ctxT", m)))
                        if m >= 1:
                            act.wait_ge(*filled(("ato", m - 1)))
                        nc.scalar.activation(ctxT, filled_bank(("ctxT", m))[:, 0:D].rearrange("p (c n) -> p c n", c=DC),
                                             ACT.Copy).then_inc(as_["ctxT"], 1)

                def exps(j):
                    n = r * B * HEADS + j
                    act.wait_ge(as_["nmax"], 2 * (n + 1))
                    if n >= 3:
                        act.wait_ge(*filled(("turn", n - 3)))
                    p = filled_bank(("score", n))
                    nc.scalar.activation(pexp[:, n % 3, 0:P], p[:, 0:P], ACT.Exp, bias=nmax[:, n % 4, 0:1])
                    nc.scalar.activation(pexp[:, n % 3, P:3 * P], p[:, P:3 * P], ACT.Exp,
                                         bias=nmax[:, n % 4, 1:2]).then_inc(as_["exp"], 1)

                def high(j):
                    n = r * B * HEADS + j
                    act.wait_ge(*filled(("turn", n)))
                    if n >= 3:
                        act.wait_ge(as_["lo"], n - 2)
                    nc.scalar.activation(p_hi[:, n % 3, :], filled_bank(("turn", n))[:, 0:3 * P], ACT.Copy).then_inc(as_["hi"], 1)

                if start is not None:
                    for i in sorted(NEXT):
                        work(NEXT[i][0], start, NEXT[i][1])
                    return
                exps(0)
                for j in range(B * HEADS):
                    if j + 1 < B * HEADS:
                        exps(j + 1)
                    high(j)
                    between(j // HEADS, j % HEADS, work)
                for i in sorted(LAST):
                    work(LAST[i][0], B - 1, LAST[i][1])

            def moe1(layer):
                r = (layer - MOE1) // 2
                s = mo_s
                for t in range(TILES + 1):
                    if t < TILES:
                        xT_copy(layer, t)
                    if t == 0:
                        continue
                    t = t - 1
                    n = r * TILES + t
                    act.wait_ge(*filled(("lg1", n)))
                    nc.scalar.activation(lg1[:, t, :], filled_bank(("lg1", n))[:, 0:E1], ACT.Copy).then_inc(s["lg"], 1)
                act.wait_ge(s["nmx"], r + 1)
                for t in range(TILES):
                    nc.scalar.activation(wts[:, t, :], mx1[:, t, 0:TOPK], ACT.Exp, bias=nmx1[:, t:t + 1],
                                         accum_out=wsum[:, t:t + 1]).then_inc(s["exw"], 1)
                base = r * NBLK

                def step(stage, m, c, first):
                    j, k = 4 * m + c, c % 2
                    if stage == TURN_X:
                        act.wait_ge(s["turned"], j + (base + 1))
                        if not first:
                            act.wait_ge(s["gu"], j + (base - 1))
                        nc.scalar.activation(xbT[:, k, :, :], bank[k][:, 0:D].rearrange("p (c n) -> p c n", c=DC),
                                             ACT.Copy).then_inc(s["xbT"], 1)
                    if stage == GATE_UP:
                        act.wait_ge(s["gu"], j + (base + 1))
                        if not first:
                            act.wait_ge(s["h"], j + (base - 1))
                        nc.scalar.activation(sgt[:, k, :], bank[2 + k][:, 0:FI], ACT.Silu).then_inc(s["sg"], 1)
                    if stage == TURN_H:
                        act.wait_ge(s["hturned"], j + (base + 1))
                        if not first:
                            act.wait_ge(s["down"], j + (base - 1))
                        nc.scalar.activation(hT[:, k, :], bank[4 + k][0:FI, 0:P], ACT.Copy).then_inc(s["hT"], 1)

                over_blocks(act, step)
                if attention_next(layer):
                    for b in range(AHEAD_SEQ):
                        attention(layer + 1, start=b)

            act.wait_ge(prep, PREPS)
            for layer in range(LAYERS):
                if layer in (MOE0, MOE0B):
                    moe0(layer)
                elif layer in (ATTA, ATTB):
                    attention(layer)
                elif layer in (MOE1, MOE1B):
                    moe1(layer)
                else:
                    {RWKV: rwkv, MAMBA: mamba}[layer]()

        @block.vector
        def _(dve):
            V = nc.vector
            steps = Steps(dve, dve_step)

            def ln_stats(layer, tiles):
                n = layer * TILES + tiles[0]
                k = slice(n % 8, n % 8 + len(tiles))
                for t in tiles:
                    if layer == 0:
                        dve.wait_ge(x_in[t], 16)
                    else:
                        dve.wait_ge(x_ready, (layer - 1) * TILES + t + 1)
                    steps.mark(V.bn_stats(st6[:, t % 8, :], X[:, t, :]))
                steps.after(steps.n)
                for t in tiles:
                    steps.mark(V.bn_aggr(mv[:, t % 8, :], st6[:, t % 8, :]))
                steps.after(steps.n)
                V.tensor_scalar(ve[:, k], mv[:, k, 1], LN_EPS, None, ALU.add).then_inc(ln_var, len(tiles))

            def ln_norm(layer, tiles):
                dve.wait_ge(ln_rstd, layer * TILES + tiles[-1] + 1)
                for t in tiles:
                    V.tensor_scalar(xn[:, t, :], X[:, t, :], mv[:, t % 8, 0:1], rstd[:, t % 8:t % 8 + 1],
                                    ALU.subtract, ALU.mult).then_inc(ln_done, 1)

            def ln(layer, tiles):
                ln_stats(layer, tiles)
                ln_norm(layer, tiles)

            def rwkv():
                dve.wait_ge(w_in["small"], 16 * SMALLS)
                V.tensor_scalar(negw[:, :], w_c, -1.0, None, ALU.mult).then_inc(rs["col"], 1)
                V.tensor_tensor(ubk[:, :], u_c, wk_c, ALU.add).then_inc(rs["col"], 1)
                for b in range(B):
                    ln(RWKV, pair(b))

                def mixes(b):
                    dve.wait_ge(rs["diff"], b + 1)
                    for i, m in enumerate((tmr, tmk, tmv)):
                        for c in range(DC):
                            V.scalar_tensor_tensor(mix[(2, 0, 1)[i]][:, c, b, :], rw_diff[:, b % 2, c, :], m[:, c:c + 1],
                                                   xT[:, c, b, 0:T], ALU.mult, ALU.add).then_inc(rs["mix"], 1)

                def recurrence(b):
                    dve.wait_ge(*filled(("kvr", b, 0)))
                    k_ = filled_bank(("kvr", b, 0))
                    if b >= 1:
                        dve.wait_ge(rs["exp"], b)
                    dve.wait_ge(rs["col"], 2)
                    for c in range(DC):
                        steps.mark(V.tensor_scalar(rw_t[:, c, :], k_[:, c * T:(c + 1) * T], ubk[:, c:c + 1], w_c[:, c:c + 1],
                                                   ALU.add, ALU.max))
                    steps.after(steps.n)
                    for c in range(DC):
                        ins = V.scalar_tensor_tensor(rw_d[:, c, :], k_[:, c * T:(c + 1) * T], ubk[:, c:c + 1], rw_t[:, c, :],
                                                     ALU.add, ALU.subtract)
                    ins.then_inc(rs["td"], 1)
                    dve.wait_ge(rs["exp"], b + 1)
                    dve.wait_ge(*filled(("kvr", b, 1)))
                    v_ = filled_bank(("kvr", b, 1))
                    for c in range(DC):
                        steps.mark(V.scalar_tensor_tensor(rw_ev[:, c, :], v_[:, c * T:(c + 1) * T], wv_c[:, c:c + 1],
                                                          rw_e2[:, c, :], ALU.add, ALU.mult))
                    for c in range(DC):
                        steps.mark(V.tensor_tensor_scan(rw_b[:, c, :], rw_e1[:, c, :], rw_e2[:, c, :], 0.0, ALU.mult, ALU.add))
                    steps.after(steps.n)
                    rb = steps.mark(V.reciprocal(rw_rb, rw_b))
                    for c in range(DC):
                        ins = V.tensor_tensor_scan(rw_a[:, c, :], rw_e1[:, c, :], rw_ev[:, c, :], 0.0, ALU.mult, ALU.add)
                    ins.then_inc(rs["ab"], 1)
                    dve.wait_ge(rs["ab"], b + 1)
                    steps.after(rb)
                    steps.link(V.tensor_tensor(rw_q, rw_a, rw_rb, ALU.mult))
                    dve.wait_ge(*filled(("kvr", b, 2)))
                    if b >= 1:
                        dve.wait_ge(*filled(("rwo", b * HALVES - 1)))
                    r_ = filled_bank(("kvr", b, 2))
                    for c in range(DC):
                        ins = V.scalar_tensor_tensor(rw_z[:, c, :], r_[:, c * T:(c + 1) * T], wr_c[:, c:c + 1],
                                                     rw_q[:, c, :], ALU.add, ALU.mult)
                    ins.then_inc(rs["z"], 1)

                def residual(b):
                    for h in range(HALVES):
                        t = b * HALVES + h
                        dve.wait_ge(*filled(("rwo", t)))
                        dve.wait_ge(xb_ready, t + 1)
                        V.tensor_tensor(X[:, t, :], filled_bank(("rwo", t))[:, 0:D], X[:, t, :], ALU.add).then_inc(x_ready, 1)

                for b in range(B):
                    mixes(b)
                for b in range(B):
                    recurrence(b)
                    residual(b)

            def moe0(layer):
                base = (0 if layer == MOE0 else 1) * TILES

                r = base // TILES
                ln(layer, range(TILES))
                dve.wait_ge(m0["lg"], r + 1)
                for t in range(TILES):
                    steps.mark(V.max(mx0[:, t, :], lg0[:, t, :]))
                steps.after(steps.n)
                V.tensor_scalar(nmx0[:, :], mx0[:, :, 0], -1.0, None, ALU.mult).then_inc(m0["nmx"], 1)
                for t in range(TILES):
                    steps.mark(V.max_index(ix0[:, t, :], mx0[:, t, :], lg0[:, t, :]))
                steps.after(steps.n)
                steps.link(V.tensor_copy(idx0[:, :], ix0[:, :, 0]))
                steps.mark(V.tensor_tensor(cmb[:, :, :], iota_row[:, 0:E0].unsqueeze(1).to_broadcast([P, TILES, E0]),
                                           idx0[:, :].unsqueeze(2).to_broadcast([P, TILES, E0]), ALU.is_equal))
                dve.wait_ge(m0["sum"], r + 1)
                steps.link(V.reciprocal(gate0[:, :], sum0[:, :]))
                V.tensor_tensor(cmb[:, :, :], cmb[:, :, :], gate0[:, :].unsqueeze(2).to_broadcast([P, TILES, E0]),
                                ALU.mult).then_inc(m0["cmb"], 1)
                dve.wait_ge(m0["cmb"], r + 1)
                for t in range(TILES):
                    n = base + t
                    if n >= 1:
                        dve.wait_ge(x_ready, layer * TILES + t)
                    for e in range(E0):
                        dve.wait_ge(*filled(("ex0", n, e // 2)))
                        src = filled_bank(("ex0", n, e // 2))[:, (e % 2) * D:(e % 2 + 1) * D]
                        if e == 1:
                            ins = V.tensor_scalar(acc[:, 1, :], src, cmb[:, t, e:e + 1], None, ALU.mult)
                        else:
                            if e:
                                dve.wait_ge(m0["ex"], E0 * n + e - 1)
                            ins = V.scalar_tensor_tensor(acc[:, e % 2, :], src, cmb[:, t, e:e + 1],
                                                         acc[:, e % 2, :] if e else X[:, t, :], ALU.mult, ALU.add)
                        ins.then_inc(m0["ex"], 1)
                    dve.wait_ge(*filled(("bias0", n)))
                    dve.wait_ge(m0["ex"], E0 * (n + 1))
                    steps.link(V.tensor_tensor(acc[:, 0, :], filled_bank(("bias0", n))[:, 0:D], acc[:, 0, :], ALU.add))
                    V.tensor_tensor(X[:, t, :], acc[:, 0, :], acc[:, 1, :], ALU.add).then_inc(x_ready, 1)
                    if t == TILES - 2 and attention_next(layer):
                        ln(layer + 1, range(AHEAD_SEQ * HALVES))

            def mamba():
                layer = MAMBA
                ln(layer, range(TILES))
                heads = "p (t h) -> p t h"
                dve.wait_ge(*filled(("dt",)))
                V.tensor_tensor(dtr.rearrange(heads, h=MH), filled_bank(("dt",))[:, 0:TILES * MH].rearrange(heads, h=MH),
                                dt_bias.unsqueeze(1).to_broadcast([P, TILES, MH]), ALU.add).then_inc(ms["dtr"], 1)
                dve.wait_ge(ms["dtr"], 1)
                V.scalar_tensor_tensor(sp_neg, dtr, -1.0, dtr, ALU.mult, ALU.min).then_inc(ms["spu"], 1)
                dve.wait_ge(ms["spe"], 1)
                V.tensor_scalar(sp_u, sp_e, 1.0, None, ALU.add).then_inc(ms["spu"], 1)
                dve.wait_ge(ms["spu"], 2)
                steps.link(V.tensor_scalar(sp_d, sp_u, -1.0, None, ALU.add))
                steps.link(V.tensor_scalar(sp_mask, sp_d, 0.0, None, ALU.is_equal))
                steps.link(V.tensor_tensor(sp_d, sp_d, sp_mask, ALU.add))
                steps.link(V.reciprocal(sp_q, sp_d))
                dve.wait_ge(ms["spl"], 1)
                steps.link(V.tensor_tensor(sp_q, sp_q, sp_l, ALU.mult))
                steps.link(V.tensor_tensor(sp_q, sp_q, sp_mask, ALU.add))
                steps.link(V.tensor_tensor(sp_q, sp_q, sp_e, ALU.mult))
                steps.link(V.scalar_tensor_tensor(dt, dtr, 0.0, sp_q, ALU.max, ALU.add))
                dve.wait_ge(ms["dtneg"], 1)
                V.scalar_tensor_tensor(a_d.rearrange(heads, h=MH), dt.rearrange(heads, h=MH), -1.0,
                                       a_row[:, :].unsqueeze(1).to_broadcast([P, TILES, MH]),
                                       ALU.mult, ALU.mult).then_inc(ms["ad"], 1)
                for b in range(B):
                    for k in range(TAPS - 1):
                        sh = k + 1
                        for ch in range(CHUNKS):
                            n = P if ch < MC else MN
                            if k == 0:
                                dve.wait_ge(ms["cv"], CHUNKS * b + ch // 2 * 2 + 2)
                            else:
                                dve.wait_ge(ms["tap"], 3 * CHUNKS * b + CHUNKS * (k - 1) + ch + 1)
                            src = filled_bank(("conv", b, ch // 2))[0:n, (ch % 2) * T:(ch % 2 + 1) * T - sh]
                            V.scalar_tensor_tensor(hcv[0:n, b % 2, ch, sh:T], src,
                                                   mb_conv[0:n, ch, TAPS - 1 - sh:TAPS - sh], hcv[0:n, b % 2, ch, sh:T],
                                                   ALU.mult, ALU.add).then_inc(ms["tap"], 1)

                def turned(t):
                    dve.wait_ge(*filled(("yfT", t)))
                    if t >= 1:
                        dve.wait_ge(*filled(("mbo", t - 1)))
                    V.tensor_tensor(yfT, filled_bank(("yfT", t))[:, :].rearrange("p (c n) -> p c n", c=MC),
                                    mb_norm[:, :].unsqueeze(2).to_broadcast([P, MC, P]), ALU.mult).then_inc(ms["yfT"], 1)

                def residual(t):
                    dve.wait_ge(ms["rs"], t + 1)
                    dve.wait_ge(*filled(("mbo", t)))
                    V.scalar_tensor_tensor(X[:, t, :], filled_bank(("mbo", t))[:, 0:D], mrs[:, t:t + 1], X[:, t, :],
                                           ALU.mult, ALU.add).then_inc(x_ready, 1)

                wide = "p (h n) -> p h n"
                def mixing(t):
                    b, h = t // HALVES, t % HALVES
                    dve.wait_ge(*filled(("gm", t)))
                    if t >= 1:
                        dve.wait_ge(ms["mt"], MH * t)
                    V.tensor_tensor(gm, filled_bank(("gm", t))[:, 0:P], tri_le, ALU.mult).then_inc(ms["gm"], 1)
                    if h == 0:
                        dve.wait_ge(ms["esuf"], b + 1)
                        if b >= 1:
                            dve.wait_ge(ms["hdec"], b)
                        V.tensor_tensor(dsc[:, :], esuf[:, :], dt[:, t * MH:(t + 1) * MH], ALU.mult).then_inc(ms["dsc"], 1)
                    dve.wait_ge(ms["gm"], t + 1)
                    if t >= 1:
                        dve.wait_ge(*filled(("ydiag", t - 1)))
                    for i in range(MH):
                        if i % 4 == 0:
                            dve.wait_ge(ms["L"], 2 * t + i // 4 + 1)
                        V.scalar_tensor_tensor(mt[:, i, :], Lx[:, i, :], dt[:, t * MH + i:t * MH + i + 1], gm,
                                               ALU.mult, ALU.mult).then_inc(ms["mt"], 1)

                mixing(0)
                for t in range(TILES):
                    b, h = t // HALVES, t % HALVES
                    dve.wait_ge(*filled(("ydiag", t)))
                    dve.wait_ge(ms["dh"], t + 1)
                    if t >= 1:
                        dve.wait_ge(*filled(("yfT", t - 1)))
                        dve.wait_ge(act_step, t)
                    yd = filled_bank(("ydiag", t))
                    V.tensor_tensor(yf, yd[:, :], dh, ALU.add).then_inc(ms["y"], 1)
                    dve.wait_ge(ms["y"], t + 1)
                    if h == 1:
                        dve.wait_ge(*filled(("yoff", b)))
                        dve.wait_ge(ms["epre"], b + 1)
                        V.tensor_tensor(y1.rearrange(wide, h=MH), filled_bank(("yoff", b))[:, :].rearrange(wide, h=MH),
                                        epre[:, :].unsqueeze(2).to_broadcast([P, MH, MP]), ALU.mult).then_inc(ms["y1"], 1)
                        dve.wait_ge(ms["y1"], b + 1)
                        steps.link(V.tensor_tensor(yf, yf, y1, ALU.add))
                    dve.wait_ge(ms["sg"], t + 1)
                    V.tensor_tensor(yf, yf, sg[:, t, :], ALU.mult).then_inc(ms["yf"], 1)
                    if t + 1 < TILES:
                        mixing(t + 1)
                    turned(t)
                    if t >= 1:
                        residual(t - 1)
                residual(TILES - 1)

            def attention(layer, start=None):
                r = (layer - ATTA) // 2

                def work(name, b, h):
                    if name == "project":
                        t = b * HALVES + h
                        m = r * TILES + t
                        dve.wait_ge(*filled(("ato", m)))
                        dve.wait_ge(xb_ready, BIASED[layer] * TILES + t + 1)
                        V.tensor_tensor(X[:, t, :], filled_bank(("ato", m))[:, 0:D], X[:, t, :], ALU.add).then_inc(x_ready, 1)

                def maxima(j):
                    n = r * B * HEADS + j
                    dve.wait_ge(*filled(("score", n)))
                    if n >= 4:
                        dve.wait_ge(as_["exp"], n - 3)
                    p = filled_bank(("score", n))
                    V.tensor_reduce(nmax[:, n % 4, 0:1], p[:, 0:P], AX_X, ALU.max, negate=True).then_inc(as_["nmax"], 1)
                    V.tensor_reduce(nmax[:, n % 4, 1:2], p[:, P:3 * P], AX_X, ALU.max, negate=True).then_inc(as_["nmax"], 1)

                def low(j):
                    n = r * B * HEADS + j
                    dve.wait_ge(as_["hi"], n + 1)
                    V.tensor_tensor(p_lo[:, n % 3, :], filled_bank(("turn", n))[:, 0:3 * P], p_hi[:, n % 3, :],
                                    ALU.subtract).then_inc(as_["lo"], 1)

                def context(b):
                    for h in range(HALVES):
                        t = b * HALVES + h
                        m = r * TILES + t
                        dve.wait_ge(*filled(("av", m)))
                        av = filled_bank(("av", m))[:, 0:HEADS * VW].rearrange("p (i d) -> p i d", d=VW)
                        if m >= 1:
                            dve.wait_ge(as_["ctx"], m)
                        steps.link(V.reciprocal(rsum.unsqueeze(2), av[:, :, HD:VW]))
                        if m >= 2:
                            dve.wait_ge(*filled(("ctxT", m - 2)))
                        V.tensor_tensor(ctx_t[:, t % 2, :].rearrange("p (i d) -> p i d", d=HD), av[:, :, 0:HD],
                                        rsum.unsqueeze(2).to_broadcast([P, HEADS, HD]), ALU.mult).then_inc(as_["ctx"], 1)

                maxima(0)
                maxima(1)
                for j in range(B * HEADS):
                    b, i = j // HEADS, j % HEADS
                    if j + 2 < B * HEADS:
                        maxima(j + 2)
                    if i == 2 and b >= 1:
                        context(b - 1)
                    low(j)
                    between(b, i, work)
                    if b + AHEAD_SEQ < B and i == STATS:
                        ln_stats(layer, pair(b + AHEAD_SEQ))
                    if b + AHEAD_SEQ < B and i == NORM:
                        ln_norm(layer, pair(b + AHEAD_SEQ))
                context(B - 1)
                for i in sorted(LAST):
                    work(LAST[i][0], B - 1, LAST[i][1])

            def moe1(layer):
                r = (layer - MOE1) // 2
                s = mo_s
                ln(layer, range(TILES))
                for t in range(TILES):
                    dve.wait_ge(s["lg"], r * TILES + t + 1)
                    steps.mark(V.max(mx1[:, t, :], lg1[:, t, :]))
                steps.after(steps.n)
                V.tensor_scalar(nmx1[:, :], mx1[:, :, 0], -1.0, None, ALU.mult).then_inc(s["nmx"], 1)
                for t in range(TILES):
                    steps.mark(V.max_index(ix1[:, t, :], mx1[:, t, :], lg1[:, t, :]))
                steps.after(steps.n)
                steps.link(V.tensor_copy(ixf[:, :, :], ix1[:, :, 0:TOPK]))
                steps.link(V.tensor_tensor(oh.rearrange("p t k e -> p (t k) e"),
                                           iota_row.unsqueeze(1).to_broadcast([P, TILES * TOPK, E1]),
                                           ixf[:, :, :].rearrange("p t k -> p (t k)").unsqueeze(2).to_broadcast([P, TILES * TOPK, E1]),
                                           ALU.is_equal))
                with nc.allow_low_precision(reason="sums of zeros and ones"):
                    V.tensor_reduce(sel[:, :, :], oh.rearrange("p t k e -> p t e k"), AX_X, ALU.add).then_inc(s["sel"], 1)
                dve.wait_ge(*filled(("rnk", r)))
                V.tensor_copy(rnk[:, :, :], filled_bank(("rnk", r))[:, 0:TILES * E1].rearrange("p (t e) -> p t e", e=E1)
                              ).then_inc(s["rnk"], 1)
                dve.wait_ge(*filled(("cnt", r)))
                V.tensor_scalar(cnt_i[:, 0, :], filled_bank(("cnt", r))[:, 0:E1], float(P - 1), None,
                                ALU.add).then_inc(s["cnt"], 1)
                dve.wait_ge(s["cnt"], r + 1)
                steps.link(V.tensor_scalar(cnt_i[:, 1, :], cnt_i[:, 0, :], P.bit_length() - 1, None,
                                           ALU.logical_shift_right))
                steps.link(V.tensor_copy(nblk[:, :], cnt_i[:, 1, :]))
                steps.link(V.tensor_tensor_scan(cum[:, :], ones[:, 0:E1], nblk[:, :], 0.0, ALU.mult, ALU.add))
                V.tensor_scalar(blk_c[:, :], cum[:, :], iota_col, None, ALU.is_le, ALU.add,
                                accum_out=blk_e[:, :]).then_inc(s["blk"], 1)
                steps.link(V.tensor_tensor(start[:, :], cum[:, :], nblk[:, :], ALU.subtract))
                dve.wait_ge(s["rnk"], r + 1)
                steps.link(V.scalar_tensor_tensor(pos, start[:, :].unsqueeze(1).to_broadcast([P, TILES, E1]), float(P),
                                                  rnk[:, :, :], ALU.mult, ALU.add))
                for t in range(TILES):
                    steps.mark(V.tensor_tensor(oh[:, t, :, :], oh[:, t, :, :],
                                               pos[:, t, :].unsqueeze(1).to_broadcast([P, TOPK, E1]), ALU.mult))
                steps.after(steps.n)
                steps.link(V.tensor_reduce(slot_f[:, :, :], oh, AX_X, ALU.add))
                V.tensor_copy(slot[:, :], slot_f[:, :, :].rearrange("p t k -> p (t k)")).then_inc(s["slot"], 1)
                dve.wait_ge(s["slot"], r + 1)
                steps.mark(V.tensor_scalar(row_blk[:, 0, :], slot[:, :].bitcast(I32), P - 1, None, ALU.bitwise_and))
                steps.link(V.tensor_scalar(row_blk[:, 1, :], slot[:, :].bitcast(I32), P.bit_length() - 1, None,
                                           ALU.logical_shift_right))
                steps.link(V.tensor_copy(row_f[:, :, :], row_blk[:, :, :]))
                for i in range(TILES * TOPK):
                    n = r * (TILES * TOPK - 1) + i
                    if i >= PAIRS:
                        dve.wait_ge(s["paired"], n - PAIRS + 1)
                    V.tensor_scalar(at_row[:, i % PAIRS, :], iota_h[:, :], row_f[:, 0, i:i + 1], None,
                                    ALU.is_equal).then_inc(s["pair"], 1)
                    V.tensor_scalar(at_blk[:, i % PAIRS, :], iota_h[:, 0:NBLK], row_f[:, 1, i:i + 1],
                                    tok_id[:, i // TOPK:i // TOPK + 1], ALU.is_equal, ALU.mult).then_inc(s["pair"], 1)
                dve.wait_ge(*filled(("tok", r)))
                V.tensor_copy(tok[:, :], filled_bank(("tok", r))[:, 0:NBLK]).then_inc(s["tok"], 1)
                dve.wait_ge(*filled(("blk", r)))
                V.tensor_scalar(blk_i[:, :], filled_bank(("blk", r))[0:1, 0:P], float(E1 - 1), None,
                                ALU.min).then_inc(s["blki"], 1)
                dve.wait_ge(s["blki"], 2 * r + 1)
                for i in range(WORD):
                    steps.mark(V.tensor_scalar(shifted[:, i, :], blk_i[:, i:i + NBLK].rearrange("p (q i) -> p q i", i=4)[:, :, 0],
                                               BITS * i, None, ALU.logical_shift_left))
                steps.after(steps.n)
                steps.link(V.tensor_tensor(shifted[:, 0:3, :], shifted[:, 0:3, :], shifted[:, 3:6, :], ALU.bitwise_or))
                steps.link(V.tensor_tensor(shifted[:, 0, :], shifted[:, 0, :], shifted[:, 1, :], ALU.bitwise_or))
                V.tensor_tensor(words[:, :], shifted[:, 0, :], shifted[:, 2, :], ALU.bitwise_or).then_inc(s["blki"], 1)
                dve.wait_ge(s["exw"], (r + 1) * TILES)
                steps.link(V.reciprocal(wsum[:, :], wsum[:, :]))
                V.tensor_tensor(wts[:, :, :], wts[:, :, :], wsum[:, :].unsqueeze(2).to_broadcast([P, TILES, TOPK]),
                                ALU.mult).then_inc(s["ws"], 1)
                base = r * NBLK

                def step(stage, m, c, first):
                    j, k = 4 * m + c, c % 2
                    if stage == GATE_UP:
                        dve.wait_ge(s["sg"], j + (base + 1))
                        if not first:
                            dve.wait_ge(s["hturned"], j + (base - 1))
                        V.tensor_tensor(hh[:, k, :], sgt[:, k, :], bank[2 + k][:, FI:2 * FI], ALU.mult).then_inc(s["h"], 1)
                    if stage == DOWN:
                        dve.wait_ge(s["down"], j + (base + 1))
                        if c + base >= NXB:
                            dve.wait_ge(y_out[c % NXB], (m + (c // NXB + base // NXB)) * 16)
                        V.tensor_copy(yb[:, c % NXB, :], bank[6 + k][:, 0:D]).then_inc(s["yb"], 1)

                over_blocks(dve, step)
                dve.wait_ge(s["ws"], r + 1)
                for t in range(TILES):
                    for k in range(TOPK):
                        i = t * TOPK + k
                        dve.wait_ge(y_in[i % NYG], 16 * (i // NYG + 1 + r * TILES * TOPK // NYG))
                        if k:
                            dve.wait_ge(s["comb"], 3 * (r * TILES + t) + k)
                        ins = V.scalar_tensor_tensor(X[:, t, :], yg[:, i % NYG, :], wts[:, t, k:k + 1], X[:, t, :],
                                                     ALU.mult, ALU.add)
                        ins.then_inc(s["comb"] if k < TOPK - 1 else x_ready, 1)
                    if attention_next(layer):
                        if t == 3:
                            ln_stats(layer + 1, range(AHEAD_SEQ * HALVES))
                        if t == 5:
                            ln_norm(layer + 1, range(AHEAD_SEQ * HALVES))

            dve.wait_ge(w_in["mats"], 16)
            for layer in range(LAYERS):
                if layer in (MOE0, MOE0B):
                    moe0(layer)
                elif layer in (ATTA, ATTB):
                    attention(layer)
                elif layer in (MOE1, MOE1B):
                    moe1(layer)
                else:
                    {RWKV: rwkv, MAMBA: mamba}[layer]()

        @block.gpsimd
        def _(pool):
            G = nc.gpsimd
            steps = Steps(pool, pool_step)

            def ln_pow(layer, tiles):
                k = slice(tiles[0] % 8, tiles[0] % 8 + len(tiles))
                pool.wait_ge(ln_var, layer * TILES + tiles[-1] + 1)
                G.tensor_tensor(rstd[:, k], ve[:, k], neghalf[:, 0:len(tiles)], ALU.pow).then_inc(ln_rstd, len(tiles))

            def add_bias(layer, t):
                pool.wait_ge(ln_done, layer * TILES + t + 1)
                G.tensor_tensor(X[:, t, :], X[:, t, :], bo_row(layer), ALU.add).then_inc(xb_ready, 1)

            def rwkv():
                for b in range(B):
                    ln_pow(RWKV, pair(b))
                for b in range(B):
                    pool.wait_ge(xT_ready, (b + 1) * HALVES)
                    if b >= 2:
                        pool.wait_ge(rs["mix"], MIXES * (b - 1))
                    G.tensor_tensor(rw_diff[:, b % 2, :, :], xT[:, :, b, 1:T + 1], xT[:, :, b, 0:T],
                                    ALU.subtract).then_inc(rs["diff"], 1)
                for t in range(TILES):
                    add_bias(RWKV, t)

            def mamba():
                ln_pow(MAMBA, range(TILES))
                pool.wait_ge(ms["ad"], 1)

                def decays(t):
                    if t >= 2:
                        pool.wait_ge(*filled(("seg", t - 2, 1)))
                    for i in range(MH):
                        G.tensor_scalar(m1[:, t % 2, i, :], tri_gt, a_d[:, t * MH + i:t * MH + i + 1], 1.0,
                                        ALU.mult, ALU.mult).then_inc(ms["m1"], 1)

                wide = "p (h n) -> p h n"
                decays(0)
                decays(1)
                for t in range(TILES):
                    b, h = t // HALVES, t % HALVES
                    pool.wait_ge(ms["htok"], t + 1)
                    if t >= 1:
                        pool.wait_ge(ms["y"], t)
                    G.tensor_tensor(dh.rearrange(wide, h=MH), htok[:, t % 2, :].rearrange(wide, h=MH),
                                    d_row.unsqueeze(2).to_broadcast([P, MH, MP]), ALU.mult).then_inc(ms["dh"], 1)
                    if h == 0:
                        pool.wait_ge(ms["dsc"], b + 1)
                        if b >= 1:
                            pool.wait_ge(*filled(("state", b - 1)))
                        G.tensor_tensor(hdec.rearrange(wide, h=MH), htok[:, t % 2, :].rearrange(wide, h=MH),
                                        dsc[:, :].unsqueeze(2).to_broadcast([P, MH, MP]), ALU.mult).then_inc(ms["hdec"], 1)
                    if t + 2 < TILES:
                        decays(t + 2)
                    if t >= 1:
                        rms(t - 1)
                rms(TILES - 1)

            def rms(t):
                pool.wait_ge(act_step, t + 1)
                steps.link(G.tensor_scalar(mvar[:, t:t + 1], mss[:, t:t + 1], 1.0 / ME, RMS_EPS, ALU.mult, ALU.add))
                G.tensor_tensor(mrs[:, t:t + 1], mvar[:, t:t + 1], neghalf[:, 0:1], ALU.pow).then_inc(ms["rs"], 1)

            def attention(layer, start=None):
                r = (layer - ATTA) // 2

                def take_apart(parts, whole, rest):
                    steps.link(G.tensor_copy(parts[0], whole))
                    steps.link(G.tensor_tensor(rest, whole, parts[0], ALU.subtract))
                    steps.link(G.tensor_copy(parts[1], rest))
                    return G.tensor_tensor(parts[2], rest, parts[1], ALU.subtract)

                def split(b):
                    seq = r * B + b
                    pool.wait_ge(as_["k"], seq + 1)
                    if seq >= 1:
                        pool.wait_ge(k_out, 16 * seq)
                        pool.wait_ge(as_["kparts"], seq)
                    rows_, cols_ = slice(0, NG * HD), slice(DC * T, QK)
                    take_apart([qk_part[rows_, l, cols_] for l in range(PARTS)], qkf[rows_, cols_],
                               q_rest[rows_, cols_]).then_inc(as_["kparts"], 1)
                    for c in range(DC):
                        pool.wait_ge(as_["q"], DC * seq + c + 1)
                        if seq >= 1:
                            pool.wait_ge(q_out, 16 * DC * seq)
                            pool.wait_ge(as_["qparts"], DC * (seq - 1) + c + 1)
                        cols_ = slice(c * T, (c + 1) * T)
                        take_apart([qk_part[:, l, cols_] for l in range(PARTS)], qkf[:, cols_],
                                   q_rest[:, cols_]).then_inc(as_["qparts"], 1)
                    pool.wait_ge(as_["v"], seq + 1)
                    if seq >= 1:
                        pool.wait_ge(as_["vparts"], seq)
                    if seq >= 3:
                        pool.wait_ge(*filled(("av", (seq - 2) * HALVES - 1)))
                    inner = "p (n d) -> p n d"
                    take_apart([vt[:, seq % 3, l, :, 0:HD] for l in range(PARTS)], vf.rearrange(inner, d=HD),
                               v_rest.rearrange(inner, d=HD)).then_inc(as_["vparts"], 1)

                if start is not None:
                    split(start)
                    for h in range(HALVES):
                        add_bias(layer, start * HALVES + h)
                    return
                for b in range(AHEAD_SEQ, B):
                    ln_pow(layer, pair(b))
                    split(b)
                    for h in range(HALVES):
                        add_bias(layer, b * HALVES + h)

            def moe1(layer):
                r = (layer - MOE1) // 2
                s = mo_s
                ln_pow(layer, range(TILES))
                pool.wait_ge(s["tok"], r + 1)
                pool.wait_ge(xn_out, 16 * TILES * (r + 1))
                for j in range(NBLK):
                    if j + r * NBLK >= NXB:
                        pool.wait_ge(s["turned"], r * NBLK + j - NXB + 1)
                    G.indirect_dma_start(out=xb[:, j % NXB, :], out_offset=None, in_=xn_d[:],
                                         in_offset=bass.IndirectOffsetOnAxis(ap=tok[:, j:j + 1], axis=0)
                                         ).then_inc(xb_in[j % NXB], 16)
                for k in range(NXB):
                    pool.wait_ge(y_out[k], 16 * (NBLK // NXB) * (r + 1))
                for t in range(TILES):
                    for k in range(TOPK):
                        i = t * TOPK + k
                        if i >= NYG:
                            if k < TOPK - 1:
                                pool.wait_ge(s["comb"], 3 * (r * TILES + t - NYG // TOPK) + k + 1)
                            else:
                                pool.wait_ge(x_ready, layer * TILES + t - NYG // TOPK + 1)
                        G.indirect_dma_start(out=yg[:, i % NYG, :], out_offset=None, in_=yg_d[:],
                                             in_offset=bass.IndirectOffsetOnAxis(ap=slot[:, i:i + 1], axis=0)
                                             ).then_inc(y_in[i % NYG], 16)
                    if t == 5 and attention_next(layer):
                        ln_pow(layer + 1, range(AHEAD_SEQ * HALVES))
                if attention_next(layer):
                    for b in range(AHEAD_SEQ):
                        attention(layer + 1, start=b)

            G.memset(xT[:, :, :, 0:1], 0.0).then_inc(prep, 1)
            G.memset(neghalf[:, :], -0.5).then_inc(prep, 1)
            G.memset(vt[:, :, 0, :, :], 1.0).then_inc(prep, 1)
            G.memset(vt[:, :, 1:PARTS, :, :], 0.0).then_inc(prep, 1)
            pool.wait_ge(w_in["small"], 16 * SMALLS)
            pool.wait_ge(w_in["mats"], 16)
            G.tensor_copy(mask_b[:, :], mask_f).then_inc(prep, 1)
            G.tensor_copy(ident_b[:, :], ident).then_inc(prep, 1)
            G.tensor_copy(tri_lt_b[:, :], tri_lt).then_inc(prep, 1)
            G.tensor_copy(ones_b[:, :], ones).then_inc(prep, 1)
            G.tensor_copy(iota_h[:, :], iotas[:, 0:P]).then_inc(prep, 1)
            pool.wait_ge(prep, PREPS)
            for layer in range(LAYERS):
                if layer in (MOE0, MOE0B):
                    ln_pow(layer, range(TILES))
                    if attention_next(layer):
                        ln_pow(layer + 1, range(AHEAD_SEQ * HALVES))
                        for b in range(AHEAD_SEQ):
                            attention(layer + 1, start=b)
                elif layer in (ATTA, ATTB):
                    attention(layer)
                elif layer in (MOE1, MOE1B):
                    moe1(layer)
                else:
                    {RWKV: rwkv, MAMBA: mamba}[layer]()

        @block.sync
        def _(sp):
            first_use = {"moe0": MOE0, "mamba": MAMBA, "att": ATTA}

            def load(key, tile, name):
                if first_use.get(key, 0) < LAYERS:
                    sp.dma_start(tile, a[name]).then_inc(w_in[key], 16)

            xv = a["x"].rearrange("(t p) d -> p t d", p=P)
            for t in range(TILES):
                sp.dma_start(X[:, t, :], xv[:, t, :]).then_inc(x_in[t], 16)
                if t == 0:
                    load("mats", mats[:, :, :], "mats")
            for tile, name in ((cols, "cols"), (rows, "rows"), (iotas, "iotas"), (mb_conv, "mb_conv"), (mb_norm, "mb_norm"),
                               (mask_f, "mask"), (rt_w, "rt_w"), (f0_wg, "f0_wg")):
                load("small", tile[:], name)
            load("rwkv", rw_w[:], "rw_w")
            load("moe0", f0_w[:], "f0_w")
            load("moe0", f0_b[:], "f0_b")
            load("mamba", mb_in[:], "mb_in")
            load("mamba", mb_out[:], "mb_out")
            for tile, name in ((at_q, "at_q"), (at_k, "at_k"), (at_v, "at_v"), (at_o, "at_o")):
                load("att", tile[:], name)
            if LAYERS > MOE1:
                sp.wait_ge(x_ready, (MAMBA + 1) * TILES)
                load("moe1", gu_w, "gu_w")
                load("moe1", dn_w, "dn_w")

            def alibi():
                for k in range(2):
                    for tile, name in ((Qs, "al_q"), (Ks, "al_k")):
                        view = a[name].bitcast(BF16).rearrange("p (h t) -> p h t", t=T)
                        sp.dma_start(tile[QROWS:QROWS + AROWS, k, :, :], view).then_inc(w_in["alibi"], 16)

            def stack(layer):
                for b in range(B):
                    seq = (layer - ATTA) // 2 * B + b
                    if seq >= 1:
                        sp.wait_ge(qk_in, 16 * 2 * len(SLOTS_Q) * seq)
                    sp.wait_ge(as_["kparts"], seq + 1)
                    sp.dma_start(k_d.rearrange("l h d t -> (h d) l t"), qk_part[0:NG * HD, :, DC * T:QK]).then_inc(k_out, 16)
                    for c in range(DC):
                        sp.wait_ge(as_["qparts"], DC * seq + c + 1)
                        sp.dma_start(q_d[:, c * HEADS // DC:(c + 1) * HEADS // DC].rearrange("l h d t -> (h d) l t"),
                                     qk_part[:, :, c * T:(c + 1) * T]).then_inc(q_out, 16)
                    sp.wait_ge(k_out, 16 * (seq + 1))
                    if seq == 0:
                        sp.wait_ge(x_ready, ATTA * TILES)
                        alibi()
                    if seq >= 2:
                        sp.wait_ge(as_["exp"], HEADS * (seq - 1))
                    for i, l in enumerate(SLOTS_K):
                        sp.dma_start(Ks[i * HD:(i + 1) * HD, seq % 2, :, :], k_d[l].rearrange("h d t -> d h t")).then_inc(qk_in, 16)
                    sp.wait_ge(q_out, 16 * DC * (seq + 1))
                    for i, l in enumerate(SLOTS_Q):
                        sp.dma_start(Qs[i * HD:(i + 1) * HD, seq % 2, :, :], q_d[l].rearrange("h d t -> d h t")).then_inc(qk_in, 16)

            for layer in range(ATTA, LAYERS):
                if layer in (ATTA, ATTB):
                    stack(layer)
                    continue
                base = (layer - MOE1) // 2 * NBLK
                xnv = xn_d.rearrange("(t p) d -> p t d", p=P)
                for t in range(TILES):
                    sp.wait_ge(ln_done, layer * TILES + t + 1)
                    sp.dma_start(xnv[:, t, :], xn[:, t, :]).then_inc(xn_out, 16)

                def store(j, c):
                    sp.wait_ge(mo_s["yb"], j + (base + 1))
                    sp.dma_start(yg_d[bass.ds(j * P, P), :], yb[:, c, :]).then_inc(y_out[c], 16)

                with sp.Fori(0, NBLK // NXB) as m:
                    for c in range(NXB):
                        store(NXB * m + c, c)
            ov = out.rearrange("(t p) d -> p t d", p=P)
            for t in range(TILES):
                sp.wait_ge(x_ready, (LAYERS - 1) * TILES + t + 1)
                sp.dma_start(ov[:, t, :], X[:, t, :]).then_inc(out_done, 16)
            sp.wait_ge(out_done, 16 * TILES)


def kernel(**inputs):
    import numpy as np
    import concourse.bacc as bacc
    from concourse import mybir as mb
    from concourse.bass_utils import run_bass_kernel_spmd

    def np32(name):
        return np.asarray(inputs[name])

    def feature(w):
        return w.reshape(-1, P, w.shape[-1]).transpose(1, 0, 2)

    def column(v):
        return v.reshape(-1, P).T

    def everywhere(v):
        return np.broadcast_to(v, (P, v.shape[-1]))

    L0, L1, L2, L3 = "L0_attn_a_", "L0_attn_b_", "L1_attn_a_", "L1_attn_b_"
    x = np32(L0 + "x")
    f = np.float32
    arrays = {"x": x.reshape(-1, D)}
    arrays["rw_w"] = np.stack([feature(np32(L0 + n).T) for n in ("Wk", "Wv", "Wr", "Wo")], axis=1)
    arrays["cols"] = np.stack([column(np32(L0 + n)) for n in ("bk", "bv", "br", "tmk", "tmv", "tmr", "u", "w")], axis=1)
    arrays["rows"] = everywhere(np.concatenate([np32(L1 + "dt_bias"), np32(L1 + "A_log"), np32(L1 + "D"),
                                                np32(L0 + "bo"), np32(L2 + "bo"), np32(L3 + "bo")]))
    arrays["f0_wg"] = feature(np32("L0_ffn_wg"))
    arrays["f0_w"] = feature(np32("L0_ffn_W").transpose(2, 0, 1).reshape(D, E0 * D))
    arrays["f0_b"] = np32("L0_ffn_b")
    arrays["mb_in"] = feature(np32(L1 + "in_proj_w").T)
    taps = np.concatenate([np32(L1 + "conv_w"), np32(L1 + "conv_b")[:, None]], axis=1)
    conv = np.zeros((P, CHUNKS, TAPS + 1), f)
    conv[:, :MC] = feature(taps[:ME])
    conv[:MN, MC:] = taps[ME:].reshape(2, MN, TAPS + 1).transpose(1, 0, 2)
    arrays["mb_conv"] = conv
    arrays["mb_norm"] = column(np32(L1 + "norm_w"))
    arrays["mb_out"] = feature(np32(L1 + "out_proj_w").T)

    wkv = np32(L3 + "Wkv")
    arrays["at_q"] = np.stack([feature(np32(L2 + "Wq")), feature(np32(L3 + "Wq"))], axis=1)
    arrays["at_k"] = np.stack([feature(np32(L2 + "Wk")), feature(wkv[:, :NG * HD])], axis=1)
    arrays["at_v"] = np.stack([feature(np32(L2 + "Wv")), feature(wkv[:, NG * HD:])], axis=1)
    arrays["at_o"] = np.stack([feature(np32(L2 + "Wo")), feature(np32(L3 + "Wo"))], axis=1)
    arrays["rt_w"] = feature(np32("L1_ffn_router_w").T)
    gate_up = np.concatenate([np32("L1_ffn_gate_w"), np32("L1_ffn_up_w")], axis=1)
    arrays["gu_w"] = feature(gate_up.transpose(2, 0, 1).reshape(D, E1 * 2 * FI))
    arrays["dn_w"] = np32("L1_ffn_down_w").transpose(2, 0, 1).reshape(FI, E1 * D)

    i, j = np.arange(P)[:, None], np.arange(P)[None, :]
    arrays["mats"] = np.stack([i == j, i > j, i <= j, i < j, i >= 0 * j], axis=1).astype(f)
    arrays["iotas"] = np.concatenate([np.broadcast_to(j, (P, P)), i + P * np.arange(TILES)[None, :]], axis=1).astype(f)
    later = np.where(j > i, f(-1e30), f(0))
    arrays["mask"] = later

    def parts(v):
        found = []
        for _ in range(PARTS):
            upper = v.view(np.uint32) >> 16
            found.append(upper.astype(np.uint16))
            v = v - (upper << 16).astype(np.uint32).view(f)
        return found

    first = 2.0 ** (-2.0 ** (-(np.log2(HEADS) - 3.0)))
    slopes = np.array([first ** (h + 1) for h in range(HEADS)], f)[:, None]
    counter = np.arange(T, dtype=f)[None, :]
    q_rows = parts(slopes + 0 * counter) + parts(-slopes * counter)
    k_rows = PARTS * [parts(counter + np.zeros((NG, 1), f))[0]] + PARTS * [parts(np.ones((NG, T), f))[0]]
    for name, r in (("al_q", q_rows), ("al_k", k_rows)):
        arrays[name] = np.stack(r).reshape(AROWS, -1).view(f)

    nc = bacc.Bacc("TRN2", target_bir_lowering=False, num_devices=1)
    arrays = {f"in_{k}": np.ascontiguousarray(v) for k, v in arrays.items()}
    aps = {k[3:]: nc.dram_tensor(k, v.shape, mb.dt.float32, kind="ExternalInput").ap() for k, v in arrays.items()}
    out = nc.dram_tensor("out_0", (B * T, D), mb.dt.float32, kind="ExternalOutput").ap()
    build(nc, aps, out)
    r = run_bass_kernel_spmd(nc, [arrays], core_ids=[0])
    return r.results[0]["out_0"].reshape(x.shape)
```

```python
from contextlib import ExitStack

import concourse.bass as bass
from concourse import mybir

ALU = mybir.AluOpType
ACT = mybir.ActivationFunctionType
AX_X = mybir.AxisListType.X
F32 = mybir.dt.float32
BF16 = mybir.dt.bfloat16
F16 = mybir.dt.float16
I32 = mybir.dt.int32
U32 = mybir.dt.uint32

LAYERS = 8
P = 128
B, T, D = 4, 256, 256
TILES = B * T // P
HALVES = T // P
DC = D // P
E0 = 8
MH, MP, MN = 8, 64, 64
ME = MH * MP
MC = ME // P
MPROJ = 2 * ME + 2 * MN + MH
TAPS = 4
NG, NS, HD = 4, 4, 16
PARTS = 3
SLOTS_Q, SLOTS_K = (0, 0, 0, 1, 1, 2), (0, 1, 2, 0, 1, 0)
QROWS = len(SLOTS_Q) * HD
AROWS = 2 * PARTS
HEADS = NS * NG
P_SCALE = 2.0 ** 15
VW = HD + 1
E1, TOPK, FI = 32, 4, 96
NBLK = B * T * TOPK // P + E1
SLOTS = NBLK * P
BITS = (E1 - 1).bit_length()
WORD = 6
LN_EPS, RMS_EPS = 1e-5, 1e-6
CHUNKS = MC + 2
RWKV, MOE0, MAMBA, MOE0B, ATTA, MOE1, ATTB, MOE1B = range(8)
BIASED = {RWKV: 0, ATTA: 1, ATTB: 2}


def build(nc, a, out):
    with ExitStack() as ctx:
        def sb(name, shape, dt=F32):
            return ctx.enter_context(nc.sbuf_tensor(name, shape, dt))[:]

        def sem(name):
            return ctx.enter_context(nc.semaphore(name))

        X = sb("X", [P, TILES, D])
        xn = sb("xn", [P, TILES, D])
        xT = sb("xT", [P, DC, B, T + 1])
        cols = sb("cols", [P, 8, DC])
        rows = sb("rows", [P, 3 * MH + 3 * D])
        f0_wg = sb("f0_wg", [P, DC, E0])
        f0_b = sb("f0_b", [E0, D])
        mb_conv = sb("mb_conv", [P, CHUNKS, TAPS + 1])
        mb_norm = sb("mb_norm", [P, MC])
        at_q = sb("at_q", [P, 2, DC, HEADS * HD])
        at_k = sb("at_k", [P, 2, DC, NG * HD])
        at_v = sb("at_v", [P, 2, DC, NG * HD])
        at_o = sb("at_o", [P, 2, DC, D])
        rt_w = sb("rt_w", [P, DC, E1])
        mats = sb("mats", [P, 5, P])
        iotas = sb("iotas", [P, P + TILES])
        mask_b = sb("mask_b", [P, P], BF16)
        ident_b, tri_lt_b, ones_b = (sb(name, [P, P], BF16) for name in ("ident_b", "tri_lt_b", "ones_b"))
        neghalf = sb("neghalf", [P, TILES])
        ident, tri_gt, tri_le, tri_lt, ones = (mats[:, i, :] for i in range(5))
        iota_row, iota_col = iotas[:, 0:E1], iotas[:, P:P + 1]
        tok_id = iotas[:, P:P + TILES]
        wk_c, wv_c, wr_c, tmk, tmv, tmr, u_c, w_c = (cols[:, i, :] for i in range(8))
        dt_bias, a_log, d_row = (rows[:, i * MH:(i + 1) * MH] for i in range(3))

        def bo_row(layer):
            i = 3 * MH + BIASED[layer] * D
            return rows[:, i:i + D]

        st6 = sb("st6", [P, 8, 6])
        mv = sb("mv", [P, 8, 2])
        ve = sb("ve", [P, 8])
        rstd = sb("rstd", [P, 8])

        GUW = DC * E1 * 2 * FI
        arena = sb("arena", [P, GUW + E1 * D])
        gu_w = arena[:, 0:GUW].rearrange("p (c n) -> p c n", c=DC)
        dn_w = arena[0:FI, GUW:GUW + E1 * D]

        class Carver:
            def __init__(self, tensor, size):
                self.tensor, self.at, self.size = tensor, 0, size

            def take(self, *dims, parts=P):
                n = 1
                for d in dims:
                    n *= d
                ap = self.tensor[0:parts, self.at:self.at + n]
                self.at += n
                assert self.at <= self.size, (self.at, self.size)
                if len(dims) == 2:
                    return ap.rearrange("p (a b) -> p a b", a=dims[0])
                if len(dims) == 3:
                    return ap.rearrange("p (a b c) -> p a b c", a=dims[0], b=dims[1])
                return ap

        EARLY = 4 * DC * D + DC * E0 * D + DC * MPROJ + MC * D
        early = sb("early", [P, EARLY])
        ew = Carver(early, EARLY)
        rw_w = ew.take(4 * DC, D).rearrange("p (i c) n -> p i c n", i=4)
        f0_w = ew.take(DC, E0 * D)
        MAMBA_AT = ew.at
        mb_in = ew.take(DC, MPROJ)
        mb_out = ew.take(MC, D)
        ea = Carver(early, EARLY)

        rw = Carver(arena, GUW + E1 * D)
        mix = [rw.take(DC, B, T) for _ in range(3)]
        rw_diff = rw.take(2, DC, T)
        rw_t, rw_d, rw_e1, rw_e2, rw_a, rw_b = ([rw.take(DC, T) for _ in range(2)] for _ in range(6))
        rw_ev, rw_q, rw_z = (rw.take(DC, T) for _ in range(3))

        mb = Carver(arena, GUW + E1 * D)
        hs = mb.take(MC, B, T)
        bc = mb.take(2, B, T, parts=MN)
        sg = mb.take(TILES, ME)
        hcv = mb.take(2, CHUNKS, T)
        htok = mb.take(2, ME)
        btok = mb.take(MN)
        m1 = mb.take(2, MH, P)
        Lx = mb.take(MH, P)
        mt = mb.take(MH, P)
        gm = mb.take(P)
        hdec = mb.take(ME)
        dh = mb.take(ME)
        mst = mb.take(ME, parts=MN)
        a_row = sb("a_row", [P, MH])
        epre = sb("epre", [P, MH])
        esuf = sb("esuf", [P, MH])
        dsc = sb("dsc", [P, MH])
        mss = sb("mss", [P, TILES])
        mvar = sb("mvar", [P, TILES])
        mrs = sb("mrs", [P, TILES])
        negw = sb("negw", [P, DC])
        ubk = sb("ubk", [P, DC])

        lg0 = sb("lg0", [P, TILES, E0])
        mx0 = sb("mx0", [P, TILES, 8])
        ix0 = sb("ix0", [P, TILES, 8], U32)
        ex0 = sb("ex0", [P, TILES, E0])
        nmx0, sum0, gate0, idx0 = (sb(name, [P, TILES]) for name in ("nmx0", "sum0", "gate0", "idx0"))
        cmb = sb("cmb", [P, TILES, E0])
        cmbT = sb("cmbT", [E0, TILES, P])
        acc = sb("acc", [P, 2, D])

        LATE = 6700
        late = sb("late", [P, LATE])
        mb_late = Carver(late, LATE)
        y1 = mb_late.take(ME)
        yf = mb_late.take(ME)
        ysq = mb_late.take(ME)
        yfT = mb_late.take(MC, P)
        dtr, sp_neg, sp_e, sp_u, sp_d, sp_l, dt, a_d, sp_mask, sp_q = (mb_late.take(TILES * MH) for _ in range(10))
        mask_f = late[:, 0:P]
        at = Carver(late, LATE)
        QK = DC * T + T
        qkf = at.take(QK)
        vf = at.take(HALVES * NG * HD)
        q_rest = at.take(QK)
        v_rest = at.take(HALVES * NG * HD)
        qk_part = at.take(PARTS * QK // 2).bitcast(BF16).rearrange("p (l n) -> p l n", l=PARTS)
        pexp = at.take(3, 3 * P)
        p_hi, p_lo = (at.take(3 * 3 * P // 2).bitcast(F16).rearrange("p (i n) -> p i n", i=3) for _ in range(2))
        rsum = at.take(NG * NS)
        ctx_t = at.take(2, D)
        ctxT = at.take(2, DC, P)
        nmax = sb("nmax", [P, 4, 2])
        vt = sb("vt", [P, 3, PARTS, HALVES * NG, VW], BF16)

        NXB, NYG = 4, 8
        mo = Carver(late, LATE)
        xb = mo.take(NXB, D)
        xbT = mo.take(2, DC, P)
        sgt = mo.take(2, FI)
        hh = mo.take(2, FI)
        hT = mo.take(2, P, parts=FI)
        yb = mo.take(NXB, D)
        lg1 = sb("lg1", [P, TILES, E1])
        mx1 = sb("mx1", [P, TILES, 8])
        ix1 = sb("ix1", [P, TILES, 8], U32)
        ixf = sb("ixf", [P, TILES, TOPK])
        oh = mo.take(TILES, TOPK, E1)
        pos = mo.take(TILES, E1)
        nmx1 = sb("nmx1", [P, TILES])
        wts = sb("wts", [P, TILES, TOPK])
        wsum = sb("wsum", [P, TILES])
        sel = sb("sel", [P, TILES, E1], BF16)
        rnk = sb("rnk", [P, TILES, E1])
        cnt = sb("cnt", [P, E1])
        cnt_i = sb("cnt_i", [P, 2, E1], I32)
        nblk = sb("nblk", [P, E1])
        cum = sb("cum", [P, E1])
        start = sb("start", [P, E1])
        blk_e = sb("blk_e", [P, 1])
        blk_c = sb("blk_c", [P, E1])
        blk_i = sb("blk_i", [1, P], I32)
        shifted = sb("shifted", [1, WORD, NBLK // 4], I32)
        words = sb("words", [1, NBLK // 4], I32)
        slot_f = sb("slot_f", [P, TILES, TOPK])
        slot = sb("slot", [P, TILES * TOPK], U32)
        row_blk = sb("row_blk", [P, 2, TILES * TOPK], I32)
        row_f = sb("row_f", [P, 2, TILES * TOPK])
        iota_h = sb("iota_h", [P, P], F16)
        PAIRS = 4
        Qs = [ea.take(HEADS * T // 2)]
        yg = ea.take(NYG, D)
        at_row = ea.take(PAIRS * P // 2).bitcast(F16).rearrange("p (i n) -> p i n", i=PAIRS)
        at_blk = ea.take(PAIRS * NBLK // 2).bitcast(F16).rearrange("p (i n) -> p i n", i=PAIRS)
        ea.at = MAMBA_AT
        Qs.append(ea.take(HEADS * T // 2))
        Qs = [q.bitcast(BF16).rearrange("p (h t) -> p h t", h=HEADS) for q in Qs]
        Ks = [ea.take(NG * T // 2).bitcast(BF16).rearrange("p (h t) -> p h t", h=NG) for _ in range(2)]
        tok = sb("tok", [P, NBLK], U32)

        bank = [ctx.enter_context(nc.psum_tensor(f"bank{i}", [P, 512], F32)) for i in range(8)]

        xn_d = nc.dram_tensor("normed_x", [B * T, D], F32, kind="Internal").ap()
        q_d = nc.dram_tensor("q_parts", [PARTS, HEADS, HD, T], BF16, kind="Internal").ap()
        k_d = nc.dram_tensor("k_parts", [PARTS, NG, HD, T], BF16, kind="Internal").ap()
        yg_d = nc.dram_tensor("grouped_y", [SLOTS, D], F32, kind="Internal").ap()

        x_in = [sem(f"x_in{t}") for t in range(TILES)]
        w_in = {k: sem(f"w_{k}") for k in ("small", "mats", "rwkv", "moe0", "mamba", "att", "alibi", "moe1")}
        xn_out = sem("xn_out")
        out_done = sem("out_done")
        k_out, q_out = sem("k_out"), sem("q_out")
        qk_in = sem("qk_in")
        dve_step, act_step, pool_step = sem("dve_step"), sem("act_step"), sem("pool_step")
        prep = sem("prep")
        ln_var, ln_rstd, ln_done = sem("ln_var"), sem("ln_rstd"), sem("ln_done")
        xT_ready = sem("xT_ready")
        xb_ready = sem("xb_ready")
        x_ready = sem("x_ready")
        full = [sem(f"bank_full{i}") for i in range(8)]

        fills = {}
        used = [0] * 8
        free_at = [None] * 8

        def claim(pe, b, key, freed_by):
            if free_at[b] is not None:
                pe.wait_ge(*free_at[b])
            free_at[b] = freed_by
            used[b] += 1
            fills[key] = b, used[b]
            return bank[b]

        def filled(key):
            b, count = fills[key]
            return full[b], count

        def filled_bank(key):
            return bank[fills[key][0]]

        class Steps:
            def __init__(self, eng, s):
                self.eng, self.s, self.n = eng, s, 0

            def mark(self, ins):
                ins.then_inc(self.s, 1)
                self.n += 1
                return self.n

            def after(self, n):
                self.eng.wait_ge(self.s, n)

            def link(self, ins):
                self.after(self.mark(ins))

        MIXES = 3 * DC
        PREPS = 9
        SMALLS = 8
        TPB = (0, 1)

        def xcols(t):
            return xT[:, :, t // HALVES, 1 + (t % HALVES) * P:1 + (t % HALVES + 1) * P]

        rs = {k: sem(f"rw_{k}") for k in ("diff", "mix", "silu", "td", "exp", "ab", "rb", "q", "z", "col")}
        m0 = {k: sem(f"m0_{k}") for k in ("lg", "nmx", "sum", "cmb", "cmbT", "ex")}
        ms = {k: sem(f"mb_{k}") for k in ("dtr", "dtneg", "spe", "spu", "spl", "ad", "tap", "cv", "cvs", "sg", "htok", "btok",
                                          "gm", "esuf", "epre", "dsc", "m1", "L", "mt", "hdec", "dh", "st", "y", "yf",
                                          "yfT", "rs", "y1")}
        as_ = {k: sem(f"at_{k}") for k in ("k", "v", "q", "kparts", "qparts", "vparts", "nmax", "exp", "hi", "lo", "ctx", "ctxT")}
        mo_s = {k: sem(f"m1_{k}") for k in ("lg", "nmx", "exw", "sel", "rnk", "cnt", "blk", "blki", "slot",
                                            "xbT", "sg", "h", "hT", "yb", "comb", "rowf", "row", "row_odd", "pair",
                                            "paired", "tok", "turned", "gu", "hturned", "down", "ws")}

        xb_in = [sem(f"xb_in{k}") for k in range(NXB)]
        y_out = [sem(f"y_out{k}") for k in range(NXB)]
        y_in = [sem(f"y_in{k}") for k in range(NYG)]

        NEXT = {8: ("turn_x", 0), 9: ("turn_x", 1), 10: ("keys", 0), 11: ("queries", 0), 12: ("queries", 1), 13: ("values", 0)}
        LAST = {3: ("turn_ctx", 0), 4: ("project", 0), 5: ("turn_ctx", 1), 6: ("project", 1)}

        def pair(b):
            return range(b * HALVES, (b + 1) * HALVES)

        EARLY_SEQ = B - 1

        def eager_next(layer):
            return layer in (RWKV, MOE0, MAMBA) and layer + 1 < LAYERS

        def attention_next(layer):
            return layer + 1 in (ATTA, ATTB) and layer + 1 < LAYERS

        START = {5: 0, 7: 1}
        AHEAD_SEQ = 2
        STATS, NORM = 3, 7

        FINAL = (("turn_ctx", 0, 0), ("turn_ctx", 1, 5), ("project", 0, 0), ("project", 1, 5))

        COMBINE = {0: 4, 1: 5, 12: 6, 14: 7}

        EARLY_TILES = 4
        TURN_NEXT = {8: 0, 9: 1, 10: 2, 11: 3}

        def moe_next(layer):
            return layer in (ATTA, ATTB) and layer + 1 < LAYERS

        def between(b, i, work):
            if i in NEXT and b + AHEAD_SEQ < B:
                work(NEXT[i][0], b + AHEAD_SEQ, NEXT[i][1])
            if i in LAST and b >= 1:
                work(LAST[i][0], b - 1, LAST[i][1])

        TURN_X, GATE_UP, TURN_H, DOWN, FETCH = range(5)
        AHEAD = ((TURN_X, 3), (GATE_UP, 2), (TURN_H, 1), (DOWN, 0))
        PEEL = 4
        GROUP = 8
        LOOPS = (NBLK - PEEL - 3 - NXB) // GROUP

        def over_blocks(eng, step):
            step(FETCH, 0, 0, True)
            for j in range(-3, PEEL):
                for stage, ahead in AHEAD:
                    if j + ahead >= 0:
                        step(stage, 0, j + ahead, j + ahead < 2)
            with eng.Fori(0, LOOPS) as turn:
                m = turn * (GROUP // 4)
                for c in range(PEEL, PEEL + GROUP, 4):
                    step(FETCH, m, c, False)
                for c in range(PEEL, PEEL + GROUP):
                    for stage, ahead in AHEAD:
                        step(stage, m, c + ahead, False)
            for j in range(PEEL + GROUP * LOOPS, NBLK):
                if j % 4 == 0:
                    step(FETCH, 0, j, False)
                for stage, ahead in AHEAD:
                    if j + ahead < NBLK:
                        step(stage, 0, j + ahead, False)

        def take_apart(eng, steps, parts, whole, rest):
            steps.link(eng.tensor_copy(parts[0], whole))
            steps.link(eng.tensor_tensor(rest, whole, parts[0], ALU.subtract))
            steps.link(eng.tensor_copy(parts[1], rest))
            return eng.tensor_tensor(parts[2], rest, parts[1], ALU.subtract)

        def split(queue, eng, steps, r, b):
            seq = r * B + b
            queue.wait_ge(as_["k"], seq + 1)
            if seq >= 1:
                queue.wait_ge(k_out, 16 * seq)
                queue.wait_ge(as_["kparts"], seq)
            rows_, cols_ = slice(0, NG * HD), slice(DC * T, QK)
            take_apart(eng, steps, [qk_part[rows_, l, cols_] for l in range(PARTS)], qkf[rows_, cols_],
                       q_rest[rows_, cols_]).then_inc(as_["kparts"], 1)
            for c in range(DC):
                queue.wait_ge(as_["q"], DC * seq + c + 1)
                if seq >= 1:
                    queue.wait_ge(q_out, 16 * DC * seq)
                    queue.wait_ge(as_["qparts"], DC * (seq - 1) + c + 1)
                cols_ = slice(c * T, (c + 1) * T)
                take_apart(eng, steps, [qk_part[:, l, cols_] for l in range(PARTS)], qkf[:, cols_],
                           q_rest[:, cols_]).then_inc(as_["qparts"], 1)
            queue.wait_ge(as_["v"], seq + 1)
            if seq >= 1:
                queue.wait_ge(as_["vparts"], seq)
            if seq >= 3:
                queue.wait_ge(*filled(("av", (seq - 2) * HALVES - 1)))
            inner = "p (n d) -> p n d"
            take_apart(eng, steps, [vt[:, seq % 3, l, :, 0:HD] for l in range(PARTS)], vf.rearrange(inner, d=HD),
                       v_rest.rearrange(inner, d=HD)).then_inc(as_["vparts"], 1)

        block = ctx.enter_context(nc.Block())

        @block.tensor
        def _(pe):
            mm = nc.tensor.matmul

            def ln_T(layer, t, bk=None):
                n = layer * TILES + t
                bk = TPB[t % 2] if bk is None else bk
                pe.wait_ge(ln_done, n + 1)
                p = claim(pe, bk, ("xT", n), (xT_ready, n + 1))
                for c in range(DC):
                    ins = nc.tensor.transpose(p[:, c * P:(c + 1) * P], xn[:, t, c * P:(c + 1) * P], ident)
                ins.then_inc(full[bk], 1)

            def rwkv():
                layer = RWKV
                pe.wait_ge(w_in["mats"], 16)
                for t in range(TILES):
                    ln_T(layer, t)
                pe.wait_ge(w_in["rwkv"], 16)

                def kvr(b):
                    pe.wait_ge(rs["mix"], MIXES * (b + 1))
                    for i, freed in enumerate(((rs["td"], b + 1), (rs["ab"], b + 1), (rs["z"], b + 1))):
                        bk = 2 + 3 * (b % 2) + i
                        if i == 2:
                            pe.wait_ge(rs["silu"], b + 1)
                        p = claim(pe, bk, ("kvr", b, i), freed)
                        for e in range(DC):
                            for c in range(DC):
                                ins = mm(p[:, e * T:(e + 1) * T], rw_w[:, i, c, e * P:(e + 1) * P],
                                         mix[i][:, c, b, :], start=(c == 0), stop=(c == DC - 1))
                        ins.then_inc(full[bk], 1)

                def project(b):
                    pe.wait_ge(rs["z"], b + 1)
                    for h in range(HALVES):
                        t = b * HALVES + h
                        p = claim(pe, TPB[t % 2], ("rwo", t), (x_ready, t + 1))
                        for c in range(DC):
                            ins = mm(p[:, 0:D], rw_z[:, c, h * P:(h + 1) * P], rw_w[:, 3, c, :],
                                     start=(c == 0), stop=(c == DC - 1))
                        ins.then_inc(full[TPB[t % 2]], 1)

                kvr(0)
                kvr(1)
                for b in range(B):
                    project(b)
                    if b + 2 < B:
                        kvr(b + 2)
                    if b >= 1 and eager_next(layer):
                        turn_pair(layer + 1, b - 1)

            def turn_pair(layer, b):
                for t in pair(b):
                    ln_T(layer, t)

            def moe0(layer):
                base = (0 if layer == MOE0 else 1) * TILES
                if layer == MOE0:
                    pe.wait_ge(w_in["moe0"], 32)

                def logits(t):
                    pe.wait_ge(xT_ready, layer * TILES + t + 1)
                    for c in range(DC):
                        ins = mm(bank[6][:, t * E0:(t + 1) * E0], xcols(t)[:, c, :], f0_wg[:, c, :],
                                 start=(c == 0), stop=(c == DC - 1))
                    if t == TILES - 1:
                        ins.then_inc(full[6], 1)

                def experts(t):
                    for pair in range(E0 // 2):
                        p = claim(pe, 2 + pair, ("ex0", base + t, pair), (m0["ex"], E0 * (base + t) + 2 * pair + 2))
                        for c in range(DC):
                            ins = mm(p[:, :], xcols(t)[:, c, :], f0_w[:, c, pair * 512:(pair + 1) * 512],
                                     start=(c == 0), stop=(c == DC - 1))
                        ins.then_inc(full[2 + pair], 1)

                r = base // TILES
                claim(pe, 6, ("lg0", r), (m0["lg"], r + 1))
                for t in range(EARLY_SEQ * HALVES):
                    logits(t)
                turn_pair(layer, B - 1)
                for t in pair(B - 1):
                    logits(t)
                experts(0)
                pe.wait_ge(m0["cmb"], r + 1)
                for k in range(2):
                    p = claim(pe, 6 + k, ("cmbT", r, k), (m0["cmbT"], 2 * r + k + 1))
                    for i in range(TILES // 2):
                        ins = nc.tensor.transpose(p[0:E0, i * P:(i + 1) * P], cmb[:, k * TILES // 2 + i, :], ident)
                    ins.then_inc(full[6 + k], 1)
                for t in range(TILES):
                    if t >= 1:
                        experts(t)
                    pe.wait_ge(m0["cmbT"], 2 * r + t // (TILES // 2) + 1)
                    bk = 6 + t % 2
                    p = claim(pe, bk, ("bias0", base + t), (x_ready, layer * TILES + t + 1))
                    mm(p[:, 0:D], cmbT[:, t, :], f0_b[:, :], start=True, stop=True).then_inc(full[bk], 1)
                    if t in (3, 5, 7) and eager_next(layer):
                        turn_pair(layer + 1, (t - 3) // 2)
                    if t in START and attention_next(layer):
                        attention(layer + 1, start=START[t])

            def mamba():
                layer = MAMBA
                pe.wait_ge(w_in["mamba"], 32)
                for t in range(EARLY_SEQ * HALVES):
                    dt_proj(layer, t)
                turn_pair(layer, B - 1)
                for t in pair(B - 1):
                    dt_proj(layer, t)
                for b in range(B):
                    xb_ = xT[:, :, b, 1:T + 1]
                    for i in range(3):
                        bk = 2 + 3 * (b % 2) + i
                        p = claim(pe, bk, ("conv", b, i), (ms["tap"], 3 * CHUNKS * b + 2 * CHUNKS + 2 * i + 2))
                        for j in range(2):
                            lo = ME + (2 * i + j) * P if i < 2 else 2 * ME + j * MN
                            m = P if i < 2 else MN
                            for c in range(DC):
                                ins = mm(p[0:m, j * T:(j + 1) * T], mb_in[:, c, lo:lo + m], xb_[:, c, :],
                                         start=(c == 0), stop=(c == DC - 1))
                        ins.then_inc(full[bk], 1)
                    for h in range(HALVES):
                        t = b * HALVES + h
                        p = claim(pe, TPB[h], ("gate", t), (ms["sg"], t + 1))
                        for c in range(DC):
                            ins = mm(p[:, :], xcols(t)[:, c, :], mb_in[:, c, 0:ME], start=(c == 0), stop=(c == DC - 1))
                        ins.then_inc(full[TPB[h]], 1)

                def head_work(t):
                    b, h = t // HALVES, t % HALVES
                    lo = h * P
                    pe.wait_ge(ms["cvs"], 2 * (b + 1))
                    p = claim(pe, TPB[0], ("htok", t), (ms["htok"], t + 1))
                    for c in range(MC):
                        ins = nc.tensor.transpose(p[:, c * P:(c + 1) * P], hs[:, c, b, lo:lo + P], ident)
                    ins.then_inc(full[TPB[0]], 1)
                    p = claim(pe, 2, ("gm", t), (ms["gm"], t + 1))
                    ins = mm(p[:, 0:P], bc[:, 0, b, lo:lo + P], bc[:, 1, b, lo:lo + P], start=True, stop=True)
                    ins.then_inc(full[2], 1)
                    pe.wait_ge(ms["ad"], 1)
                    if h == 0:
                        p = claim(pe, 7, ("btok", b), (ms["btok"], b + 1))
                        nc.tensor.transpose(p[:, 0:MN], bc[:, 0, b, lo:lo + P], ident[0:MN, 0:MN]).then_inc(full[7], 1)
                        p = claim(pe, 6, ("suf", b), (ms["esuf"], b + 1))
                        mm(p[:, 0:MH], tri_gt, a_d[:, t * MH:(t + 1) * MH], start=True, stop=True).then_inc(full[6], 1)
                    else:
                        p = claim(pe, 6, ("pre", b), (ms["epre"], b + 1))
                        mm(p[:, 0:MH], tri_le, a_d[:, t * MH:(t + 1) * MH], start=True, stop=True).then_inc(full[6], 1)
                    pe.wait_ge(ms["m1"], MH * (t + 1))
                    for q in range(2):
                        p = claim(pe, 3 + q, ("seg", t, q), (ms["L"], 2 * t + q + 1))
                        for i in range(4):
                            ins = mm(p[:, i * P:(i + 1) * P], m1[:, t % 2, 4 * q + i, :], tri_le, start=True, stop=True)
                        ins.then_inc(full[3 + q], 1)

                def outputs(t):
                    b, h = t // HALVES, t % HALVES
                    lo = h * P
                    if h == 0:
                        pe.wait_ge(ms["hdec"], b + 1)
                        pe.wait_ge(ms["btok"], b + 1)
                        p = claim(pe, 6, ("state", b), (ms["st"], b + 1))
                        mm(p[0:MN, :], btok, hdec, start=True, stop=True).then_inc(full[6], 1)
                    else:
                        pe.wait_ge(ms["st"], b + 1)
                        p = claim(pe, 6, ("yoff", b), (ms["y1"], b + 1))
                        mm(p[:, :], bc[:, 1, b, lo:lo + P], mst, start=True, stop=True).then_inc(full[6], 1)
                    p = claim(pe, 5, ("ydiag", t), (ms["y"], t + 1))
                    for i in range(MH):
                        pe.wait_ge(ms["mt"], MH * t + i + 1)
                        ins = mm(p[:, i * MP:(i + 1) * MP], mt[:, i, :], htok[:, t % 2, i * MP:(i + 1) * MP],
                                 start=True, stop=True)
                    ins.then_inc(full[5], 1)

                def turn_y(t):
                    pe.wait_ge(ms["yf"], t + 1)
                    p = claim(pe, TPB[1], ("yfT", t), (ms["yfT"], t + 1))
                    for c in range(MC):
                        ins = nc.tensor.transpose(p[:, c * P:(c + 1) * P], yf[:, c * P:(c + 1) * P], ident)
                    ins.then_inc(full[TPB[1]], 1)

                def project(t):
                    pe.wait_ge(ms["yfT"], t + 1)
                    p = claim(pe, 7, ("mbo", t), (x_ready, layer * TILES + t + 1))
                    for c in range(MC):
                        ins = mm(p[:, 0:D], yfT[:, c, :], mb_out[:, c, :], start=(c == 0), stop=(c == MC - 1))
                    ins.then_inc(full[7], 1)

                head_work(0)
                for t in range(TILES):
                    if t + 1 < TILES:
                        head_work(t + 1)
                    outputs(t)
                    if t >= 1:
                        project(t - 1)
                    turn_y(t)
                    if t in (3, 5, 7) and eager_next(layer):
                        turn_pair(layer + 1, (t - 3) // 2)
                project(TILES - 1)

            def dt_proj(layer, t):
                pe.wait_ge(xT_ready, layer * TILES + t + 1)
                if t == 0:
                    claim(pe, 7, ("dt",), (ms["dtr"], 1))
                for c in range(DC):
                    ins = mm(bank[7][:, t * MH:(t + 1) * MH], xcols(t)[:, c, :], mb_in[:, c, MPROJ - MH:MPROJ],
                             start=(c == 0), stop=(c == DC - 1))
                if t == TILES - 1:
                    ins.then_inc(full[7], 1)

            def attention(layer, start=None):
                r = (layer - ATTA) // 2
                if r == 0 and start == 0:
                    pe.wait_ge(w_in["att"], 64)
                    pe.wait_ge(prep, PREPS)
                SCORE, TURN = (2, 3, 4), (5, 6)
                K = QROWS + (AROWS if layer == ATTB else 0)

                def work(name, b, h, bk=0):
                    t = b * HALVES + h
                    n, m = layer * TILES + t, r * TILES + t
                    if name == "turn_x":
                        ln_T(layer, t, 0)
                        return
                    seq = r * B + b
                    if name == "keys":
                        pe.wait_ge(xT_ready, layer * TILES + (b + 1) * HALVES)
                        p = claim(pe, 0, ("k", seq), (as_["k"], seq + 1))
                        for c in range(DC):
                            ins = mm(p[0:NG * HD, 0:T], at_k[:, r, c, :], xT[:, c, b, 1:T + 1],
                                     start=(c == 0), stop=(c == DC - 1))
                    if name == "values":
                        p = claim(pe, 0, ("v", seq), (as_["v"], seq + 1))
                        for k in range(HALVES):
                            lo = k * NG * HD
                            for c in range(DC):
                                ins = mm(p[:, lo:lo + NG * HD], xcols(b * HALVES + k)[:, c, :], at_v[:, r, c, :],
                                         start=(c == 0), stop=(c == DC - 1))
                    if name == "queries":
                        p = claim(pe, 0, ("q", seq, h), (as_["q"], DC * seq + h + 1))
                        for c in range(DC):
                            ins = mm(p[:, 0:T], at_q[:, r, c, h * P:(h + 1) * P], xT[:, c, b, 1:T + 1],
                                     start=(c == 0), stop=(c == DC - 1))
                    if name == "turn_ctx":
                        pe.wait_ge(as_["ctx"], m + 1)
                        p = claim(pe, bk, ("ctxT", m), (as_["ctxT"], m + 1))
                        for c in range(DC):
                            ins = nc.tensor.transpose(p[:, c * P:(c + 1) * P], ctx_t[:, t % 2, c * P:(c + 1) * P], ident)
                    if name == "project":
                        pe.wait_ge(as_["ctxT"], m + 1)
                        p = claim(pe, bk, ("ato", m), (x_ready, n + 1))
                        for c in range(DC):
                            ins = mm(p[:, 0:D], ctxT[:, m % 2, c, :], at_o[:, r, c, :], start=(c == 0), stop=(c == DC - 1))
                    ins.then_inc(full[bk], 1)

                def group(i):
                    return i // NS if layer == ATTA else i % NG

                def scores(j):
                    b, i, n = j // HEADS, j % HEADS, r * B * HEADS + j
                    seq = r * B + b
                    if j == HEADS and r == 0:
                        pe.wait_ge(w_in["alibi"], 64)
                    if i == 0:
                        pe.wait_ge(qk_in, 16 * 2 * len(SLOTS_Q) * (seq + 1))
                    bk = SCORE[n % 3]
                    p = claim(pe, bk, ("score", n), (as_["exp"], n + 1))
                    q_, k_ = Qs[seq % 2][0:K, i, :], Ks[seq % 2][0:K, group(i), :]
                    mm(p[:, 0:P], q_[:, 0:P], k_[:, 0:P], start=True, stop=False)
                    mm(p[:, 0:P], ident_b[:, :], mask_b[:, :], start=False, stop=True)
                    mm(p[:, P:3 * P], q_[:, P:T], k_, start=True, stop=False)
                    mm(p[:, 2 * P:3 * P], ident_b[:, :], mask_b[:, :], start=False, stop=True).then_inc(full[bk], 1)

                def turn(j):
                    n = r * B * HEADS + j
                    pe.wait_ge(as_["exp"], n + 1)
                    bk = TURN[n % 2]
                    p = claim(pe, bk, ("turn", n), (as_["lo"], n + 1))
                    for c in range(3):
                        ins = nc.tensor.transpose(p[:, c * P:(c + 1) * P], pexp[:, n % 3, c * P:(c + 1) * P], ident)
                    ins.then_inc(full[bk], 1)

                def values(j):
                    b, i, n = j // HEADS, j % HEADS, r * B * HEADS + j
                    g, seq = group(i), r * B + b
                    pe.wait_ge(as_["lo"], n + 1)
                    if i == 0:
                        pe.wait_ge(as_["vparts"], seq + 1)
                        m = r * TILES + b * HALVES
                        claim(pe, 7, ("av", m), (as_["ctx"], m + 1))
                        claim(pe, 1, ("av", m + 1), (as_["ctx"], m + 2))
                    lo = i * VW
                    products = [(p_hi, l) for l in range(PARTS)] + [(p_lo, l) for l in range(PARTS - 1)]
                    for bk, halves in ((7, ((0, 0),)), (1, ((1, 0), (2, 1)))):
                        todo = [(w, l, c, h) for c, h in halves for w, l in products]
                        for k, (w, l, c, h) in enumerate(todo):
                            ins = mm(bank[bk][:, lo:lo + VW], w[:, n % 3, c * P:(c + 1) * P], vt[:, seq % 3, l, h * NG + g, :],
                                     start=(k == 0), stop=(k == len(todo) - 1))
                        if i == HEADS - 1:
                            ins.then_inc(full[bk], 1)

                if start is not None:
                    for i in sorted(NEXT):
                        work(NEXT[i][0], start, NEXT[i][1])
                    return
                scores(0)
                scores(1)
                for j in range(B * HEADS):
                    if j + 2 < B * HEADS:
                        scores(j + 2)
                    turn(j)
                    if j >= 2:
                        values(j - 2)
                    between(j // HEADS, j % HEADS, work)
                    if j // HEADS == B - 1 and j % HEADS in TURN_NEXT and moe_next(layer):
                        ln_T(layer + 1, TURN_NEXT[j % HEADS], 0)
                values(B * HEADS - 2)
                values(B * HEADS - 1)
                for name, h, bk in FINAL:
                    work(name, B - 1, h, bk)

            def moe1(layer):
                r = (layer - MOE1) // 2
                s = mo_s
                if r == 0:
                    pe.wait_ge(w_in["moe1"], 32)

                def logits(t):
                    pe.wait_ge(xT_ready, layer * TILES + t + 1)
                    n = r * TILES + t
                    p = claim(pe, 2 + t % 2, ("lg1", n), (s["lg"], n + 1))
                    for c in range(DC):
                        ins = mm(p[:, 0:E1], xcols(t)[:, c, :], rt_w[:, c, :], start=(c == 0), stop=(c == DC - 1))
                    ins.then_inc(full[2 + t % 2], 1)

                for t in range(EARLY_TILES):
                    logits(t)
                for t in range(EARLY_TILES, TILES):
                    ln_T(layer, t)
                    if t > EARLY_TILES:
                        logits(t - 1)
                logits(TILES - 1)
                p = claim(pe, 4, ("rnk", r), (s["rnk"], r + 1))
                q = claim(pe, 5, ("cnt", r), (s["cnt"], r + 1))
                pe.wait_ge(s["sel"], r + 1)
                for t in range(TILES):
                    for j in range(t + 1):
                        ins = mm(p[:, t * E1:(t + 1) * E1], tri_lt_b[:, :] if j == t else ones_b[:, :], sel[:, j, :],
                                 start=(j == 0), stop=(j == t))
                ins.then_inc(full[4], 1)
                for t in range(TILES):
                    ins = mm(q[:, 0:E1], ones_b[:, :], sel[:, t, :], start=(t == 0), stop=(t == TILES - 1))
                ins.then_inc(full[5], 1)
                p = claim(pe, 7, ("tok", r), (s["tok"], r + 1))
                for i in range(TILES * TOPK):
                    n = r * TILES * TOPK + i
                    pe.wait_ge(s["pair"], n + 1)
                    pe.wait_ge(s["row"] if i % 2 == 0 else s["row_odd"], n // 2 + 1)
                    ins = mm(p[:, 0:NBLK], at_row[:, i % PAIRS, :], at_blk[:, i % PAIRS, :],
                             start=(i == 0), stop=(i == TILES * TOPK - 1))
                    if i < TILES * TOPK - 1:
                        ins.then_inc(s["paired"], 1)
                ins.then_inc(full[7], 1)

                pe.wait_ge(s["blk"], r + 1)
                p = claim(pe, 6, ("blk", r), (s["blki"], 2 * r + 2))
                nc.tensor.transpose(p[0:1, 0:P], blk_e[:, :], ident).then_inc(full[6], 1)
                pe.wait_ge(s["blki"], 2 * r + 2)

                for k in range(8):
                    if free_at[k] is not None:
                        pe.wait_ge(*free_at[k])
                    free_at[k] = ((s["xbT"], s["h"], s["hT"], s["yb"])[k // 2], (r + 1) * NBLK)
                base = r * NBLK
                col_g, col_d = {}, {}

                def step(stage, m, c, first):
                    j, k = 4 * m + c, c % 2
                    if stage == TURN_X:
                        pe.wait_ge(xb_in[c % 4], (m + (c // 4 + 1 + r * NBLK // 4)) * 16)
                        if not first:
                            pe.wait_ge(s["xbT"], j + (base - 1))
                        for i in range(DC):
                            ins = nc.tensor.transpose(bank[k][:, i * P:(i + 1) * P], xb[:, c % 4, i * P:(i + 1) * P], ident)
                        ins.then_inc(s["turned"], 1)
                    if stage == FETCH:
                        word = nc.tensor.value_load(words[0:1, bass.ds(m + c // 4, 1)], min_val=0, max_val=2 ** (BITS * WORD) - 1)
                        for i in range(WORD):
                            e = (word >> BITS * i) & (E1 - 1)
                            if i < 4:
                                col_d[c + i] = nc.tensor.snap(e * D, min_val=0, max_val=(E1 - 1) * D)
                            if i >= 2 or first:
                                col_g[c + i] = nc.tensor.snap(e * (2 * FI), min_val=0, max_val=(E1 - 1) * 2 * FI)
                    if stage == GATE_UP:
                        e = col_g[c]
                        pe.wait_ge(s["xbT"], j + (base + 1))
                        if not first:
                            pe.wait_ge(s["h"], j + (base - 1))
                        for i in range(DC):
                            ins = mm(bank[2 + k][:, 0:2 * FI], xbT[:, k, i, :], gu_w[:, i, bass.ds(e, 2 * FI)],
                                     start=(i == 0), stop=(i == DC - 1))
                        ins.then_inc(s["gu"], 1)
                    if stage == TURN_H:
                        pe.wait_ge(s["h"], j + (base + 1))
                        if not first:
                            pe.wait_ge(s["hT"], j + (base - 1))
                        nc.tensor.transpose(bank[4 + k][0:FI, 0:P], hh[:, k, :], ident).then_inc(s["hturned"], 1)
                    if stage == DOWN:
                        e = col_d[c]
                        pe.wait_ge(s["hT"], j + (base + 1))
                        if not first:
                            pe.wait_ge(s["yb"], j + (base - 1))
                        mm(bank[6 + k][:, 0:D], hT[:, k, :], dn_w[:, bass.ds(e, D)],
                           start=True, stop=True).then_inc(s["down"], 1)

                over_blocks(pe, step)
                if attention_next(layer):
                    for b in range(AHEAD_SEQ):
                        attention(layer + 1, start=b)

            run = {RWKV: rwkv, MAMBA: mamba}
            for layer in range(LAYERS):
                if layer in (MOE0, MOE0B):
                    moe0(layer)
                elif layer in (ATTA, ATTB):
                    attention(layer)
                elif layer in (MOE1, MOE1B):
                    moe1(layer)
                else:
                    run[layer]()

        @block.scalar
        def _(act):
            steps = Steps(act, act_step)

            def xT_copy(layer, t):
                n = layer * TILES + t
                act.wait_ge(*filled(("xT", n)))
                b = t // HALVES
                nc.scalar.activation(xcols(t), filled_bank(("xT", n))[:, 0:D].rearrange("p (c n) -> p c n", c=DC),
                                     ACT.Copy).then_inc(xT_ready, 1)

            def rwkv():
                for t in range(TILES):
                    xT_copy(RWKV, t)
                for b in range(B):
                    act.wait_ge(rs["mix"], MIXES * b + DC)
                    nc.scalar.activation(mix[2][:, :, b, :], mix[2][:, :, b, :], ACT.Silu).then_inc(rs["silu"], 1)
                def exps(b):
                    k = b % 2
                    act.wait_ge(rs["td"], b + 1)
                    if b >= 2:
                        act.wait_ge(rs["ab"], b - 1)
                    nc.scalar.activation(rw_e2[k], rw_d[k], ACT.Exp)
                    for c in range(DC):
                        ins = nc.scalar.activation(rw_e1[k][:, c, :], rw_t[k][:, c, :], ACT.Exp, bias=negw[:, c:c + 1], scale=-1.0)
                    ins.then_inc(rs["exp"], 1)

                exps(0)
                for b in range(B):
                    if b + 1 < B:
                        exps(b + 1)
                    if b >= 1 and eager_next(RWKV):
                        for t in pair(b - 1):
                            xT_copy(RWKV + 1, t)

            def moe0(layer):
                base = (0 if layer == MOE0 else 1) * TILES

                r = base // TILES
                for t in pair(B - 1):
                    xT_copy(layer, t)
                act.wait_ge(*filled(("lg0", r)))
                nc.scalar.activation(lg0[:, :, :], filled_bank(("lg0", r))[:, 0:TILES * E0].rearrange("p (t e) -> p t e", e=E0),
                                     ACT.Copy).then_inc(m0["lg"], 1)
                act.wait_ge(m0["nmx"], r + 1)
                for t in range(TILES):
                    ins = nc.scalar.activation(ex0[:, t, :], lg0[:, t, :], ACT.Exp, bias=nmx0[:, t:t + 1],
                                               accum_out=sum0[:, t:t + 1])
                ins.then_inc(m0["sum"], 1)
                for k in range(2):
                    act.wait_ge(*filled(("cmbT", r, k)))
                    half = slice(k * TILES // 2, (k + 1) * TILES // 2)
                    nc.scalar.activation(cmbT[:, half, :],
                                         filled_bank(("cmbT", r, k))[0:E0, :].rearrange("p (t n) -> p t n", n=P),
                                         ACT.Copy).then_inc(m0["cmbT"], 1)
                if eager_next(layer):
                    for t in range(EARLY_SEQ * HALVES):
                        xT_copy(layer + 1, t)
                if attention_next(layer):
                    for b in range(AHEAD_SEQ):
                        attention(layer + 1, start=b)

            def mamba():
                layer = MAMBA
                nc.scalar.activation(a_row, a_log, ACT.Exp).then_inc(ms["dtneg"], 1)
                for t in pair(B - 1):
                    xT_copy(layer, t)
                act.wait_ge(ms["spu"], 1)
                nc.scalar.activation(sp_e, sp_neg, ACT.Exp).then_inc(ms["spe"], 1)
                act.wait_ge(ms["spu"], 2)
                nc.scalar.activation(sp_l, sp_u, ACT.Ln).then_inc(ms["spl"], 1)

                def conv(b):
                    for i in range(3):
                        act.wait_ge(*filled(("conv", b, i)))
                        if i == 0 and b >= 2:
                            act.wait_ge(ms["cvs"], 2 * (b - 1))
                        n = P if i < 2 else MN
                        for j in range(2):
                            ch = 2 * i + j
                            nc.scalar.activation(hcv[0:n, b % 2, ch, :], filled_bank(("conv", b, i))[0:n, j * T:(j + 1) * T],
                                                 ACT.Identity, bias=mb_conv[0:n, ch, TAPS:TAPS + 1],
                                                 scale=mb_conv[0:n, ch, TAPS - 1:TAPS]).then_inc(ms["cv"], 1)

                def convolved(b):
                    act.wait_ge(ms["tap"], 3 * CHUNKS * (b + 1))
                    nc.scalar.activation(hs[:, :, b, :], hcv[:, b % 2, 0:MC, :], ACT.Silu).then_inc(ms["cvs"], 1)
                    nc.scalar.activation(bc[:, :, b, :], hcv[0:MN, b % 2, MC:CHUNKS, :], ACT.Silu).then_inc(ms["cvs"], 1)

                def gates(b):
                    for h in range(HALVES):
                        t = b * HALVES + h
                        act.wait_ge(*filled(("gate", t)))
                        nc.scalar.activation(sg[:, t, :], filled_bank(("gate", t))[:, :], ACT.Silu).then_inc(ms["sg"], 1)

                for b in range(B):
                    conv(b)
                    gates(b)
                    if b >= 1:
                        convolved(b - 1)
                convolved(B - 1)

                def head_work(t):
                    b, h = t // HALVES, t % HALVES
                    act.wait_ge(*filled(("htok", t)))
                    if t >= 2:
                        act.wait_ge(*filled(("ydiag", t - 2)))
                        act.wait_ge(ms["dh"], t - 1)
                        act.wait_ge(ms["hdec"], (t - 2) // 2 + 1)
                    nc.scalar.activation(htok[:, t % 2, :], filled_bank(("htok", t))[:, :], ACT.Copy).then_inc(ms["htok"], 1)
                    if h == 0:
                        act.wait_ge(*filled(("btok", b)))
                        if b >= 1:
                            act.wait_ge(*filled(("state", b - 1)))
                        nc.scalar.activation(btok, filled_bank(("btok", b))[:, 0:MN], ACT.Copy).then_inc(ms["btok"], 1)
                        act.wait_ge(*filled(("suf", b)))
                        if b >= 1:
                            act.wait_ge(ms["dsc"], b)
                        nc.scalar.activation(esuf, filled_bank(("suf", b))[:, 0:MH], ACT.Exp).then_inc(ms["esuf"], 1)
                    else:
                        act.wait_ge(*filled(("pre", b)))
                        if b >= 1:
                            act.wait_ge(ms["y1"], b)
                        nc.scalar.activation(epre, filled_bank(("pre", b))[:, 0:MH], ACT.Exp).then_inc(ms["epre"], 1)
                    for q in range(2):
                        act.wait_ge(*filled(("seg", t, q)))
                        if t >= 1:
                            act.wait_ge(ms["mt"], MH * (t - 1) + 4 * q + 4)
                        nc.scalar.activation(Lx[:, 4 * q:4 * q + 4, :],
                                             filled_bank(("seg", t, q))[:, :].rearrange("p (i n) -> p i n", i=4),
                                             ACT.Exp).then_inc(ms["L"], 1)

                head_work(0)
                for t in range(TILES):
                    b, h = t // HALVES, t % HALVES
                    if t + 1 < TILES:
                        head_work(t + 1)
                    if h == 0:
                        act.wait_ge(*filled(("state", b)))
                        if b >= 1:
                            act.wait_ge(*filled(("yoff", b - 1)))
                        nc.scalar.activation(mst, filled_bank(("state", b))[0:MN, :], ACT.Copy).then_inc(ms["st"], 1)
                    act.wait_ge(ms["yf"], t + 1)
                    if t >= 1:
                        steps.after(steps.n)
                    ins = nc.scalar.activation(ysq, yf, ACT.Square, accum_out=mss[:, t:t + 1])
                    steps.mark(ins)
                    if t in (3, 5, 7) and eager_next(layer):
                        for k in pair((t - 3) // 2):
                            xT_copy(layer + 1, k)

            def attention(layer, start=None):
                r = (layer - ATTA) // 2

                def work(name, b, h, bk=0):
                    t = b * HALVES + h
                    seq, m = r * B + b, r * TILES + t
                    if name == "turn_x":
                        xT_copy(layer, t)
                    if name == "keys":
                        act.wait_ge(*filled(("k", seq)))
                        if seq >= 1:
                            act.wait_ge(as_["kparts"], seq)
                        nc.scalar.activation(qkf[0:NG * HD, DC * T:QK], filled_bank(("k", seq))[0:NG * HD, 0:T],
                                             ACT.Copy).then_inc(as_["k"], 1)
                    if name == "values":
                        act.wait_ge(*filled(("v", seq)))
                        if seq >= 1:
                            act.wait_ge(as_["vparts"], seq)
                        nc.scalar.activation(vf, filled_bank(("v", seq))[:, 0:HALVES * NG * HD], ACT.Copy).then_inc(as_["v"], 1)
                    if name == "queries":
                        act.wait_ge(*filled(("q", seq, h)))
                        if seq >= 1:
                            act.wait_ge(as_["qparts"], DC * (seq - 1) + h + 1)
                        nc.scalar.activation(qkf[:, h * T:(h + 1) * T], filled_bank(("q", seq, h))[:, 0:T], ACT.Copy,
                                             scale=HD ** -0.5).then_inc(as_["q"], 1)
                    if name == "turn_ctx":
                        act.wait_ge(*filled(("ctxT", m)))
                        if m >= 2:
                            act.wait_ge(*filled(("ato", m - 2)))
                        nc.scalar.activation(ctxT[:, m % 2], filled_bank(("ctxT", m))[:, 0:D].rearrange("p (c n) -> p c n", c=DC),
                                             ACT.Copy).then_inc(as_["ctxT"], 1)

                def exps(j):
                    n = r * B * HEADS + j
                    act.wait_ge(as_["nmax"], 2 * (n + 1))
                    if n >= 3:
                        act.wait_ge(*filled(("turn", n - 3)))
                    p = filled_bank(("score", n))
                    nc.scalar.activation(pexp[:, n % 3, 0:P], p[:, 0:P], ACT.Exp, bias=nmax[:, n % 4, 0:1])
                    nc.scalar.activation(pexp[:, n % 3, P:3 * P], p[:, P:3 * P], ACT.Exp,
                                         bias=nmax[:, n % 4, 1:2]).then_inc(as_["exp"], 1)

                def high(j):
                    n = r * B * HEADS + j
                    act.wait_ge(*filled(("turn", n)))
                    if n >= 3:
                        act.wait_ge(as_["lo"], n - 2)
                    nc.scalar.activation(p_hi[:, n % 3, :], filled_bank(("turn", n))[:, 0:3 * P], ACT.Copy,
                                         scale=P_SCALE).then_inc(as_["hi"], 1)

                if start is not None:
                    for i in sorted(NEXT):
                        work(NEXT[i][0], start, NEXT[i][1])
                    return
                exps(0)
                for j in range(B * HEADS):
                    if j + 1 < B * HEADS:
                        exps(j + 1)
                    high(j)
                    between(j // HEADS, j % HEADS, work)
                    if j // HEADS == B - 1 and j % HEADS in TURN_NEXT and moe_next(layer):
                        xT_copy(layer + 1, TURN_NEXT[j % HEADS])
                for name, h, bk in FINAL:
                    work(name, B - 1, h, bk)

            def moe1(layer):
                r = (layer - MOE1) // 2
                s = mo_s
                def logits(t):
                    n = r * TILES + t
                    act.wait_ge(*filled(("lg1", n)))
                    nc.scalar.activation(lg1[:, t, :], filled_bank(("lg1", n))[:, 0:E1], ACT.Copy).then_inc(s["lg"], 1)

                for t in range(EARLY_TILES):
                    logits(t)
                for t in range(EARLY_TILES, TILES):
                    xT_copy(layer, t)
                    if t > EARLY_TILES:
                        logits(t - 1)
                logits(TILES - 1)
                act.wait_ge(s["nmx"], r + 1)
                for t in range(TILES):
                    nc.scalar.activation(wts[:, t, :], mx1[:, t, 0:TOPK], ACT.Exp, bias=nmx1[:, t:t + 1],
                                         accum_out=wsum[:, t:t + 1]).then_inc(s["exw"], 1)
                base = r * NBLK

                def step(stage, m, c, first):
                    j, k = 4 * m + c, c % 2
                    if stage == TURN_X:
                        act.wait_ge(s["turned"], j + (base + 1))
                        if not first:
                            act.wait_ge(s["gu"], j + (base - 1))
                        nc.scalar.activation(xbT[:, k, :, :], bank[k][:, 0:D].rearrange("p (c n) -> p c n", c=DC),
                                             ACT.Copy).then_inc(s["xbT"], 1)
                    if stage == GATE_UP:
                        act.wait_ge(s["gu"], j + (base + 1))
                        if not first:
                            act.wait_ge(s["h"], j + (base - 1))
                        nc.scalar.activation(sgt[:, k, :], bank[2 + k][:, 0:FI], ACT.Silu).then_inc(s["sg"], 1)
                    if stage == TURN_H:
                        act.wait_ge(s["hturned"], j + (base + 1))
                        if not first:
                            act.wait_ge(s["down"], j + (base - 1))
                        nc.scalar.activation(hT[:, k, :], bank[4 + k][0:FI, 0:P], ACT.Copy).then_inc(s["hT"], 1)

                over_blocks(act, step)
                if attention_next(layer):
                    for b in range(AHEAD_SEQ):
                        attention(layer + 1, start=b)

            for layer in range(LAYERS):
                if layer in (MOE0, MOE0B):
                    moe0(layer)
                elif layer in (ATTA, ATTB):
                    attention(layer)
                elif layer in (MOE1, MOE1B):
                    moe1(layer)
                else:
                    {RWKV: rwkv, MAMBA: mamba}[layer]()

        @block.vector
        def _(dve):
            V = nc.vector
            steps = Steps(dve, dve_step)

            def ln_stats(layer, tiles):
                n = layer * TILES + tiles[0]
                k = slice(n % 8, n % 8 + len(tiles))
                for t in tiles:
                    if layer == 0:
                        dve.wait_ge(x_in[t], 16)
                    else:
                        dve.wait_ge(x_ready, (layer - 1) * TILES + t + 1)
                    steps.mark(V.bn_stats(st6[:, t % 8, :], X[:, t, :]))
                steps.after(steps.n)
                for t in tiles:
                    steps.mark(V.bn_aggr(mv[:, t % 8, :], st6[:, t % 8, :]))
                steps.after(steps.n)
                V.tensor_scalar(ve[:, k], mv[:, k, 1], LN_EPS, None, ALU.add).then_inc(ln_var, len(tiles))

            def ln_norm(layer, tiles):
                dve.wait_ge(ln_rstd, layer * TILES + tiles[-1] + 1)
                for t in tiles:
                    V.tensor_scalar(xn[:, t, :], X[:, t, :], mv[:, t % 8, 0:1], rstd[:, t % 8:t % 8 + 1],
                                    ALU.subtract, ALU.mult).then_inc(ln_done, 1)

            def ln(layer, tiles):
                ln_stats(layer, tiles)
                ln_norm(layer, tiles)

            def rwkv():
                for b in range(B):
                    ln(RWKV, pair(b))
                dve.wait_ge(w_in["small"], 16 * SMALLS)
                V.tensor_scalar(negw[:, :], w_c, -1.0, None, ALU.mult).then_inc(rs["col"], 1)
                V.tensor_tensor(ubk[:, :], u_c, wk_c, ALU.add).then_inc(rs["col"], 1)

                def mixes(b):
                    dve.wait_ge(rs["diff"], b + 1)
                    for i, m in enumerate((tmr, tmk, tmv)):
                        for c in range(DC):
                            V.scalar_tensor_tensor(mix[(2, 0, 1)[i]][:, c, b, :], rw_diff[:, b % 2, c, :], m[:, c:c + 1],
                                                   xT[:, c, b, 0:T], ALU.mult, ALU.add).then_inc(rs["mix"], 1)

                def exponents(b):
                    dve.wait_ge(*filled(("kvr", b, 0)))
                    k_, k = filled_bank(("kvr", b, 0)), b % 2
                    if b >= 2:
                        dve.wait_ge(rs["exp"], b - 1)
                    if b == 0:
                        dve.wait_ge(rs["col"], 2)
                    for c in range(DC):
                        steps.mark(V.tensor_scalar(rw_t[k][:, c, :], k_[:, c * T:(c + 1) * T], ubk[:, c:c + 1], w_c[:, c:c + 1],
                                                   ALU.add, ALU.max))
                    steps.after(steps.n)
                    for c in range(DC):
                        ins = V.scalar_tensor_tensor(rw_d[k][:, c, :], k_[:, c * T:(c + 1) * T], ubk[:, c:c + 1], rw_t[k][:, c, :],
                                                     ALU.add, ALU.subtract)
                    ins.then_inc(rs["td"], 1)

                def recurrence(b):
                    k = b % 2
                    dve.wait_ge(rs["exp"], b + 1)
                    dve.wait_ge(*filled(("kvr", b, 1)))
                    if b >= 1:
                        dve.wait_ge(rs["ab"], b)
                    v_ = filled_bank(("kvr", b, 1))
                    for c in range(DC):
                        steps.mark(V.scalar_tensor_tensor(rw_ev[:, c, :], v_[:, c * T:(c + 1) * T], wv_c[:, c:c + 1],
                                                          rw_e2[k][:, c, :], ALU.add, ALU.mult))
                    if b >= 2:
                        dve.wait_ge(rs["q"], b - 1)
                    for c in range(DC):
                        steps.mark(V.tensor_tensor_scan(rw_b[k][:, c, :], rw_e1[k][:, c, :], rw_e2[k][:, c, :], 0.0,
                                                        ALU.mult, ALU.add))
                    steps.after(steps.n)
                    for c in range(DC):
                        ins = V.tensor_tensor_scan(rw_a[k][:, c, :], rw_e1[k][:, c, :], rw_ev[:, c, :], 0.0, ALU.mult, ALU.add)
                    ins.then_inc(rs["ab"], 1)
                    V.reciprocal(rw_b[k], rw_b[k]).then_inc(rs["rb"], 1)

                def receptance(b):
                    dve.wait_ge(*filled(("kvr", b, 2)))
                    if b >= 1:
                        dve.wait_ge(*filled(("rwo", b * HALVES - 1)))
                    r_ = filled_bank(("kvr", b, 2))
                    dve.wait_ge(rs["q"], b + 1)
                    for c in range(DC):
                        ins = V.scalar_tensor_tensor(rw_z[:, c, :], r_[:, c * T:(c + 1) * T], wr_c[:, c:c + 1],
                                                     rw_q[:, c, :], ALU.add, ALU.mult)
                    ins.then_inc(rs["z"], 1)

                def residual(b):
                    for h in range(HALVES):
                        t = b * HALVES + h
                        dve.wait_ge(*filled(("rwo", t)))
                        dve.wait_ge(xb_ready, t + 1)
                        V.tensor_tensor(X[:, t, :], filled_bank(("rwo", t))[:, 0:D], X[:, t, :], ALU.add).then_inc(x_ready, 1)

                for b in range(B):
                    mixes(b)
                exponents(0)
                for b in range(B):
                    recurrence(b)
                    if b + 1 < B:
                        exponents(b + 1)
                    if b >= 1:
                        residual(b - 1)
                        if eager_next(RWKV):
                            ln(RWKV + 1, pair(b - 1))
                    receptance(b)
                residual(B - 1)

            def moe0(layer):
                base = (0 if layer == MOE0 else 1) * TILES

                r = base // TILES
                ln(layer, pair(B - 1))
                dve.wait_ge(m0["lg"], r + 1)
                for t in range(TILES):
                    steps.mark(V.max(mx0[:, t, :], lg0[:, t, :]))
                steps.after(steps.n)
                V.tensor_scalar(nmx0[:, :], mx0[:, :, 0], -1.0, None, ALU.mult).then_inc(m0["nmx"], 1)
                for t in range(TILES):
                    steps.mark(V.max_index(ix0[:, t, :], mx0[:, t, :], lg0[:, t, :]))
                steps.after(steps.n)
                steps.link(V.tensor_copy(idx0[:, :], ix0[:, :, 0]))
                steps.mark(V.tensor_tensor(cmb[:, :, :], iota_row[:, 0:E0].unsqueeze(1).to_broadcast([P, TILES, E0]),
                                           idx0[:, :].unsqueeze(2).to_broadcast([P, TILES, E0]), ALU.is_equal))
                dve.wait_ge(m0["sum"], r + 1)
                steps.link(V.reciprocal(gate0[:, :], sum0[:, :]))
                V.tensor_tensor(cmb[:, :, :], cmb[:, :, :], gate0[:, :].unsqueeze(2).to_broadcast([P, TILES, E0]),
                                ALU.mult).then_inc(m0["cmb"], 1)
                dve.wait_ge(m0["cmb"], r + 1)
                for t in range(TILES):
                    n = base + t
                    if n >= 1:
                        dve.wait_ge(x_ready, layer * TILES + t)
                    for e in range(E0):
                        dve.wait_ge(*filled(("ex0", n, e // 2)))
                        src = filled_bank(("ex0", n, e // 2))[:, (e % 2) * D:(e % 2 + 1) * D]
                        if e == 1:
                            ins = V.tensor_scalar(acc[:, 1, :], src, cmb[:, t, e:e + 1], None, ALU.mult)
                        else:
                            if e:
                                dve.wait_ge(m0["ex"], E0 * n + e - 1)
                            ins = V.scalar_tensor_tensor(acc[:, e % 2, :], src, cmb[:, t, e:e + 1],
                                                         acc[:, e % 2, :] if e else X[:, t, :], ALU.mult, ALU.add)
                        ins.then_inc(m0["ex"], 1)
                    dve.wait_ge(*filled(("bias0", n)))
                    dve.wait_ge(m0["ex"], E0 * (n + 1))
                    steps.link(V.tensor_tensor(acc[:, 0, :], filled_bank(("bias0", n))[:, 0:D], acc[:, 0, :], ALU.add))
                    V.tensor_tensor(X[:, t, :], acc[:, 0, :], acc[:, 1, :], ALU.add).then_inc(x_ready, 1)
                    if t in (1, 3, 5) and eager_next(layer):
                        ln(layer + 1, pair(t // 2))
                    if t == 4 and attention_next(layer):
                        ln(layer + 1, range(AHEAD_SEQ * HALVES))
                    if t == TILES - 2 and attention_next(layer):
                        attention(layer + 1, start=0)

            def mamba():
                layer = MAMBA
                ln(layer, pair(B - 1))
                heads = "p (t h) -> p t h"
                dve.wait_ge(*filled(("dt",)))
                V.tensor_tensor(dtr.rearrange(heads, h=MH), filled_bank(("dt",))[:, 0:TILES * MH].rearrange(heads, h=MH),
                                dt_bias.unsqueeze(1).to_broadcast([P, TILES, MH]), ALU.add).then_inc(ms["dtr"], 1)
                dve.wait_ge(ms["dtr"], 1)
                V.scalar_tensor_tensor(sp_neg, dtr, -1.0, dtr, ALU.mult, ALU.min).then_inc(ms["spu"], 1)
                dve.wait_ge(ms["spe"], 1)
                V.tensor_scalar(sp_u, sp_e, 1.0, None, ALU.add).then_inc(ms["spu"], 1)
                dve.wait_ge(ms["spu"], 2)
                steps.link(V.tensor_scalar(sp_d, sp_u, -1.0, None, ALU.add))
                steps.link(V.tensor_scalar(sp_mask, sp_d, 0.0, None, ALU.is_equal))
                steps.link(V.tensor_tensor(sp_d, sp_d, sp_mask, ALU.add))
                steps.link(V.reciprocal(sp_q, sp_d))
                dve.wait_ge(ms["spl"], 1)
                steps.link(V.tensor_tensor(sp_q, sp_q, sp_l, ALU.mult))
                steps.link(V.tensor_tensor(sp_q, sp_q, sp_mask, ALU.add))
                steps.link(V.tensor_tensor(sp_q, sp_q, sp_e, ALU.mult))
                steps.link(V.scalar_tensor_tensor(dt, dtr, 0.0, sp_q, ALU.max, ALU.add))
                dve.wait_ge(ms["dtneg"], 1)
                V.scalar_tensor_tensor(a_d.rearrange(heads, h=MH), dt.rearrange(heads, h=MH), -1.0,
                                       a_row[:, :].unsqueeze(1).to_broadcast([P, TILES, MH]),
                                       ALU.mult, ALU.mult).then_inc(ms["ad"], 1)
                for b in range(B):
                    for k in range(TAPS - 1):
                        sh = k + 1
                        for ch in range(CHUNKS):
                            n = P if ch < MC else MN
                            if k == 0:
                                dve.wait_ge(ms["cv"], CHUNKS * b + ch // 2 * 2 + 2)
                            else:
                                dve.wait_ge(ms["tap"], 3 * CHUNKS * b + CHUNKS * (k - 1) + ch + 1)
                            src = filled_bank(("conv", b, ch // 2))[0:n, (ch % 2) * T:(ch % 2 + 1) * T - sh]
                            V.scalar_tensor_tensor(hcv[0:n, b % 2, ch, sh:T], src,
                                                   mb_conv[0:n, ch, TAPS - 1 - sh:TAPS - sh], hcv[0:n, b % 2, ch, sh:T],
                                                   ALU.mult, ALU.add).then_inc(ms["tap"], 1)

                def turned(t):
                    dve.wait_ge(*filled(("yfT", t)))
                    if t >= 1:
                        dve.wait_ge(*filled(("mbo", t - 1)))
                    V.tensor_tensor(yfT, filled_bank(("yfT", t))[:, :].rearrange("p (c n) -> p c n", c=MC),
                                    mb_norm[:, :].unsqueeze(2).to_broadcast([P, MC, P]), ALU.mult).then_inc(ms["yfT"], 1)

                def residual(t):
                    dve.wait_ge(ms["rs"], t + 1)
                    dve.wait_ge(*filled(("mbo", t)))
                    V.scalar_tensor_tensor(X[:, t, :], filled_bank(("mbo", t))[:, 0:D], mrs[:, t:t + 1], X[:, t, :],
                                           ALU.mult, ALU.add).then_inc(x_ready, 1)

                wide = "p (h n) -> p h n"
                def mixing(t):
                    b, h = t // HALVES, t % HALVES
                    dve.wait_ge(*filled(("gm", t)))
                    if t >= 1:
                        dve.wait_ge(ms["mt"], MH * t)
                    V.tensor_tensor(gm, filled_bank(("gm", t))[:, 0:P], tri_le, ALU.mult).then_inc(ms["gm"], 1)
                    if h == 0:
                        dve.wait_ge(ms["esuf"], b + 1)
                        if b >= 1:
                            dve.wait_ge(ms["hdec"], b)
                        V.tensor_tensor(dsc[:, :], esuf[:, :], dt[:, t * MH:(t + 1) * MH], ALU.mult).then_inc(ms["dsc"], 1)
                    dve.wait_ge(ms["gm"], t + 1)
                    if t >= 1:
                        dve.wait_ge(*filled(("ydiag", t - 1)))
                    for i in range(MH):
                        if i % 4 == 0:
                            dve.wait_ge(ms["L"], 2 * t + i // 4 + 1)
                        V.scalar_tensor_tensor(mt[:, i, :], Lx[:, i, :], dt[:, t * MH + i:t * MH + i + 1], gm,
                                               ALU.mult, ALU.mult).then_inc(ms["mt"], 1)

                mixing(0)
                for t in range(TILES):
                    b, h = t // HALVES, t % HALVES
                    dve.wait_ge(*filled(("ydiag", t)))
                    dve.wait_ge(ms["dh"], t + 1)
                    if t >= 1:
                        dve.wait_ge(*filled(("yfT", t - 1)))
                        dve.wait_ge(act_step, t)
                    yd = filled_bank(("ydiag", t))
                    V.tensor_tensor(yf, yd[:, :], dh, ALU.add).then_inc(ms["y"], 1)
                    dve.wait_ge(ms["y"], t + 1)
                    if h == 1:
                        dve.wait_ge(*filled(("yoff", b)))
                        dve.wait_ge(ms["epre"], b + 1)
                        V.tensor_tensor(y1.rearrange(wide, h=MH), filled_bank(("yoff", b))[:, :].rearrange(wide, h=MH),
                                        epre[:, :].unsqueeze(2).to_broadcast([P, MH, MP]), ALU.mult).then_inc(ms["y1"], 1)
                        dve.wait_ge(ms["y1"], b + 1)
                        steps.link(V.tensor_tensor(yf, yf, y1, ALU.add))
                    dve.wait_ge(ms["sg"], t + 1)
                    V.tensor_tensor(yf, yf, sg[:, t, :], ALU.mult).then_inc(ms["yf"], 1)
                    if t + 1 < TILES:
                        mixing(t + 1)
                    turned(t)
                    if t >= 1:
                        residual(t - 1)
                    if t in (2, 4, 6) and eager_next(layer):
                        ln(layer + 1, pair((t - 2) // 2))
                residual(TILES - 1)

            def attention(layer, start=None):
                r = (layer - ATTA) // 2

                def work(name, b, h, bk=0):
                    if name == "project":
                        t = b * HALVES + h
                        m = r * TILES + t
                        dve.wait_ge(*filled(("ato", m)))
                        dve.wait_ge(xb_ready, BIASED[layer] * TILES + t + 1)
                        V.tensor_tensor(X[:, t, :], filled_bank(("ato", m))[:, 0:D], X[:, t, :], ALU.add).then_inc(x_ready, 1)

                def maxima(j):
                    n = r * B * HEADS + j
                    dve.wait_ge(*filled(("score", n)))
                    if n >= 4:
                        dve.wait_ge(as_["exp"], n - 3)
                    p = filled_bank(("score", n))
                    V.tensor_reduce(nmax[:, n % 4, 0:1], p[:, 0:P], AX_X, ALU.max, negate=True).then_inc(as_["nmax"], 1)
                    V.tensor_reduce(nmax[:, n % 4, 1:2], p[:, P:3 * P], AX_X, ALU.max, negate=True).then_inc(as_["nmax"], 1)

                def low(j):
                    n = r * B * HEADS + j
                    dve.wait_ge(as_["hi"], n + 1)
                    V.scalar_tensor_tensor(p_lo[:, n % 3, :], filled_bank(("turn", n))[:, 0:3 * P], P_SCALE, p_hi[:, n % 3, :],
                                           ALU.mult, ALU.subtract).then_inc(as_["lo"], 1)

                def context(b):
                    for h in range(HALVES):
                        t = b * HALVES + h
                        m = r * TILES + t
                        dve.wait_ge(*filled(("av", m)))
                        av = filled_bank(("av", m))[:, 0:HEADS * VW].rearrange("p (i d) -> p i d", d=VW)
                        if m >= 1:
                            dve.wait_ge(as_["ctx"], m)
                        steps.link(V.reciprocal(rsum.unsqueeze(2), av[:, :, HD:VW]))
                        if m >= 2:
                            dve.wait_ge(*filled(("ctxT", m - 2)))
                        V.tensor_tensor(ctx_t[:, t % 2, :].rearrange("p (i d) -> p i d", d=HD), av[:, :, 0:HD],
                                        rsum.unsqueeze(2).to_broadcast([P, HEADS, HD]), ALU.mult).then_inc(as_["ctx"], 1)

                if start is not None:
                    split(dve, V, steps, r, start)
                    return
                maxima(0)
                maxima(1)
                for j in range(B * HEADS):
                    b, i = j // HEADS, j % HEADS
                    if j + 2 < B * HEADS:
                        maxima(j + 2)
                    if i == 2 and b >= 1:
                        context(b - 1)
                    low(j)
                    between(b, i, work)
                    if layer == ATTB and b == 0 and i in COMBINE:
                        combine(MOE1, COMBINE[i])
                    if b + AHEAD_SEQ < B and i == STATS:
                        ln_stats(layer, pair(b + AHEAD_SEQ))
                    if b + AHEAD_SEQ < B and i == NORM:
                        ln_norm(layer, pair(b + AHEAD_SEQ))
                    if b == B - 1 and i == STATS and moe_next(layer):
                        ln_stats(layer + 1, range(EARLY_TILES))
                    if b == B - 1 and i == NORM and moe_next(layer):
                        ln_norm(layer + 1, range(EARLY_TILES))
                context(B - 1)
                for name, h, bk in FINAL:
                    work(name, B - 1, h, bk)

            def moe1(layer):
                r = (layer - MOE1) // 2
                s = mo_s
                ln(layer, range(EARLY_TILES, TILES))
                for t in range(TILES):
                    dve.wait_ge(s["lg"], r * TILES + t + 1)
                    steps.mark(V.max(mx1[:, t, :], lg1[:, t, :]))
                steps.after(steps.n)
                V.tensor_scalar(nmx1[:, :], mx1[:, :, 0], -1.0, None, ALU.mult).then_inc(s["nmx"], 1)
                for t in range(TILES):
                    steps.mark(V.max_index(ix1[:, t, :], mx1[:, t, :], lg1[:, t, :]))
                steps.after(steps.n)
                steps.link(V.tensor_copy(ixf[:, :, :], ix1[:, :, 0:TOPK]))
                steps.link(V.tensor_tensor(oh.rearrange("p t k e -> p (t k) e"),
                                           iota_row.unsqueeze(1).to_broadcast([P, TILES * TOPK, E1]),
                                           ixf[:, :, :].rearrange("p t k -> p (t k)").unsqueeze(2).to_broadcast([P, TILES * TOPK, E1]),
                                           ALU.is_equal))
                with nc.allow_low_precision(reason="sums of zeros and ones"):
                    V.tensor_reduce(sel[:, :, :], oh.rearrange("p t k e -> p t e k"), AX_X, ALU.add).then_inc(s["sel"], 1)
                dve.wait_ge(*filled(("rnk", r)))
                V.tensor_copy(rnk[:, :, :], filled_bank(("rnk", r))[:, 0:TILES * E1].rearrange("p (t e) -> p t e", e=E1)
                              ).then_inc(s["rnk"], 1)
                dve.wait_ge(*filled(("cnt", r)))
                V.tensor_scalar(cnt_i[:, 0, :], filled_bank(("cnt", r))[:, 0:E1], float(P - 1), None,
                                ALU.add).then_inc(s["cnt"], 1)
                dve.wait_ge(s["cnt"], r + 1)
                steps.link(V.tensor_scalar(cnt_i[:, 1, :], cnt_i[:, 0, :], P.bit_length() - 1, None,
                                           ALU.logical_shift_right))
                steps.link(V.tensor_copy(nblk[:, :], cnt_i[:, 1, :]))
                steps.link(V.tensor_tensor_scan(cum[:, :], ones[:, 0:E1], nblk[:, :], 0.0, ALU.mult, ALU.add))
                V.tensor_scalar(blk_c[:, :], cum[:, :], iota_col, None, ALU.is_le, ALU.add,
                                accum_out=blk_e[:, :]).then_inc(s["blk"], 1)
                steps.link(V.tensor_tensor(start[:, :], cum[:, :], nblk[:, :], ALU.subtract))
                dve.wait_ge(s["rnk"], r + 1)
                steps.link(V.scalar_tensor_tensor(pos, start[:, :].unsqueeze(1).to_broadcast([P, TILES, E1]), float(P),
                                                  rnk[:, :, :], ALU.mult, ALU.add))
                for t in range(TILES):
                    steps.mark(V.tensor_tensor(oh[:, t, :, :], oh[:, t, :, :],
                                               pos[:, t, :].unsqueeze(1).to_broadcast([P, TOPK, E1]), ALU.mult))
                steps.after(steps.n)
                steps.link(V.tensor_reduce(slot_f[:, :, :], oh, AX_X, ALU.add))
                V.tensor_copy(slot[:, :], slot_f[:, :, :].rearrange("p t k -> p (t k)")).then_inc(s["slot"], 1)
                dve.wait_ge(s["slot"], r + 1)
                steps.mark(V.tensor_scalar(row_blk[:, 0, :], slot[:, :].bitcast(I32), P - 1, None, ALU.bitwise_and))
                steps.link(V.tensor_scalar(row_blk[:, 1, :], slot[:, :].bitcast(I32), P.bit_length() - 1, None,
                                           ALU.logical_shift_right))
                V.tensor_copy(row_f[:, :, :], row_blk[:, :, :]).then_inc(s["rowf"], 1)
                dve.wait_ge(s["rowf"], r + 1)
                for i in range(TILES * TOPK):
                    n = r * (TILES * TOPK - 1) + i
                    if i >= PAIRS:
                        dve.wait_ge(s["paired"], n - PAIRS + 1)
                    if i % 2 == 0:
                        V.tensor_scalar(at_row[:, i % PAIRS, :], iota_h[:, :], row_f[:, 0, i:i + 1], None,
                                        ALU.is_equal).then_inc(s["row"], 1)
                    V.tensor_scalar(at_blk[:, i % PAIRS, :], iota_h[:, 0:NBLK], row_f[:, 1, i:i + 1],
                                    tok_id[:, i // TOPK:i // TOPK + 1], ALU.is_equal, ALU.mult).then_inc(s["pair"], 1)
                dve.wait_ge(*filled(("tok", r)))
                V.tensor_copy(tok[:, :], filled_bank(("tok", r))[:, 0:NBLK]).then_inc(s["tok"], 1)
                dve.wait_ge(*filled(("blk", r)))
                V.tensor_scalar(blk_i[:, :], filled_bank(("blk", r))[0:1, 0:P], float(E1 - 1), None,
                                ALU.min).then_inc(s["blki"], 1)
                dve.wait_ge(s["blki"], 2 * r + 1)
                for i in range(WORD):
                    steps.mark(V.tensor_scalar(shifted[:, i, :], blk_i[:, i:i + NBLK].rearrange("p (q i) -> p q i", i=4)[:, :, 0],
                                               BITS * i, None, ALU.logical_shift_left))
                steps.after(steps.n)
                steps.link(V.tensor_tensor(shifted[:, 0:3, :], shifted[:, 0:3, :], shifted[:, 3:6, :], ALU.bitwise_or))
                steps.link(V.tensor_tensor(shifted[:, 0, :], shifted[:, 0, :], shifted[:, 1, :], ALU.bitwise_or))
                V.tensor_tensor(words[:, :], shifted[:, 0, :], shifted[:, 2, :], ALU.bitwise_or).then_inc(s["blki"], 1)
                dve.wait_ge(s["exw"], (r + 1) * TILES)
                steps.link(V.reciprocal(wsum[:, :], wsum[:, :]))
                V.tensor_tensor(wts[:, :, :], wts[:, :, :], wsum[:, :].unsqueeze(2).to_broadcast([P, TILES, TOPK]),
                                ALU.mult).then_inc(s["ws"], 1)
                base = r * NBLK

                def step(stage, m, c, first):
                    j, k = 4 * m + c, c % 2
                    if stage == GATE_UP:
                        dve.wait_ge(s["sg"], j + (base + 1))
                        if not first:
                            dve.wait_ge(s["hturned"], j + (base - 1))
                        V.tensor_tensor(hh[:, k, :], sgt[:, k, :], bank[2 + k][:, FI:2 * FI], ALU.mult).then_inc(s["h"], 1)
                    if stage == DOWN:
                        dve.wait_ge(s["down"], j + (base + 1))
                        if c + base >= NXB:
                            dve.wait_ge(y_out[c % NXB], (m + (c // NXB + base // NXB)) * 16)
                        V.tensor_copy(yb[:, c % NXB, :], bank[6 + k][:, 0:D]).then_inc(s["yb"], 1)

                over_blocks(dve, step)
                dve.wait_ge(s["ws"], r + 1)
                if attention_next(layer):
                    combine(layer, 0)
                    combine(layer, 1)
                    ln_stats(layer + 1, pair(0))
                    combine(layer, 2)
                    ln_norm(layer + 1, pair(0))
                    combine(layer, 3)
                    ln_stats(layer + 1, pair(1))
                    attention(layer + 1, start=0)
                    ln_norm(layer + 1, pair(1))
                else:
                    for t in range(TILES):
                        combine(layer, t)

            def combine(layer, t):
                r = (layer - MOE1) // 2
                s = mo_s
                for k in range(TOPK):
                    i = t * TOPK + k
                    dve.wait_ge(y_in[i % NYG], 16 * (i // NYG + 1 + r * TILES * TOPK // NYG))
                    if k:
                        dve.wait_ge(s["comb"], 3 * (r * TILES + t) + k)
                    ins = V.scalar_tensor_tensor(X[:, t, :], yg[:, i % NYG, :], wts[:, t, k:k + 1], X[:, t, :],
                                                 ALU.mult, ALU.add)
                    ins.then_inc(s["comb"] if k < TOPK - 1 else x_ready, 1)

            for layer in range(LAYERS):
                if layer in (MOE0, MOE0B):
                    moe0(layer)
                elif layer in (ATTA, ATTB):
                    attention(layer)
                elif layer in (MOE1, MOE1B):
                    moe1(layer)
                else:
                    {RWKV: rwkv, MAMBA: mamba}[layer]()

        @block.gpsimd
        def _(pool):
            G = nc.gpsimd
            steps = Steps(pool, pool_step)

            def constants():
                G.memset(vt[:, :, 0, :, :], 1.0).then_inc(prep, 1)
                G.memset(vt[:, :, 1:PARTS, :, :], 0.0).then_inc(prep, 1)
                pool.wait_ge(w_in["small"], 16 * SMALLS)
                pool.wait_ge(w_in["mats"], 16)
                G.tensor_copy(mask_b[:, :], mask_f).then_inc(prep, 1)
                G.tensor_copy(ident_b[:, :], ident).then_inc(prep, 1)
                G.tensor_copy(tri_lt_b[:, :], tri_lt).then_inc(prep, 1)
                G.tensor_copy(ones_b[:, :], ones).then_inc(prep, 1)
                G.tensor_copy(iota_h[:, :], iotas[:, 0:P]).then_inc(prep, 1)
                pool.wait_ge(prep, PREPS)

            def ln_pow(layer, tiles):
                k = slice(tiles[0] % 8, tiles[0] % 8 + len(tiles))
                pool.wait_ge(ln_var, layer * TILES + tiles[-1] + 1)
                G.tensor_tensor(rstd[:, k], ve[:, k], neghalf[:, 0:len(tiles)], ALU.pow).then_inc(ln_rstd, len(tiles))

            def add_bias(layer, t):
                pool.wait_ge(ln_done, layer * TILES + t + 1)
                G.tensor_tensor(X[:, t, :], X[:, t, :], bo_row(layer), ALU.add).then_inc(xb_ready, 1)

            def rwkv():
                for b in range(B):
                    pool.wait_ge(xT_ready, (b + 1) * HALVES)
                    if b >= 2:
                        pool.wait_ge(rs["mix"], MIXES * (b - 1))
                    G.tensor_tensor(rw_diff[:, b % 2, :, :], xT[:, :, b, 1:T + 1], xT[:, :, b, 0:T],
                                    ALU.subtract).then_inc(rs["diff"], 1)
                for t in range(TILES):
                    add_bias(RWKV, t)
                constants()
                for b in range(B):
                    pool.wait_ge(rs["rb"], b + 1)
                    if b >= 1:
                        pool.wait_ge(rs["z"], b)
                    G.tensor_tensor(rw_q, rw_a[b % 2], rw_b[b % 2], ALU.mult).then_inc(rs["q"], 1)
                    if b >= 1 and eager_next(RWKV):
                        ln_pow(RWKV + 1, pair(b - 1))

            def mamba():
                ln_pow(MAMBA, pair(B - 1))
                pool.wait_ge(ms["ad"], 1)

                def decays(t):
                    if t >= 2:
                        pool.wait_ge(*filled(("seg", t - 2, 1)))
                    for i in range(MH):
                        G.tensor_scalar(m1[:, t % 2, i, :], tri_gt, a_d[:, t * MH + i:t * MH + i + 1], 1.0,
                                        ALU.mult, ALU.mult).then_inc(ms["m1"], 1)

                wide = "p (h n) -> p h n"
                decays(0)
                decays(1)
                for t in range(TILES):
                    b, h = t // HALVES, t % HALVES
                    pool.wait_ge(ms["htok"], t + 1)
                    if t >= 1:
                        pool.wait_ge(ms["y"], t)
                    G.tensor_tensor(dh.rearrange(wide, h=MH), htok[:, t % 2, :].rearrange(wide, h=MH),
                                    d_row.unsqueeze(2).to_broadcast([P, MH, MP]), ALU.mult).then_inc(ms["dh"], 1)
                    if h == 0:
                        pool.wait_ge(ms["dsc"], b + 1)
                        if b >= 1:
                            pool.wait_ge(*filled(("state", b - 1)))
                        G.tensor_tensor(hdec.rearrange(wide, h=MH), htok[:, t % 2, :].rearrange(wide, h=MH),
                                        dsc[:, :].unsqueeze(2).to_broadcast([P, MH, MP]), ALU.mult).then_inc(ms["hdec"], 1)
                    if t + 2 < TILES:
                        decays(t + 2)
                    if t >= 1:
                        rms(t - 1)
                    if t in (2, 4, 6) and eager_next(MAMBA):
                        ln_pow(MAMBA + 1, pair((t - 2) // 2))
                rms(TILES - 1)

            def rms(t):
                pool.wait_ge(act_step, t + 1)
                steps.link(G.tensor_scalar(mvar[:, t:t + 1], mss[:, t:t + 1], 1.0 / ME, RMS_EPS, ALU.mult, ALU.add))
                G.tensor_tensor(mrs[:, t:t + 1], mvar[:, t:t + 1], neghalf[:, 0:1], ALU.pow).then_inc(ms["rs"], 1)

            def attention(layer, start=None):
                r = (layer - ATTA) // 2

                if start is not None:
                    if start >= 1:
                        split(pool, G, steps, r, start)
                    for h in range(HALVES):
                        add_bias(layer, start * HALVES + h)
                    return
                for b in range(AHEAD_SEQ, B):
                    if b > AHEAD_SEQ or layer == ATTA:
                        ln_pow(layer, pair(b))
                    split(pool, G, steps, r, b)
                    for h in range(HALVES):
                        add_bias(layer, b * HALVES + h)
                if moe_next(layer):
                    ln_pow(layer + 1, range(EARLY_TILES))

            def moe1(layer):
                r = (layer - MOE1) // 2
                s = mo_s
                ln_pow(layer, range(EARLY_TILES, TILES))
                pool.wait_ge(s["rowf"], r + 1)
                for i in range(1, TILES * TOPK, 2):
                    if i >= PAIRS:
                        pool.wait_ge(s["paired"], r * (TILES * TOPK - 1) + i - PAIRS + 1)
                    G.tensor_scalar(at_row[:, i % PAIRS, :], iota_h[:, :], row_f[:, 0, i:i + 1], None,
                                    ALU.is_equal).then_inc(s["row_odd"], 1)
                pool.wait_ge(s["tok"], r + 1)
                pool.wait_ge(xn_out, 16 * TILES * (r + 1))
                for j in range(NBLK):
                    if j + r * NBLK >= NXB:
                        pool.wait_ge(s["turned"], r * NBLK + j - NXB + 1)
                    G.indirect_dma_start(out=xb[:, j % NXB, :], out_offset=None, in_=xn_d[:],
                                         in_offset=bass.IndirectOffsetOnAxis(ap=tok[:, j:j + 1], axis=0)
                                         ).then_inc(xb_in[j % NXB], 16)
                for k in range(NXB):
                    pool.wait_ge(y_out[k], 16 * (NBLK // NXB) * (r + 1))
                for t in range(TILES):
                    for k in range(TOPK):
                        i = t * TOPK + k
                        if i >= NYG:
                            if k < TOPK - 1:
                                pool.wait_ge(s["comb"], 3 * (r * TILES + t - NYG // TOPK) + k + 1)
                            else:
                                pool.wait_ge(x_ready, layer * TILES + t - NYG // TOPK + 1)
                        G.indirect_dma_start(out=yg[:, i % NYG, :], out_offset=None, in_=yg_d[:],
                                             in_offset=bass.IndirectOffsetOnAxis(ap=slot[:, i:i + 1], axis=0)
                                             ).then_inc(y_in[i % NYG], 16)
                    if t == 5 and attention_next(layer):
                        for b in range(AHEAD_SEQ):
                            attention(layer + 1, start=b)
                        ln_pow(layer + 1, pair(AHEAD_SEQ))
                    if t in (2, 4) and attention_next(layer):
                        ln_pow(layer + 1, pair(t // 2 - 1))

            G.memset(xT[:, :, :, 0:1], 0.0).then_inc(prep, 1)
            G.memset(neghalf[:, :], -0.5).then_inc(prep, 1)
            pool.wait_ge(prep, 2)
            for b in range(B):
                ln_pow(RWKV, pair(b))

            for layer in range(LAYERS):
                if layer in (MOE0, MOE0B):
                    ln_pow(layer, pair(B - 1))
                    if eager_next(layer):
                        for b in range(EARLY_SEQ):
                            ln_pow(layer + 1, pair(b))
                    if attention_next(layer):
                        ln_pow(layer + 1, range(AHEAD_SEQ * HALVES))
                        for b in range(AHEAD_SEQ):
                            attention(layer + 1, start=b)
                elif layer in (ATTA, ATTB):
                    attention(layer)
                elif layer in (MOE1, MOE1B):
                    moe1(layer)
                else:
                    {RWKV: rwkv, MAMBA: mamba}[layer]()

        @block.sync
        def _(sp):
            first_use = {"moe0": MOE0, "mamba": MAMBA, "att": ATTA}

            def load(key, tile, name):
                if first_use.get(key, 0) < LAYERS:
                    sp.dma_start(tile, a[name]).then_inc(w_in[key], 16)

            xv = a["x"].rearrange("(t p) d -> p t d", p=P)
            for t in range(TILES):
                sp.dma_start(X[:, t, :], xv[:, t, :]).then_inc(x_in[t], 16)
                if t == 0:
                    load("mats", mats[:, :, :], "mats")
            for tile, name in ((cols, "cols"), (rows, "rows"), (iotas, "iotas"), (mb_conv, "mb_conv"), (mb_norm, "mb_norm"),
                               (mask_f, "mask"), (rt_w, "rt_w"), (f0_wg, "f0_wg")):
                load("small", tile[:], name)
            load("rwkv", rw_w[:], "rw_w")
            load("moe0", f0_w[:], "f0_w")
            load("moe0", f0_b[:], "f0_b")
            load("mamba", mb_in[:], "mb_in")
            load("mamba", mb_out[:], "mb_out")
            for tile, name in ((at_q, "at_q"), (at_k, "at_k"), (at_v, "at_v"), (at_o, "at_o")):
                load("att", tile[:], name)
            if LAYERS > MOE1:
                sp.wait_ge(x_ready, (MAMBA + 1) * TILES)
                load("moe1", gu_w, "gu_w")
                load("moe1", dn_w, "dn_w")

            def alibi():
                for k in range(2):
                    for tile, name in ((Qs, "al_q"), (Ks, "al_k")):
                        view = a[name].bitcast(BF16).rearrange("p (h t) -> p h t", t=T)
                        sp.dma_start(tile[k][QROWS:QROWS + AROWS, :, :], view).then_inc(w_in["alibi"], 16)

            def stack(layer):
                for b in range(B):
                    seq = (layer - ATTA) // 2 * B + b
                    if seq >= 1:
                        sp.wait_ge(qk_in, 16 * 2 * len(SLOTS_Q) * seq)
                    sp.wait_ge(as_["kparts"], seq + 1)
                    sp.dma_start(k_d.rearrange("l h d t -> (h d) l t"), qk_part[0:NG * HD, :, DC * T:QK]).then_inc(k_out, 16)
                    for c in range(DC):
                        sp.wait_ge(as_["qparts"], DC * seq + c + 1)
                        sp.dma_start(q_d[:, c * HEADS // DC:(c + 1) * HEADS // DC].rearrange("l h d t -> (h d) l t"),
                                     qk_part[:, :, c * T:(c + 1) * T]).then_inc(q_out, 16)
                    sp.wait_ge(k_out, 16 * (seq + 1))
                    if seq == 0:
                        sp.wait_ge(x_ready, (MAMBA + 1) * TILES)
                    if seq >= 2:
                        sp.wait_ge(as_["exp"], HEADS * (seq - 1))
                    for i, l in enumerate(SLOTS_K):
                        sp.dma_start(Ks[seq % 2][i * HD:(i + 1) * HD, :, :], k_d[l].rearrange("h d t -> d h t")).then_inc(qk_in, 16)
                    sp.wait_ge(q_out, 16 * DC * (seq + 1))
                    for i, l in enumerate(SLOTS_Q):
                        sp.dma_start(Qs[seq % 2][i * HD:(i + 1) * HD, :, :], q_d[l].rearrange("h d t -> d h t")).then_inc(qk_in, 16)
                    if seq == 0:
                        alibi()

            for layer in range(ATTA, LAYERS):
                if layer in (ATTA, ATTB):
                    stack(layer)
                    continue
                base = (layer - MOE1) // 2 * NBLK
                xnv = xn_d.rearrange("(t p) d -> p t d", p=P)
                for t in range(TILES):
                    sp.wait_ge(ln_done, layer * TILES + t + 1)
                    sp.dma_start(xnv[:, t, :], xn[:, t, :]).then_inc(xn_out, 16)

                def store(j, c):
                    sp.wait_ge(mo_s["yb"], j + (base + 1))
                    sp.dma_start(yg_d[bass.ds(j * P, P), :], yb[:, c, :]).then_inc(y_out[c], 16)

                with sp.Fori(0, NBLK // NXB) as m:
                    for c in range(NXB):
                        store(NXB * m + c, c)
            ov = out.rearrange("(t p) d -> p t d", p=P)
            for t in range(TILES):
                sp.wait_ge(x_ready, (LAYERS - 1) * TILES + t + 1)
                sp.dma_start(ov[:, t, :], X[:, t, :]).then_inc(out_done, 16)
            sp.wait_ge(out_done, 16 * TILES)


def kernel(**inputs):
    import numpy as np
    import concourse.bacc as bacc
    from concourse import mybir as mb
    from concourse.bass_utils import run_bass_kernel_spmd

    def np32(name):
        return np.asarray(inputs[name])

    def feature(w):
        return w.reshape(-1, P, w.shape[-1]).transpose(1, 0, 2)

    def column(v):
        return v.reshape(-1, P).T

    def everywhere(v):
        return np.broadcast_to(v, (P, v.shape[-1]))

    L0, L1, L2, L3 = "L0_attn_a_", "L0_attn_b_", "L1_attn_a_", "L1_attn_b_"
    x = np32(L0 + "x")
    f = np.float32
    arrays = {"x": x.reshape(-1, D)}
    arrays["rw_w"] = np.stack([feature(np32(L0 + n).T) for n in ("Wk", "Wv", "Wr", "Wo")], axis=1)
    arrays["cols"] = np.stack([column(np32(L0 + n)) for n in ("bk", "bv", "br", "tmk", "tmv", "tmr", "u", "w")], axis=1)
    arrays["rows"] = everywhere(np.concatenate([np32(L1 + "dt_bias"), np32(L1 + "A_log"), np32(L1 + "D"),
                                                np32(L0 + "bo"), np32(L2 + "bo"), np32(L3 + "bo")]))
    arrays["f0_wg"] = feature(np32("L0_ffn_wg"))
    arrays["f0_w"] = feature(np32("L0_ffn_W").transpose(2, 0, 1).reshape(D, E0 * D))
    arrays["f0_b"] = np32("L0_ffn_b")
    arrays["mb_in"] = feature(np32(L1 + "in_proj_w").T)
    taps = np.concatenate([np32(L1 + "conv_w"), np32(L1 + "conv_b")[:, None]], axis=1)
    conv = np.zeros((P, CHUNKS, TAPS + 1), f)
    conv[:, :MC] = feature(taps[:ME])
    conv[:MN, MC:] = taps[ME:].reshape(2, MN, TAPS + 1).transpose(1, 0, 2)
    arrays["mb_conv"] = conv
    arrays["mb_norm"] = column(np32(L1 + "norm_w"))
    arrays["mb_out"] = feature(np32(L1 + "out_proj_w").T)

    wkv = np32(L3 + "Wkv")
    arrays["at_q"] = np.stack([feature(np32(L2 + "Wq")), feature(np32(L3 + "Wq"))], axis=1)
    arrays["at_k"] = np.stack([feature(np32(L2 + "Wk")), feature(wkv[:, :NG * HD])], axis=1)
    arrays["at_v"] = np.stack([feature(np32(L2 + "Wv")), feature(wkv[:, NG * HD:])], axis=1)
    arrays["at_o"] = np.stack([feature(np32(L2 + "Wo")), feature(np32(L3 + "Wo"))], axis=1)
    arrays["rt_w"] = feature(np32("L1_ffn_router_w").T)
    gate_up = np.concatenate([np32("L1_ffn_gate_w"), np32("L1_ffn_up_w")], axis=1)
    arrays["gu_w"] = feature(gate_up.transpose(2, 0, 1).reshape(D, E1 * 2 * FI))
    arrays["dn_w"] = np32("L1_ffn_down_w").transpose(2, 0, 1).reshape(FI, E1 * D)

    i, j = np.arange(P)[:, None], np.arange(P)[None, :]
    arrays["mats"] = np.stack([i == j, i > j, i <= j, i < j, i >= 0 * j], axis=1).astype(f)
    arrays["iotas"] = np.concatenate([np.broadcast_to(j, (P, P)), i + P * np.arange(TILES)[None, :]], axis=1).astype(f)
    later = np.where(j > i, f(-1e30), f(0))
    arrays["mask"] = later

    def parts(v):
        found = []
        for _ in range(PARTS):
            upper = v.view(np.uint32) >> 16
            found.append(upper.astype(np.uint16))
            v = v - (upper << 16).astype(np.uint32).view(f)
        return found

    first = 2.0 ** (-2.0 ** (-(np.log2(HEADS) - 3.0)))
    slopes = np.array([first ** (h + 1) for h in range(HEADS)], f)[:, None]
    counter = np.arange(T, dtype=f)[None, :]
    q_rows = parts(slopes + 0 * counter) + parts(-slopes * counter)
    k_rows = PARTS * [parts(counter + np.zeros((NG, 1), f))[0]] + PARTS * [parts(np.ones((NG, T), f))[0]]
    for name, r in (("al_q", q_rows), ("al_k", k_rows)):
        arrays[name] = np.stack(r).reshape(AROWS, -1).view(f)

    nc = bacc.Bacc("TRN2", target_bir_lowering=False, num_devices=1)
    arrays = {f"in_{k}": np.ascontiguousarray(v) for k, v in arrays.items()}
    aps = {k[3:]: nc.dram_tensor(k, v.shape, mb.dt.float32, kind="ExternalInput").ap() for k, v in arrays.items()}
    out = nc.dram_tensor("out_0", (B * T, D), mb.dt.float32, kind="ExternalOutput").ap()
    build(nc, aps, out)
    r = run_bass_kernel_spmd(nc, [arrays], core_ids=[0])
    return r.results[0]["out_0"].reshape(x.shape)
```
